# Optimizing a Trainium2 kernel written in Bass

```python
import numpy as np
import jax
import jax.numpy as jnp

def _softmax(x, axis=-1):
    return jax.nn.softmax(x, axis=axis)

def _gelu(x):
    return jax.nn.gelu(x, approximate=True)

def _silu(x):
    return jax.nn.silu(x)

def _sigmoid(x):
    return jax.nn.sigmoid(x)

def _layernorm(x, axis=-1, eps=1e-05):
    m = jnp.mean(x, axis=axis, keepdims=True)
    v = jnp.var(x, axis=axis, keepdims=True)
    return (x - m) / jnp.sqrt(v + eps)

def _scatter_add(tgt, idx, src, axis=0):
    return tgt.at[idx].add(src)

def _segment_sum(src, seg, n):
    return jax.ops.segment_sum(src, seg, n)
kernel_name = 'mk_gnn_ffn_d2_gnn_r8_8cd1f0'

def setup_inputs(seed: int=0):
    np.random.seed(seed)
    _w = jnp.asarray

    def _rec_inputs():
        import jax
        import jax.numpy as jnp
        _gk = jax.random.key(seed)
        x = -0.0003713 + 1 * jax.random.normal(jax.random.fold_in(_gk, 1), (6250, 256), jnp.float32)
        _s = jax.random.randint(jax.random.fold_in(_gk, 2), (100000,), 0, 6250, jnp.int32)
        _d = jax.random.randint(jax.random.fold_in(_gk, 3), (100000,), 0, 6250, jnp.int32)
        _loop = jnp.arange(6250, dtype=jnp.int32)
        src = jnp.concatenate([_s, _d, _loop])
        dst = jnp.concatenate([_d, _s, _loop])
        _o = jnp.argsort(dst, stable=True)
        src = src[_o]
        dst = dst[_o]
        return (x, src, dst)
    x, src, dst = _rec_inputs()

    def _L0_gnn_setup():
        import jax, jax.numpy as jnp
        import numpy as np
        from jax.ops import segment_max, segment_sum
        N_NODES = 6250
        N_EDGES = 100000
        IN_CH = 256
        HEADS = 8
        OUT_CH = 32
        NEG_SLOPE = 0.2
        EPS = 1e-16
        key = jax.random.key(seed)
        k1, k2, k3, k4, k5 = jax.random.split(key, 5)
        x = jax.random.normal(k1, (N_NODES, IN_CH), dtype=jnp.float32)
        edge_index = jax.random.randint(k2, (2, N_EDGES), 0, N_NODES, dtype=jnp.int64)
        W = jax.random.normal(k3, (HEADS * OUT_CH, IN_CH), dtype=jnp.float32) * (1.0 / np.sqrt(IN_CH))
        a_left = jax.random.normal(k4, (HEADS, OUT_CH), dtype=jnp.float32) * (1.0 / np.sqrt(OUT_CH))
        a_right = jax.random.normal(k5, (HEADS, OUT_CH), dtype=jnp.float32) * (1.0 / np.sqrt(OUT_CH))
        return {'x': x, 'edge_index': edge_index, 'W': W, 'a_left': a_left, 'a_right': a_right}
    _L0_gnn_all = _L0_gnn_setup()
    _L0_gnn_in = {k: v for k, v in _L0_gnn_all.items() if k in ('W', 'a_left', 'a_right')}
    del _L0_gnn_all

    def _L0_ffn_setup():
        import jax, jax.numpy as jnp
        import numpy as np
        B, N, D = (16, 512, 256)
        NUM_EXPERTS, TOP_K, HEADS = (4, 2, 4)
        N_EDGES = 131072
        LN_EPS = 1e-05

        def _layernorm(x, g, b):
            mu = x.mean(-1, keepdims=True)
            var = ((x - mu) ** 2).mean(-1, keepdims=True)
            return (x - mu) * jax.lax.rsqrt(var + LN_EPS) * g + b

        def _forward(x, edge_index, W_gat, att_src, att_dst, b_gat, ln_gamma, ln_beta, W1, b1, W2, b2):
            Bc, Nc, Dc = x.shape
            M = Bc * Nc
            x_flat = x.reshape(M, Dc)
            h = (x_flat @ W_gat).reshape(M, HEADS, NUM_EXPERTS)
            loops = jnp.arange(M, dtype=edge_index.dtype)
            src = jnp.concatenate([edge_index[0], loops])
            dst = jnp.concatenate([edge_index[1], loops])
            a_src = (h * att_src).sum(-1)
            a_dst = (h * att_dst).sum(-1)
            e = jax.nn.leaky_relu(a_src[src] + a_dst[dst], negative_slope=0.2)
            e_max = jax.ops.segment_max(e, dst, num_segments=M)
            ee = jnp.exp(e - e_max[dst])
            denom = jax.ops.segment_sum(ee, dst, num_segments=M)
            alpha = ee / (denom[dst] + 1e-16)
            msg = h[src] * alpha[:, :, None]
            agg = jax.ops.segment_sum(msg, dst, num_segments=M).reshape(M, HEADS * NUM_EXPERTS) + b_gat
            scores = _layernorm(agg, ln_gamma, ln_beta).reshape(M, HEADS, NUM_EXPERTS).mean(1)
            scores = scores.reshape(Bc, Nc, NUM_EXPERTS)
            topk_s, topk_i = jax.lax.top_k(scores, TOP_K)
            w = jax.nn.softmax(topk_s, axis=-1)
            out = jnp.zeros_like(x)
            for ei in range(NUM_EXPERTS):
                g = jnp.where(topk_i == ei, w, 0.0).sum(-1)
                hh = jax.nn.gelu(x @ W1[ei] + b1[ei], approximate=False)
                out = out + g[..., None] * (hh @ W2[ei] + b2[ei])
            return out
        key = jax.random.key(seed)
        ks = jax.random.split(key, 8)
        s = 0.05
        return {'x': jax.random.normal(ks[0], (B, N, D), jnp.float32), 'W_gat': jax.random.normal(ks[1], (D, HEADS * NUM_EXPERTS), jnp.float32) * s, 'att_src': jax.random.normal(ks[2], (HEADS, NUM_EXPERTS), jnp.float32) * s, 'att_dst': jax.random.normal(ks[3], (HEADS, NUM_EXPERTS), jnp.float32) * s, 'b_gat': jnp.zeros((HEADS * NUM_EXPERTS,), jnp.float32), 'ln_gamma': jnp.ones((HEADS * NUM_EXPERTS,), jnp.float32), 'ln_beta': jnp.zeros((HEADS * NUM_EXPERTS,), jnp.float32), 'W1': jax.random.normal(ks[4], (NUM_EXPERTS, D, 2 * D), jnp.float32) * s, 'b1': jnp.zeros((NUM_EXPERTS, 2 * D), jnp.float32), 'W2': jax.random.normal(ks[5], (NUM_EXPERTS, 2 * D, D), jnp.float32) * s, 'b2': jnp.zeros((NUM_EXPERTS, D), jnp.float32), 'edge_index': jax.random.randint(ks[6], (2, N_EDGES), 0, B * N, jnp.int32)}
    _L0_ffn_all = _L0_ffn_setup()
    _L0_ffn_in = {k: v for k, v in _L0_ffn_all.items() if k in ('W_gat', 'att_src', 'att_dst', 'b_gat', 'ln_gamma', 'ln_beta', 'W1', 'b1', 'W2', 'b2', 'edge_index')}
    del _L0_ffn_all

    def _L1_gnn_setup():
        import jax, jax.numpy as jnp
        import numpy as np
        N_NODES = 6250
        N_EDGES = 100000
        IN_CH = 256
        OUT_CH = 64
        HEADS = 4
        key = jax.random.key(seed)
        k1, k2, k3, k4, k5 = jax.random.split(key, 5)
        x = jax.random.normal(k1, (N_NODES, IN_CH), dtype=jnp.float32)
        edge_index = jax.random.randint(k2, (2, N_EDGES), 0, N_NODES, dtype=jnp.int64)
        weight = jax.random.normal(k3, (HEADS, IN_CH, OUT_CH), dtype=jnp.float32) * (2.0 / (IN_CH + OUT_CH)) ** 0.5
        att_src = jax.random.normal(k4, (1, HEADS, OUT_CH), dtype=jnp.float32) * 0.1
        att_dst = jax.random.normal(k5, (1, HEADS, OUT_CH), dtype=jnp.float32) * 0.1
        bias = jnp.zeros((HEADS * OUT_CH,), dtype=jnp.float32)
        return {'x': x, 'edge_index': edge_index, 'weight': weight, 'att_src': att_src, 'att_dst': att_dst, 'bias': bias}
    _L1_gnn_all = _L1_gnn_setup()
    _L1_gnn_in = {k: v for k, v in _L1_gnn_all.items() if k in ('weight', 'att_src', 'att_dst', 'bias')}
    del _L1_gnn_all

    def _L1_ffn_setup():
        import jax, jax.numpy as jnp
        import numpy as np
        N_EXPERTS = 8
        TOP_K = 2
        key = jax.random.key(seed)
        ks = jax.random.split(key, 5)
        B, T, C, E, H = (8, 256, 256, 8, 682)
        scale = 1.0 / np.sqrt(C)
        return {'x': jax.random.normal(ks[0], (B, T, C), dtype=jnp.float32), 'router_w': jax.random.normal(ks[1], (E, C), dtype=jnp.float32) * scale, 'w1': jax.random.normal(ks[2], (E, H, C), dtype=jnp.float32) * scale, 'w2': jax.random.normal(ks[3], (E, C, H), dtype=jnp.float32) * (1.0 / np.sqrt(H)), 'w3': jax.random.normal(ks[4], (E, H, C), dtype=jnp.float32) * scale}
    _L1_ffn_all = _L1_ffn_setup()
    _L1_ffn_in = {k: v for k, v in _L1_ffn_all.items() if k in ('router_w', 'w1', 'w2', 'w3')}
    del _L1_ffn_all
    return {'x': x, 'src': src, 'dst': dst, 'L0_gnn_W': _L0_gnn_in['W'], 'L0_gnn_a_left': _L0_gnn_in['a_left'], 'L0_gnn_a_right': _L0_gnn_in['a_right'], 'L0_ffn_W_gat': _L0_ffn_in['W_gat'], 'L0_ffn_att_src': _L0_ffn_in['att_src'], 'L0_ffn_att_dst': _L0_ffn_in['att_dst'], 'L0_ffn_b_gat': _L0_ffn_in['b_gat'], 'L0_ffn_ln_gamma': _L0_ffn_in['ln_gamma'], 'L0_ffn_ln_beta': _L0_ffn_in['ln_beta'], 'L0_ffn_W1': _L0_ffn_in['W1'], 'L0_ffn_b1': _L0_ffn_in['b1'], 'L0_ffn_W2': _L0_ffn_in['W2'], 'L0_ffn_b2': _L0_ffn_in['b2'], 'L0_ffn_edge_index': _L0_ffn_in['edge_index'], 'L1_gnn_weight': _L1_gnn_in['weight'], 'L1_gnn_att_src': _L1_gnn_in['att_src'], 'L1_gnn_att_dst': _L1_gnn_in['att_dst'], 'L1_gnn_bias': _L1_gnn_in['bias'], 'L1_ffn_router_w': _L1_ffn_in['router_w'], 'L1_ffn_w1': _L1_ffn_in['w1'], 'L1_ffn_w2': _L1_ffn_in['w2'], 'L1_ffn_w3': _L1_ffn_in['w3']}

def reference(x, src, dst, L0_gnn_W, L0_gnn_a_left, L0_gnn_a_right, L0_ffn_W_gat, L0_ffn_att_src, L0_ffn_att_dst, L0_ffn_b_gat, L0_ffn_ln_gamma, L0_ffn_ln_beta, L0_ffn_W1, L0_ffn_b1, L0_ffn_W2, L0_ffn_b2, L0_ffn_edge_index, L1_gnn_weight, L1_gnn_att_src, L1_gnn_att_dst, L1_gnn_bias, L1_ffn_router_w, L1_ffn_w1, L1_ffn_w2, L1_ffn_w3):
    import jax
    import jax.numpy as jnp

    def _L0_gnn_ref(x, edge_index, W, a_left, a_right):
        import jax, jax.numpy as jnp
        import numpy as np
        from jax.ops import segment_max, segment_sum
        N_NODES = 6250
        N_EDGES = 100000
        IN_CH = 256
        HEADS = 8
        OUT_CH = 32
        NEG_SLOPE = 0.2
        EPS = 1e-16
        N = x.shape[0]
        H, C = (HEADS, OUT_CH)
        loops = jnp.arange(N, dtype=edge_index.dtype)
        src = jnp.concatenate([edge_index[0], loops])
        dst = jnp.concatenate([edge_index[1], loops])
        Wh = (x @ W.T).reshape(N, H, C)
        e_left = jnp.einsum('nhc,hc->nh', Wh, a_left)
        e_right = jnp.einsum('nhc,hc->nh', Wh, a_right)
        e = e_left[src] + e_right[dst]
        e = jnp.where(e >= 0, e, NEG_SLOPE * e)
        e_max = segment_max(e, dst, num_segments=N)
        e_max = jnp.where(jnp.isfinite(e_max), e_max, 0.0)
        e_exp = jnp.exp(e - e_max[dst])
        denom = segment_sum(e_exp, dst, num_segments=N)
        alpha = e_exp / (denom[dst] + EPS)
        out = segment_sum(Wh[src] * alpha[:, :, None], dst, num_segments=N)
        return out.reshape(N, H * C)

    def _L0_ffn_ref(x, W_gat, att_src, att_dst, b_gat, ln_gamma, ln_beta, W1, b1, W2, b2, edge_index):
        import jax, jax.numpy as jnp
        import numpy as np
        B, N, D = (16, 512, 256)
        NUM_EXPERTS, TOP_K, HEADS = (4, 2, 4)
        N_EDGES = 131072
        LN_EPS = 1e-05

        def _layernorm(x, g, b):
            mu = x.mean(-1, keepdims=True)
            var = ((x - mu) ** 2).mean(-1, keepdims=True)
            return (x - mu) * jax.lax.rsqrt(var + LN_EPS) * g + b

        def _forward(x, edge_index, W_gat, att_src, att_dst, b_gat, ln_gamma, ln_beta, W1, b1, W2, b2):
            Bc, Nc, Dc = x.shape
            M = Bc * Nc
            x_flat = x.reshape(M, Dc)
            h = (x_flat @ W_gat).reshape(M, HEADS, NUM_EXPERTS)
            loops = jnp.arange(M, dtype=edge_index.dtype)
            src = jnp.concatenate([edge_index[0], loops])
            dst = jnp.concatenate([edge_index[1], loops])
            a_src = (h * att_src).sum(-1)
            a_dst = (h * att_dst).sum(-1)
            e = jax.nn.leaky_relu(a_src[src] + a_dst[dst], negative_slope=0.2)
            e_max = jax.ops.segment_max(e, dst, num_segments=M)
            ee = jnp.exp(e - e_max[dst])
            denom = jax.ops.segment_sum(ee, dst, num_segments=M)
            alpha = ee / (denom[dst] + 1e-16)
            msg = h[src] * alpha[:, :, None]
            agg = jax.ops.segment_sum(msg, dst, num_segments=M).reshape(M, HEADS * NUM_EXPERTS) + b_gat
            scores = _layernorm(agg, ln_gamma, ln_beta).reshape(M, HEADS, NUM_EXPERTS).mean(1)
            scores = scores.reshape(Bc, Nc, NUM_EXPERTS)
            topk_s, topk_i = jax.lax.top_k(scores, TOP_K)
            w = jax.nn.softmax(topk_s, axis=-1)
            out = jnp.zeros_like(x)
            for ei in range(NUM_EXPERTS):
                g = jnp.where(topk_i == ei, w, 0.0).sum(-1)
                hh = jax.nn.gelu(x @ W1[ei] + b1[ei], approximate=False)
                out = out + g[..., None] * (hh @ W2[ei] + b2[ei])
            return out
        return _forward(x, edge_index, W_gat, att_src, att_dst, b_gat, ln_gamma, ln_beta, W1, b1, W2, b2)

    def _L1_gnn_ref(x, edge_index, weight, att_src, att_dst, bias):
        import jax, jax.numpy as jnp
        import numpy as np
        N_NODES = 6250
        N_EDGES = 100000
        IN_CH = 256
        OUT_CH = 64
        HEADS = 4
        num_nodes = x.shape[0]
        row, col = (edge_index[0], edge_index[1])
        x_h = jnp.einsum('nf,hfc->nhc', x, weight)
        alpha_src = jnp.sum(x_h * att_src[0], axis=-1)
        alpha_dst = jnp.sum(x_h * att_dst[0], axis=-1)
        alpha = alpha_src[row] + alpha_dst[col]
        alpha = jax.nn.leaky_relu(alpha, negative_slope=0.2)
        alpha_max = jax.ops.segment_max(alpha, row, num_segments=num_nodes)
        alpha = jnp.exp(alpha - alpha_max[row])
        alpha_sum = jax.ops.segment_sum(alpha, row, num_segments=num_nodes)
        alpha = alpha / jnp.clip(alpha_sum[row], 1e-16)
        messages = alpha[:, :, None] * x_h[col]
        out = jax.ops.segment_sum(messages, row, num_segments=num_nodes)
        out = out.reshape(num_nodes, -1) + bias
        return out

    def _L1_ffn_ref(x, router_w, w1, w2, w3):
        import jax, jax.numpy as jnp
        import numpy as np
        N_EXPERTS = 8
        TOP_K = 2
        B, T, C = x.shape
        flat = x.reshape(-1, C)
        logits = flat @ router_w.T
        probs = jax.nn.softmax(logits, axis=-1)
        topk_probs, topk_idx = jax.lax.top_k(probs, TOP_K)
        topk_probs = topk_probs / (jnp.sum(topk_probs, axis=-1, keepdims=True) + 1e-09)
        onehot = jax.nn.one_hot(topk_idx, N_EXPERTS, dtype=flat.dtype)
        gates = jnp.einsum('nk,nke->ne', topk_probs, onehot)
        h1 = jnp.einsum('nc,ehc->neh', flat, w1)
        h3 = jnp.einsum('nc,ehc->neh', flat, w3)
        h = jax.nn.silu(h1) * h3
        y = jnp.einsum('neh,ech->nec', h, w2)
        out = jnp.einsum('ne,nec->nc', gates, y)
        return out.reshape(B, T, C)
    edge_index = jnp.stack([src, dst])
    x = x + _L0_gnn_ref(_layernorm(x, axis=-1), edge_index, L0_gnn_W, L0_gnn_a_left, L0_gnn_a_right)
    x = x + _L0_ffn_ref(_layernorm(x, axis=-1)[None], L0_ffn_W_gat, L0_ffn_att_src, L0_ffn_att_dst, L0_ffn_b_gat, L0_ffn_ln_gamma, L0_ffn_ln_beta, L0_ffn_W1, L0_ffn_b1, L0_ffn_W2, L0_ffn_b2, L0_ffn_edge_index)[0]
    x = x + _L1_gnn_ref(_layernorm(x, axis=-1), edge_index, L1_gnn_weight, L1_gnn_att_src, L1_gnn_att_dst, L1_gnn_bias)
    x = x + _L1_ffn_ref(_layernorm(x, axis=-1)[None], L1_ffn_router_w, L1_ffn_w1, L1_ffn_w2, L1_ffn_w3)[0]
    return x

_drawn_inputs = setup_inputs


def setup_inputs(seed=0):
    import zlib

    import numpy as np

    out = dict(_drawn_inputs(seed))
    spreads = {'L0_ffn_b_gat': (0.0, 0.1),
     'L0_ffn_ln_gamma': (1.0, 0.2),
     'L0_ffn_ln_beta': (0.0, 0.1),
     'L0_ffn_b1': (0.0, 0.1),
     'L0_ffn_b2': (0.0, 0.1),
     'L1_gnn_bias': (0.0, 0.1)}
    factors = {}
    for name, (base, spread) in spreads.items():
        noise = np.random.default_rng([zlib.crc32(name.encode()), seed]).standard_normal(out[name].shape)
        drawn = base * np.exp(spread * noise) if base else spread * noise
        out[name] = jnp.asarray(drawn.astype(out[name].dtype))
    for name, factor in factors.items():
        out[name] = (out[name] * factor).astype(out[name].dtype)
    return out
```

```python
from contextlib import ExitStack

import concourse.bass as bass
from concourse import mybir

ALU = mybir.AluOpType
ACT = mybir.ActivationFunctionType
AX = mybir.AxisListType
F32 = mybir.dt.float32
I32 = mybir.dt.int32
ds = bass.ds

P = 128
N = 6250
D = 256
NT = 49
NR = NT * P
NTP = 50
NP = NTP * P
DUMMY = NP
LOG_RANKS = 13
PAD_RANKS = 2 ** LOG_RANKS - NR
ID_BITS = 13
ID_MASK = 2 ** ID_BITS - 1
KEY_BASE = 0x20000000
DEG_BASE = 1024
SLOTS = 8
WIN = 32
RING = 4
NEG = -1e30
COARSE = 512


class Cfg:

    def __init__(self, name, E, F):
        self.name, self.E, self.F = name, E, F
        self.total = P * F
        self.rows = self.total // WIN + 2
        self.max_blocks = (E + E // P) // SLOTS + 2 * NT + 4 * RING


class Scope:

    def __init__(self, nc, tag, keep=None):
        self.nc, self.tag, self.st, self.sems = nc, tag, ExitStack(), []
        self.keep = keep or self.st

    def __enter__(self):
        return self

    def __exit__(self, *a):
        if self.sems and a[0] is None:
            for x in self.sems:
                self.nc.gpsimd.sem_clear(x)
            self.nc.all_engine_barrier()
        return self.st.__exit__(*a)

    def sb(self, name, shape, dt=F32):
        return self.st.enter_context(self.nc.sbuf_tensor(f"{self.tag}_{name}", shape, dt))

    def ps(self, name, shape, dt=F32):
        return self.st.enter_context(self.nc.psum_tensor(f"{self.tag}_{name}", shape, dt))

    def sem(self, name):
        self.sems.append(self.st.enter_context(self.nc.semaphore(f"{self.tag}_{name}")))
        return self.sems[-1]

    def pool_sem(self, name):
        return self.keep.enter_context(self.nc.semaphore(f"{self.tag}_{name}"))


class Count:

    def __init__(self, sem, base=0):
        self.sem, self.base, self.n = sem, base, 0

    def inc(self, ins, by=1):
        ins.then_inc(self.sem, by)
        self.n += by
        return ins

    def wait(self, eng):
        eng.wait_ge(self.sem, self.base + self.n)

    def link(self, eng, ins):
        self.inc(ins)
        self.wait(eng)


def sort_steps(log_part, log_free):
    steps = []
    for k in range(1, log_part + log_free + 1):
        if k >= log_free:
            steps.append(("sign", k - log_free))
        if k > log_free:
            steps.append(("turn",))
            steps += [("cross", j - log_free) for j in range(k - 1, log_free - 1, -1)]
            steps.append(("back",))
        for j in range(min(k, log_free) - 1, -1, -1):
            steps.append(("free", k, j))
    return steps


class Sorter:

    def __init__(self, log_part, log_free, bufs, turned, sign, ident, cmp_done, turned_in_psum, copied):
        self.lp, self.lf = log_part, log_free
        self.PB, self.F = 2 ** log_part, 2 ** log_free
        self.nb = max(1, self.F // P)
        self.steps = sort_steps(log_part, log_free)
        self.bufs, self.turned, self.sign, self.ident = bufs, turned, sign, ident
        self.cmp_done, self.in_psum, self.copied = cmp_done, turned_in_psum, copied
        self.at = []
        n, cur = 0, 0
        for s in self.steps:
            self.at.append((n, cur))
            if s[0] in ("cross", "sign"):
                n += 2 if s[0] == "cross" else 1
            elif s[0] == "free":
                n += 4 if s[1] < self.lf else 2
            cur ^= 1
        self.result = cur
        self.total = n

    def groups(self):
        width = self.nb * P if self.F >= P else self.PB
        return [(g, min(g + 512, self.F)) for g in range(0, self.F, 512)]

    def vector(self, dve, before):
        nturn = 0
        before()
        for s, (n, cur) in zip(self.steps, self.at):
            src, dst = self.bufs[cur][0:self.PB, 0:self.F], self.bufs[cur ^ 1][0:self.PB, 0:self.F]
            if s[0] in ("turn", "back"):
                nturn += 1
                continue
            if nturn:
                dve.wait_ge(self.copied, nturn * self.ngroups)
            if n:
                dve.wait_ge(self.cmp_done, n)
            if s[0] == "sign":
                dve.tensor_scalar(dst, src, self.sign[0:self.PB, s[1]:s[1] + 1], None, ALU.mult).then_inc(self.cmp_done, 1)
            elif s[0] == "cross":
                a, b = self.bufs[cur][:, 0:self.nb * self.PB], self.bufs[cur ^ 1][:, 0:self.nb * self.PB]
                y = 2 ** s[1]
                a = a.rearrange("q (x two y) -> q x two y", two=2, y=y)
                b = b.rearrange("q (x two y) -> q x two y", two=2, y=y)
                for half, op in ((0, ALU.min), (1, ALU.max)):
                    dve.tensor_tensor(b[:, :, half, :], a[:, :, 0, :], a[:, :, 1, :], op).then_inc(self.cmp_done, 1)
            elif s[1] >= self.lf:
                y = 2 ** s[2]
                a = src.rearrange("q (x two y) -> q x two y", two=2, y=y)
                b = dst.rearrange("q (x two y) -> q x two y", two=2, y=y)
                for half, op in ((0, ALU.min), (1, ALU.max)):
                    dve.tensor_tensor(b[:, :, half, :], a[:, :, 0, :], a[:, :, 1, :], op).then_inc(self.cmp_done, 1)
            else:
                y, m = 2 ** s[2], 2 ** (s[1] - 1 - s[2])
                a = src.rearrange("q (x dir m two y) -> q x dir m two y", dir=2, m=m, two=2, y=y)
                b = dst.rearrange("q (x dir m two y) -> q x dir m two y", dir=2, m=m, two=2, y=y)
                for d in (0, 1):
                    for half, op in ((d, ALU.min), (1 - d, ALU.max)):
                        dve.tensor_tensor(b[:, :, d, :, half, :], a[:, :, d, :, 0, :], a[:, :, d, :, 1, :], op).then_inc(self.cmp_done, 1)

    @property
    def ngroups(self):
        return len(self.groups())

    def tensor(self, pe, before):
        before()
        nturn = 0
        for s, (n, cur) in zip(self.steps, self.at):
            if s[0] not in ("turn", "back"):
                continue
            pe.wait_ge(self.cmp_done, n)
            if nturn:
                pe.wait_ge(self.copied, nturn * self.ngroups)
            nturn += 1
            src = self.bufs[cur]
            for lo, hi in self.groups():
                if s[0] == "turn":
                    for b in range(lo // P, hi // P):
                        mm = pe.transpose(self.turned[:, b * self.PB:(b + 1) * self.PB], src[0:self.PB, b * P:(b + 1) * P],
                                          self.ident[0:self.PB, 0:self.PB])
                else:
                    for b in range(lo // P, hi // P):
                        mm = pe.transpose(self.turned[0:self.PB, b * P:(b + 1) * P], src[:, b * self.PB:(b + 1) * self.PB],
                                          self.ident[:, :])
                mm.then_inc(self.in_psum, 1)

    def scalar(self, act):
        nturn = 0
        for s, (n, cur) in zip(self.steps, self.at):
            if s[0] not in ("turn", "back"):
                continue
            dst = self.bufs[cur ^ 1]
            for i, (lo, hi) in enumerate(self.groups()):
                act.wait_ge(self.in_psum, nturn * self.ngroups + i + 1)
                if s[0] == "turn":
                    a, b = lo // P * self.PB, hi // P * self.PB
                    act.activation(dst[:, a:b], self.turned[:, a:b], ACT.Copy).then_inc(self.copied, 1)
                else:
                    act.activation(dst[0:self.PB, lo:hi], self.turned[0:self.PB, lo:hi], ACT.Copy).then_inc(self.copied, 1)
            nturn += 1


def preload_lists(nc, cfg, key, payload, clamp, words, firsts, copies, S):
    F, E = cfg.F, cfg.E
    full, rest = E // F, E % F
    with Scope(nc, f"sort{cfg.name}", S["keep"]) as s:
        bufs = [s.sb("words0", [P, F]), s.sb("words1", [P, F])]
        zeros = s.sb("zeros", [WIN, 2 * WIN], I32)
        turned = s.ps("turned", [P, 2048])
        cleared, loaded, packed = s.sem("cleared"), s.sem("loaded"), s.sem("packed")
        cmp_done, in_psum, copied = s.sem("cmp_done"), s.sem("in_psum"), s.sem("copied")
        ids_ready, stored = s.sem("ids_ready"), s.sem("stored")
        so = Sorter(7, F.bit_length() - 1, bufs, turned, S["sign"], S["ident"], cmp_done, in_psum, copied)
        ki, vi = bufs[0][:, :].bitcast(I32), bufs[1][:, :].bitcast(I32)
        result, ids = bufs[so.result], bufs[so.result ^ 1][:, :].bitcast(I32)
        nload = 64 if rest else 32
        with nc.Block() as block:
            @block.sync
            def _(sp):
                sp.wait_ge(cleared, 3)
                for t, src in ((ki, key), (vi, payload)):
                    sp.dma_start(t[0:full, :], src[0:full * F].rearrange("(p f) -> p f", f=F)).then_inc(loaded, 16)
                    if rest:
                        sp.dma_start(t[full:full + 1, 0:rest], src[full * F:E].rearrange("(p f) -> p f", p=1)).then_inc(loaded, 16)
                sp.dma_start(copies[:, cfg.total - WIN + WIN:cfg.rows * WIN], zeros[:, :]).then_inc(stored, 16)
                sp.wait_ge(stored, 16)
                sp.wait_ge(cmp_done, so.total)
                sp.dma_start(words.rearrange("(p f) -> p f", f=F), result[:, :]).then_inc(stored, 16)
                with nc.allow_non_contiguous_dma(reason="one word in 512"):
                    sp.dma_start(firsts.rearrange("(p f) -> p f", p=P),
                                 result[:, :].rearrange("p (f c) -> p f c", c=COARSE)[:, :, 0]).then_inc(stored, 16)
                sp.wait_ge(ids_ready, 1)
                for c in range(WIN):
                    sp.dma_start(copies[c, WIN - c:WIN - c + cfg.total].rearrange("(p f) -> p f", f=F), ids).then_inc(stored, 16)
                sp.wait_ge(stored, 16 * (3 + WIN))

            @block.vector
            def _(dve):
                dve.memset(ki, ID_MASK).then_inc(cleared, 1)
                dve.memset(vi, 0).then_inc(cleared, 1)
                dve.memset(zeros[:, :], 0).then_inc(cleared, 1)
                dve.wait_ge(loaded, nload)
                pk = Count(packed)
                if clamp is not None:
                    pk.link(dve, dve.tensor_scalar(vi, vi, clamp, None, ALU.min))
                pk.link(dve, dve.tensor_scalar(ki, ki, ID_BITS, KEY_BASE, ALU.logical_shift_left, ALU.bitwise_or))
                pk.link(dve, dve.tensor_tensor(ki, ki, vi, ALU.bitwise_or))
                so.vector(dve, lambda: None)
                dve.wait_ge(cmp_done, so.total)
                dve.tensor_scalar(ids, result[:, :].bitcast(I32), ID_MASK, None, ALU.bitwise_and).then_inc(ids_ready, 1)

            @block.tensor
            def _(pe):
                so.tensor(pe, lambda: None)

            @block.scalar
            def _(act):
                so.scalar(act)


INFO = 256
I_NB, I_NW, I_CB, I_CW, I_RINGS, I_T0, I_LEFT = 0, 50, 100, 150, 200, 201, 202
INFO_STEPS = 20


def rank_nodes(nc, cfg, words, firsts, copies, starts, inv, info, ell, maxdeg, S):
    NF = cfg.total // COARSE
    R0 = PAD_RANKS // P
    U = 7
    HALF = 5
    NSEARCH = NTP // (2 * HALF)
    with Scope(nc, f"rank{cfg.name}", S["keep"]) as s:
        thr = s.sb("thresholds", [P, NTP])
        thr_i = thr[:, :].bitcast(I32)
        firsts_b, junk = s.sb("firsts", [P, NF]), s.sb("junk", [P, COARSE])
        cnt1, cnt2, q, qi = s.sb("cnt1", [P, NTP]), s.sb("cnt2", [P, NTP]), s.sb("q", [P, NTP]), s.sb("qi", [P, NTP], I32)
        q_now = [s.sb(f"q_now{i}", [P, HALF], I32) for i in range(2)]
        row = [s.sb(f"row{i}", [P, HALF * COARSE]) for i in range(2)]
        start = s.sb("start", [P, NTP])
        zero1 = s.sb("zero1", [1, 1])
        lo, hi = s.sb("lo", [NTP, P]), s.sb("hi", [NTP, P])
        vrow = s.sb("vrow", [64, P])
        vrow_i = s.sb("vrow_i", [64, P], I32)
        real, deg, tmp, tmp_i = s.sb("real", [64, P]), s.sb("deg", [64, P]), s.sb("tmp", [64, P]), s.sb("tmp_i", [64, P], I32)
        bufs = [s.sb("dwords0", [P, P]), s.sb("dwords1", [P, P])]
        turned = s.ps("turned", [P, 512])
        idf, degf = s.sb("idf", [64, P]), s.sb("degf", [64, P])
        tr = s.ps("tr", [P, 2, 64])
        node_i, degt = s.sb("node_i", [P, 64], I32), s.sb("degt", [P, 64])
        rank_i = s.sb("rank_i", [P, NTP], I32)
        node7, rank7, start7 = s.sb("node7", [P, U], I32), s.sb("rank7", [P, U], I32), s.sb("start7", [P, U])
        start_r, si = s.sb("start_r", [P, NT]), s.sb("si", [P, NT], I32)
        qr, cr = s.sb("qr", [P, NT]), s.sb("cr", [P, NT])
        row_i = s.sb("row_i", [P, 2 * NT], I32)
        md, mdi, mdw = s.sb("md", [1, NTP]), s.sb("mdi", [1, NTP], I32), s.sb("mdw", [1, NTP], I32)
        cums, one = s.sb("cums", [1, 2 * NTP]), s.sb("one", [1, NTP])
        inf = s.sb("info", [1, INFO], I32)
        iota_w = s.sb("iota_w", [P, WIN])
        cur, rem, mask = s.sb("cur", [P, 1]), s.sb("rem", [P, 1]), s.sb("mask", [P, WIN])
        iota_2w, wide_tiles = s.sb("iota_2w", [P, 2 * WIN]), s.sb("wide_tiles", [1, 1])
        curs, ridx_all, ridx7 = s.sb("curs", [P, NT]), s.sb("ridx_all", [P, 2, NT], I32), s.sb("ridx7", [P, 2, U], I32)
        wide, wmask, slots7 = s.sb("wide", [P, U * 2 * WIN], I32), s.sb("wmask", [P, U, 2 * WIN]), s.sb("slots7", [P, U * 2 * WIN], I32)
        group_ready, group_full, group_stored = s.sem("group_ready"), s.sem("group_full"), s.sem("group_stored")
        wide_got, inv_set = s.pool_sem("wide_got"), s.pool_sem("inv_set")
        ridx, win, picked, slots = s.sb("ridx", [P, 1], I32), s.sb("win", [P, WIN], I32), s.sb("picked", [P, WIN]), s.sb("slots", [P, WIN], I32)
        empty = s.sb("empty", [P, 2 * RING * SLOTS], I32)
        made, loaded, searched, qready = s.sem("made"), s.sem("loaded"), s.sem("searched"), s.sem("qready")
        got_row = [s.pool_sem(f"got_row{i}") for i in range(2)]
        counted, startd, st_stored = s.sem("counted"), s.sem("startd"), s.sem("st_stored")
        neigh, packed, cmp_done, in_psum, copied = s.sem("neigh"), s.sem("packed"), s.sem("cmp_done"), s.sem("in_psum"), s.sem("copied")
        decoded, turned_ids, node_done, seven, seven_got = s.sem("decoded"), s.sem("turned_ids"), s.sem("node_done"), s.sem("seven"), s.pool_sem("seven_got")
        taken7, md_done, md_back, tables, passed = s.sem("taken7"), s.sem("md_done"), s.sem("md_back"), s.sem("tables"), s.sem("passed")
        info_done, info_stored, sp_passed = s.sem("info_done"), s.sem("info_stored"), s.sem("sp_passed")
        win_step, win_ready, win_got, win_full, win_stored, passed2, empty_done = [s.pool_sem(n) if n == "win_got" else s.sem(n) for n in
            ("win_step", "win_ready", "win_got", "win_full", "win_stored", "passed2", "empty_done")]
        so = Sorter(6, 7, bufs, turned, S["sign"], S["ident"], cmp_done, in_psum, copied)
        key_i = bufs[0][0:64, :].bitcast(I32)
        res = bufs[so.result][0:64, 0:P]
        res_i = res.bitcast(I32)
        with nc.Block() as block:
            @block.sync
            def _(sp):
                sp.dma_start(firsts_b[:, :], firsts.rearrange("(a f) -> a f", a=1).to_broadcast([P, NF])).then_inc(loaded, 16)
                sp.wait_ge(startd, 4)
                with nc.allow_non_contiguous_dma(reason="node order"):
                    sp.dma_start(starts[0:NP].rearrange("(t p) -> p t", p=P), start[:, :]).then_inc(st_stored, 16)
                sp.dma_start(starts[NP:NP + 1].rearrange("(a b) -> a b", a=1), zero1[:, :]).then_inc(st_stored, 16)
                sp.wait_ge(made, 3)
                with nc.allow_non_contiguous_dma(reason="node order"):
                    sp.dma_start(inv[NR:NP].rearrange("(t p) -> p t", p=P), rank_i[:, NT:NTP]).then_inc(st_stored, 16)
                sp.wait_ge(st_stored, 48)
                sp.dma_start(lo[:, :], starts[0:NP].rearrange("(t p) -> t p", p=P)).then_inc(neigh, 16)
                sp.dma_start(hi[:, :], starts[1:NP + 1].rearrange("(t p) -> t p", p=P)).then_inc(neigh, 16)
                sp.wait_ge(decoded, 5)
                with nc.allow_non_contiguous_dma(reason="one per tile"):
                    sp.dma_start(maxdeg.rearrange("(t a) -> t a", a=1), degf[R0:64, P - 1:P]).then_inc(md_back, 16)
                sp.wait_ge(md_back, 16)
                sp.dma_start(md[:, 0:NT], maxdeg.rearrange("(a t) -> a t", a=1)).then_inc(md_back, 16)
                sp.wait_ge(info_done, INFO_STEPS)
                sp.dma_start(info, inf[:, :]).then_inc(info_stored, 16)
                sp.wait_ge(info_stored, 16)
                with sp.Fori(0, NT // U) as i:
                    sp.wait_ge(group_full, i + 1)
                    sp.sem_inc(sp_passed, 1)
                    for u in range(U):
                        c0 = sp.value_load(inf[0:1, ds(i * U + (u + I_CB), 1)], min_val=0, max_val=cfg.max_blocks - 2 * WIN // SLOTS)
                        sp.dma_start(ell[ds(c0, 2 * WIN // SLOTS), :, :].rearrange("b p j -> p b j"),
                                     slots7[:, u * 2 * WIN:(u + 1) * 2 * WIN].rearrange("p (b j) -> p b j", j=SLOTS)).then_inc(group_stored, 16)
                        sp.wait_ge(group_stored, i * (16 * U) + (u + 1) * 16)
                        sp.sem_inc(sp_passed, 1)
                t0 = sp.value_load(inf[0:1, I_T0:I_T0 + 1], min_val=0, max_val=NT - 1)
                left = sp.value_load(inf[0:1, I_LEFT:I_LEFT + 1], min_val=1, max_val=NT)
                with sp.Fori(0, left) as i:
                    t = nc.s_assert_within(t0 + i, 0, NT - 1, skip_runtime_bounds_check_because="the tiles from t0 on")
                    n = sp.value_load(inf[0:1, ds(t + I_NW, 1)], min_val=1, max_val=cfg.max_blocks)
                    c0 = sp.value_load(inf[0:1, ds(t + I_CB, 1)], min_val=0, max_val=cfg.max_blocks)
                    w0 = sp.value_load(inf[0:1, ds(t + I_CW, 1)], min_val=0, max_val=cfg.max_blocks)
                    with sp.Fori(0, n) as w:
                        sp.wait_ge(win_full, w0 + w + 1)
                        sp.sem_inc(sp_passed, 1)
                        sp.dma_start(ell[ds(nc.s_assert_within(c0 + w * 4, 0, cfg.max_blocks - 4, skip_runtime_bounds_check_because="a window's blocks lie within the list's"), 4), :, :].rearrange("b p j -> p b j"),
                                     slots[:, :].rearrange("p (b j) -> p b j", j=SLOTS)).then_inc(win_stored, 16)
                        sp.wait_ge(win_stored, (w0 + w + 1) * 16)
                        sp.sem_inc(sp_passed, 1)
                last = sp.value_load(inf[0:1, I_CB + NT:I_CB + NT + 1], min_val=1, max_val=cfg.max_blocks - 2 * RING)
                sp.wait_ge(made, 5)
                sp.dma_start(ell[ds(last, 2 * RING), :, :].rearrange("b p j -> p b j"),
                             empty[:, :].rearrange("p (b j) -> p b j", j=SLOTS)).then_inc(empty_done, 16)
                sp.wait_ge(empty_done, 16)

            @block.gpsimd
            def _(pool):
                pool.iota(thr_i, [[P, NTP]], base=0, channel_multiplier=1).then_inc(made, 1)
                pool.iota(vrow_i[:, :], [[1, P]], base=0, channel_multiplier=P).then_inc(made, 1)
                pool.iota(rank_i[:, :], [[P, NTP]], base=0, channel_multiplier=1).then_inc(made, 1)
                pool.iota(iota_w[:, :], [[1, WIN]], base=0, channel_multiplier=0,
                          allow_small_or_imprecise_dtypes=True).then_inc(made, 1)
                pool.memset(empty[:, :], DUMMY).then_inc(made, 1)
                pool.iota(iota_2w[:, :], [[1, 2 * WIN]], base=0, channel_multiplier=0,
                          allow_small_or_imprecise_dtypes=True).then_inc(made, 1)
                rows = words.rearrange("(r c) -> r c", c=COARSE)
                with pool.Fori(0, NSEARCH) as i:
                    for u in range(2):
                        pool.wait_ge(qready, i * 2 + u + 1)
                        pool.sem_inc(passed, 1)
                        for v in range(HALF):
                            pool.indirect_dma_start(out=row[u][:, v * COARSE:(v + 1) * COARSE], out_offset=None, in_=rows,
                                                    in_offset=bass.IndirectOffsetOnAxis(ap=q_now[u][:, v:v + 1], axis=0)).then_inc(got_row[u], 16)
                pool.wait_ge(st_stored, 48)
                with pool.Fori(0, NT // U) as i:
                    pool.wait_ge(seven, i + 1)
                    pool.sem_inc(passed, 1)
                    for u in range(U):
                        pool.indirect_dma_start(out=start7[:, u:u + 1], out_offset=None, in_=starts.rearrange("(n a) -> n a", a=1),
                                                in_offset=bass.IndirectOffsetOnAxis(ap=node7[:, u:u + 1], axis=0)).then_inc(seven_got, 16)
                with pool.Fori(0, NT // U) as i:
                    pool.wait_ge(group_ready, i + 1)
                    pool.sem_inc(passed, 1)
                    for u in range(U):
                        for w in range(2):
                            at = (u * 2 + w) * WIN
                            pool.indirect_dma_start(out=wide[:, at:at + WIN], out_offset=None, in_=copies.rearrange("c (r w) -> (c r) w", w=WIN),
                                                    in_offset=bass.IndirectOffsetOnAxis(ap=ridx7[:, w, u:u + 1], axis=0)).then_inc(wide_got, 16)
                    for u in range(U):
                        pool.indirect_dma_start(out=inv.rearrange("(n a) -> n a", a=1), in_=rank7[:, u:u + 1], in_offset=None,
                                                out_offset=bass.IndirectOffsetOnAxis(ap=node7[:, u:u + 1], axis=0)).then_inc(inv_set, 16)
                pool.wait_ge(inv_set, NT * 16)
                pool.wait_ge(info_done, INFO_STEPS)
                t0 = pool.value_load(inf[0:1, I_T0:I_T0 + 1], min_val=0, max_val=NT - 1)
                left = pool.value_load(inf[0:1, I_LEFT:I_LEFT + 1], min_val=1, max_val=NT)
                with pool.Fori(0, left) as i:
                    t = nc.s_assert_within(t0 + i, 0, NT - 1, skip_runtime_bounds_check_because="the tiles from t0 on")
                    n = pool.value_load(inf[0:1, ds(t + I_NW, 1)], min_val=1, max_val=cfg.max_blocks)
                    w0 = pool.value_load(inf[0:1, ds(t + I_CW, 1)], min_val=0, max_val=cfg.max_blocks)
                    with pool.Fori(0, n) as w:
                        pool.wait_ge(win_ready, w0 + w + 1)
                        pool.sem_inc(passed2, 1)
                        pool.indirect_dma_start(out=win[:, :], out_offset=None, in_=copies.rearrange("c (r w) -> (c r) w", w=WIN),
                                                in_offset=bass.IndirectOffsetOnAxis(ap=ridx[:, :], axis=0)).then_inc(win_got, 16)

            @block.vector
            def _(dve):
                dve.wait_ge(made, 6)
                sc = Count(searched)
                dve.memset(zero1[:, :], 0.0)
                dve.memset(one[:, :], 1.0)
                sc.link(dve, dve.tensor_scalar(thr_i, thr_i, ID_BITS, KEY_BASE, ALU.logical_shift_left, ALU.bitwise_or))
                dve.wait_ge(loaded, 16)
                with dve.Fori(0, NTP) as t:
                    dve.wait_ge(searched, t + 1)
                    dve.tensor_scalar(junk[:, 0:NF], firsts_b[:, :], thr[:, ds(t, 1)], 0.0, ALU.is_lt, ALU.add,
                                      accum_out=cnt1[:, ds(t, 1)]).then_inc(searched, 1)
                sc.n += NTP
                sc.wait(dve)
                sc.link(dve, dve.tensor_scalar(q[:, :], cnt1[:, :], -1.0, 0.0, ALU.add, ALU.max))
                sc.link(dve, dve.tensor_copy(qi[:, :], q[:, :]))
                for u in range(2):
                    dve.tensor_copy(q_now[u][:, :], qi[:, u * HALF:(u + 1) * HALF]).then_inc(qready, 1)

                def count_rows(i, u):
                    dve.wait_ge(got_row[u], i * (16 * HALF) + 16 * HALF)
                    for v in range(HALF):
                        t = i * (2 * HALF) + (u * HALF + v)
                        dve.wait_ge(counted, t)
                        col = slice(t, t + 1) if isinstance(t, int) else ds(t, 1)
                        dve.tensor_scalar(junk[:, :], row[u][:, v * COARSE:(v + 1) * COARSE], thr[:, col], 0.0, ALU.is_lt, ALU.add,
                                          accum_out=cnt2[:, col]).then_inc(counted, 1)

                with dve.Fori(0, NSEARCH - 1) as i:
                    for u in range(2):
                        count_rows(i, u)
                        dve.wait_ge(counted, i * (2 * HALF) + (u + 1) * HALF)
                        dve.tensor_copy(q_now[u][:, :], qi[:, ds((i + 1) * (2 * HALF) + u * HALF, HALF)]).then_inc(qready, 1)
                for u in range(2):
                    count_rows(NSEARCH - 1, u)
                dve.wait_ge(counted, NTP)
                sd = Count(startd)
                sd.link(dve, dve.scalar_tensor_tensor(out=start[:, :], in0=q[:, :], scalar=float(COARSE), in1=cnt2[:, :],
                                                      op0=ALU.mult, op1=ALU.add))
                sd.link(dve, dve.tensor_copy(vrow[:, :], vrow_i[:, :]))
                sd.link(dve, dve.tensor_scalar(real[:, :], vrow[:, :], float(N), None, ALU.is_lt))
                sd.link(dve, dve.memset(deg[:, :], 0.0))
                pk = Count(packed)
                pk.link(dve, dve.tensor_scalar(tmp[:, :], real[:, :], float(PAD_RANKS), float(-PAD_RANKS), ALU.mult, ALU.add))
                pk.link(dve, dve.tensor_tensor(tmp_i[:, :], tmp[:, :], vrow[:, :], ALU.add))
                dve.wait_ge(neigh, 32)
                pk.link(dve, dve.tensor_tensor(deg[0:NTP, :], hi[:, :], lo[:, :], ALU.subtract))
                pk.link(dve, dve.scalar_tensor_tensor(out=deg[:, :], in0=deg[:, :], scalar=1.0, in1=real[:, :], op0=ALU.add, op1=ALU.mult))
                pk.link(dve, dve.tensor_scalar(key_i, deg[:, :], float(DEG_BASE), None, ALU.add))
                pk.link(dve, dve.tensor_scalar(key_i, key_i, ID_BITS, None, ALU.logical_shift_left))
                pk.link(dve, dve.tensor_tensor(key_i, key_i, tmp_i[:, :], ALU.bitwise_or))
                so.vector(dve, lambda: None)
                dve.wait_ge(cmp_done, so.total)
                dc = Count(decoded)
                dc.link(dve, dve.tensor_scalar(vrow_i[:, :], res_i, ID_MASK, None, ALU.bitwise_and))
                dc.link(dve, dve.tensor_copy(idf[:, :], vrow_i[:, :]))
                dc.link(dve, dve.tensor_scalar(tmp_i[:, :], res_i, ID_BITS, None, ALU.logical_shift_right))
                dc.link(dve, dve.tensor_scalar(degf[:, :], tmp_i[:, :], -float(DEG_BASE + 1), 0.0, ALU.add, ALU.max))
                dc.link(dve, dve.tensor_copy(tmp[:, :], degf[:, :]))
                dve.wait_ge(turned_ids, 2)
                nd = Count(node_done)
                nd.link(dve, dve.tensor_copy(node_i[:, :], tr[:, 0, :]))
                nd.link(dve, dve.tensor_copy(degt[:, :], tr[:, 1, :]))
                ic = Count(info_done)
                ic.link(dve, dve.memset(inf[:, :], 0))
                dve.wait_ge(md_back, 32)
                ic.link(dve, dve.memset(mdw[:, :], 0))
                ic.link(dve, dve.tensor_scalar(mdi[:, 0:NT], md[:, 0:NT], float(SLOTS - 1), None, ALU.add))
                ic.link(dve, dve.tensor_scalar(mdi[:, 0:NT], mdi[:, 0:NT], 3, None, ALU.logical_shift_right))
                ic.link(dve, dve.tensor_scalar(inf[:, I_NB:I_NB + NT], mdi[:, 0:NT], 1, None, ALU.max))
                ic.link(dve, dve.tensor_scalar(mdw[:, 0:NT], inf[:, I_NB:I_NB + NT], 3, None, ALU.add))
                ic.link(dve, dve.tensor_scalar(inf[:, I_NW:I_NW + NT], mdw[:, 0:NT], 2, None, ALU.logical_shift_right))
                ic.link(dve, dve.memset(cums[:, :], 0.0))
                ic.link(dve, dve.tensor_copy(md[:, 0:NT], inf[:, I_NW:I_NW + NT]))
                ic.link(dve, dve.scalar_tensor_tensor(out=md[:, 0:NT], in0=md[:, 0:NT], scalar=2.0, in1=md[:, 0:NT], op0=ALU.is_gt, op1=ALU.mult))
                for k, sizes in ((0, inf[:, I_NB:I_NB + NT]), (1, md[:, 0:NT])):
                    ic.link(dve, dve.tensor_tensor_scan(cums[:, k * NTP + 1:k * NTP + NTP], one[:, 0:NT], sizes, 0.0,
                                                        ALU.mult, ALU.add))
                ic.link(dve, dve.tensor_copy(inf[:, I_CB:I_CB + 2 * NTP], cums[:, :]))
                ic.link(dve, dve.tensor_scalar(md[:, 0:NT], inf[:, I_NW:I_NW + NT], 2.0, None, ALU.is_le))
                ic.link(dve, dve.tensor_reduce(wide_tiles[:, :], md[:, 0:NT], AX.X, ALU.add))
                ic.link(dve, dve.tensor_scalar(inf[:, I_T0:I_T0 + 1], wide_tiles[:, :], float(NT - 1), None, ALU.min))
                ic.link(dve, dve.tensor_scalar(wide_tiles[:, :], wide_tiles[:, :], -1.0, float(NT), ALU.mult, ALU.add))
                ic.link(dve, dve.tensor_scalar(inf[:, I_LEFT:I_LEFT + 1], wide_tiles[:, :], 1.0, None, ALU.max))
                ic.link(dve, dve.tensor_scalar(mdi[:, 0:1], inf[:, I_CB + NT:I_CB + NT + 1], RING - 1, None, ALU.add))
                ic.link(dve, dve.tensor_scalar(inf[:, I_RINGS:I_RINGS + 1], mdi[:, 0:1], 2, None, ALU.logical_shift_right))
                assert ic.n == INFO_STEPS
                with dve.Fori(0, NT // U) as i:
                    dve.wait_ge(taken7, i)
                    dve.tensor_copy(node7[:, :], node_i[:, ds(i * U + R0, U)]).then_inc(seven, 1)
                    dve.wait_ge(seven_got, i * (U * 16) + U * 16)
                    dve.tensor_copy(start_r[:, ds(i * U, U)], start7[:, :]).then_inc(taken7, 1)
                dve.wait_ge(taken7, NT // U)
                tb = Count(tables)
                tb.link(dve, dve.tensor_copy(si[:, :], start_r[:, :]))
                tb.link(dve, dve.tensor_scalar(row_i[:, 0:NT], si[:, :], 5, None, ALU.logical_shift_right))
                tb.link(dve, dve.tensor_scalar(row_i[:, NT:2 * NT], si[:, :], WIN - 1, None, ALU.bitwise_and))
                tb.link(dve, dve.tensor_scalar(qr[:, :], row_i[:, 0:NT], 1.0, None, ALU.add))
                tb.link(dve, dve.tensor_scalar(cr[:, :], row_i[:, NT:2 * NT], float(cfg.rows), None, ALU.mult))
                for w in range(2):
                    tb.link(dve, dve.tensor_scalar(curs[:, :], qr[:, :], float(w), float(cfg.rows - 1), ALU.add, ALU.min))
                    tb.link(dve, dve.tensor_tensor(ridx_all[:, w, :], curs[:, :], cr[:, :], ALU.add))
                with dve.Fori(0, NT // U) as i:
                    dve.wait_ge(inv_set, i * (U * 16))
                    dve.tensor_copy(rank7[:, :], rank_i[:, ds(i * U, U)]).then_inc(md_done, 1)
                    dve.tensor_copy(node7[:, :], node_i[:, ds(i * U + R0, U)]).then_inc(md_done, 1)
                    dve.tensor_copy(ridx7[:, :, :], ridx_all[:, :, ds(i * U, U)]).then_inc(md_done, 1)
                    dve.wait_ge(md_done, i * 6 + 3)
                    dve.sem_inc(group_ready, 1)
                    dve.tensor_tensor(wmask[:, :, :], iota_2w[:, :].unsqueeze(1).to_broadcast([P, U, 2 * WIN]),
                                      degt[:, ds(i * U + R0, U)].unsqueeze(2).to_broadcast([P, U, 2 * WIN]), ALU.is_lt).then_inc(md_done, 1)
                    dve.wait_ge(md_done, i * 6 + 4)
                    dve.wait_ge(wide_got, i * (2 * U * 16) + 2 * U * 16)
                    dve.scalar_tensor_tensor(out=wmask[:, :, :], in0=wide[:, :].rearrange("p (u w) -> p u w", u=U), scalar=float(-DUMMY),
                                             in1=wmask[:, :, :], op0=ALU.add, op1=ALU.mult).then_inc(md_done, 1)
                    dve.wait_ge(md_done, i * 6 + 5)
                    dve.wait_ge(group_stored, i * (16 * U))
                    dve.tensor_scalar(slots7[:, :].rearrange("p (u w) -> p u w", u=U), wmask[:, :, :], float(DUMMY), None, ALU.add).then_inc(md_done, 1)
                    dve.wait_ge(md_done, i * 6 + 6)
                    dve.sem_inc(group_full, 1)
                t0 = dve.value_load(inf[0:1, I_T0:I_T0 + 1], min_val=0, max_val=NT - 1)
                left = dve.value_load(inf[0:1, I_LEFT:I_LEFT + 1], min_val=1, max_val=NT)
                with dve.Fori(0, left) as i:
                    t = nc.s_assert_within(t0 + i, 0, NT - 1, skip_runtime_bounds_check_because="the tiles from t0 on")
                    n = dve.value_load(inf[0:1, ds(t + I_NW, 1)], min_val=1, max_val=cfg.max_blocks)
                    w0 = dve.value_load(inf[0:1, ds(t + I_CW, 1)], min_val=0, max_val=cfg.max_blocks)
                    a = i * 2 + w0 * 6
                    dve.wait_ge(win_step, a)
                    dve.tensor_copy(cur[:, :], qr[:, ds(t, 1)]).then_inc(win_step, 1)
                    dve.tensor_copy(rem[:, :], degt[:, ds(t + R0, 1)]).then_inc(win_step, 1)
                    with dve.Fori(0, n) as w:
                        b = i * 2 + w0 * 6 + w * 6 + 2
                        dve.wait_ge(win_step, b)
                        dve.tensor_scalar(ridx[:, :], cur[:, :], float(cfg.rows - 1), cr[:, ds(t, 1)], ALU.min, ALU.add).then_inc(win_step, 1)
                        dve.wait_ge(win_step, b + 1)
                        dve.sem_inc(win_ready, 1)
                        dve.tensor_scalar(mask[:, :], iota_w[:, :], rem[:, 0:1], None, ALU.is_lt).then_inc(win_step, 1)
                        dve.tensor_scalar(cur[:, :], cur[:, :], 1.0, None, ALU.add).then_inc(win_step, 1)
                        dve.wait_ge(win_step, b + 3)
                        dve.tensor_scalar(rem[:, :], rem[:, :], float(-WIN), None, ALU.add).then_inc(win_step, 1)
                        dve.wait_ge(win_got, (w0 + w + 1) * 16)
                        dve.scalar_tensor_tensor(out=picked[:, :], in0=win[:, :], scalar=float(-DUMMY), in1=mask[:, :],
                                                 op0=ALU.add, op1=ALU.mult).then_inc(win_step, 1)
                        dve.wait_ge(win_step, b + 5)
                        dve.wait_ge(win_stored, (w0 + w) * 16)
                        dve.tensor_scalar(slots[:, :], picked[:, :], float(DUMMY), None, ALU.add).then_inc(win_step, 1)
                        dve.wait_ge(win_step, b + 6)
                        dve.sem_inc(win_full, 1)

            @block.tensor
            def _(pe):
                so.tensor(pe, lambda: None)
                pe.wait_ge(decoded, 5)
                pe.transpose(tr[:, 0, :], idf[:, :], S["ident"][0:64, 0:64]).then_inc(turned_ids, 1)
                pe.transpose(tr[:, 1, :], degf[:, :], S["ident"][0:64, 0:64]).then_inc(turned_ids, 1)

            @block.scalar
            def _(act):
                so.scalar(act)


def constants(nc, outer):
    S = {"ident": outer.sb("ident", [P, P]), "sign": outer.sb("sign", [P, 8]), "keep": outer.st}
    with Scope(nc, "const") as s:
        pi, sh, g = s.sb("pi", [P, 1], I32), s.sb("sh", [P, 1], I32), s.sb("g", [P, 8], I32)
        gf = s.sb("gf", [P, 8])
        made, step = s.sem("made"), s.sem("step")
        with nc.Block() as block:
            @block.gpsimd
            def _(pool):
                pool.memset(S["ident"][:, :], 0.0).then_inc(made, 1)
                pool.iota(pi[:, :], [[0, 1]], base=0, channel_multiplier=1).then_inc(made, 1)
                pool.wait_ge(made, 2)
                pool.affine_select(out=S["ident"][:, :], in_=S["ident"][:, :], compare_op=ALU.not_equal, fill=1.0, base=0,
                                   pattern=[[-1, P]], channel_multiplier=1).then_inc(made, 1)

            @block.vector
            def _(dve):
                dve.wait_ge(made, 3)
                st = Count(step)
                st.link(dve, dve.tensor_scalar(sh[:, :], pi[:, :], 1, None, ALU.logical_shift_left))
                st.link(dve, dve.tensor_tensor(sh[:, :], sh[:, :], pi[:, :], ALU.bitwise_xor))
                for r in range(8):
                    st.inc(dve.tensor_scalar(g[:, r:r + 1], sh[:, :], r, 1, ALU.logical_shift_right, ALU.bitwise_and))
                st.wait(dve)
                st.link(dve, dve.tensor_copy(gf[:, :], g[:, :]))
                st.link(dve, dve.tensor_scalar(S["sign"][:, :], gf[:, :], -2.0, 1.0, ALU.mult, ALU.add))
    return S


def aggregate(nc, cfg, H, C, table, own_rows, info, ell, out, self_loop, S, ffn=None):
    CW = H * (C + 1)
    RW = CW + 2 * H
    HB, HT = 9, 4 if self_loop else 3
    TT = HT + 2
    with Scope(nc, f"agg{cfg.name}", S["keep"]) as s:
        inf = s.sb("info", [1, INFO], I32)
        idx = [s.sb(f"idx{i}", [P, SLOTS], I32) for i in range(RING)]
        ring = s.sb("ring", [P, RING * SLOTS * RW])
        own = s.sb("own", [P, 2 * RW])
        er = s.sb("er", [P, H])
        score = s.sb("score", [P, (SLOTS + 1) * H])
        prob = s.sb("prob", [P, (SLOTS + 1) * H])
        m, bm, mn = s.sb("m", [P, H]), s.sb("bm", [P, H]), s.sb("mn", [P, H])
        weighted, summed, acc = s.sb("weighted", [P, SLOTS * CW]), s.sb("summed", [P, CW]), s.sb("acc", [P, CW])
        den, res = s.sb("den", [P, H]), s.sb("res", [P, H * C])
        info_in, start_pool, ready, freed = s.sem("info_in"), s.sem("start_pool"), s.sem("ready"), s.sem("freed")
        idx_in = [s.sem(f"idx_in{i}") for i in range(RING)]
        got = [s.pool_sem(f"got{i}") for i in range(RING)]
        sp_passed, act_passed = s.sem("sp_passed"), s.sem("act_passed")
        own_in, tstep, bstep = s.sem("own_in"), s.sem("tstep"), s.sem("bstep")
        scored, probs, tile_done, out_stored = s.sem("scored"), s.sem("probs"), s.sem("tile_done"), s.sem("out_stored")
        if ffn:
            ffn.allocate(nc, s)
        with nc.Block() as block:
            @block.sync
            def _(sp):
                sp.dma_start(inf[:, :], info).then_inc(info_in, 16)
                sp.wait_ge(info_in, 16)
                rings = sp.value_load(inf[0:1, I_RINGS:I_RINGS + 1], min_val=1, max_val=cfg.max_blocks // RING - 2)
                for i in range(RING):
                    sp.dma_start(idx[i][:, :], ell[i, :, :]).then_inc(idx_in[i], 16)
                with sp.Fori(0, rings) as r:
                    for i in range(RING):
                        sp.wait_ge(got[i], (r + 1) * (16 * SLOTS))
                        sp.sem_inc(ready, 1)
                        nxt = nc.s_assert_within(r * RING + (i + RING), 0, cfg.max_blocks - 1,
                                                 skip_runtime_bounds_check_because="the list ends in two rings of empty blocks")
                        sp.dma_start(idx[i][:, :], ell[ds(nxt, 1), :, :].rearrange("b p j -> (b p) j")).then_inc(idx_in[i], 16)
                for i in range(RING):
                    sp.wait_ge(idx_in[i], (rings + 1) * 16)
                    sp.sem_inc(sp_passed, 1)

            @block.gpsimd
            def _(pool):
                pool.wait_ge(info_in, 16)
                rings = pool.value_load(inf[0:1, I_RINGS:I_RINGS + 1], min_val=1, max_val=cfg.max_blocks // RING - 2)
                with pool.Fori(0, rings) as r:
                    for i in range(RING):
                        pool.wait_ge(freed, r * RING + i + 1)
                        pool.wait_ge(idx_in[i], (r + 1) * 16)
                        pool.sem_inc(start_pool, 1)
                        for j in range(SLOTS):
                            at = (i * SLOTS + j) * RW
                            pool.indirect_dma_start(out=ring[:, at:at + RW], out_offset=None, in_=table,
                                                    in_offset=bass.IndirectOffsetOnAxis(ap=idx[i][:, j:j + 1], axis=0)).then_inc(got[i], 16)

            @block.vector
            def _(dve):
                dve.sem_inc(freed, RING)
                dve.wait_ge(info_in, 16)
                with dve.Fori(0, NT) as t:
                    n = dve.value_load(inf[0:1, ds(t + I_NB, 1)], min_val=1, max_val=cfg.max_blocks)
                    c0 = dve.value_load(inf[0:1, ds(t + I_CB, 1)], min_val=0, max_val=cfg.max_blocks)
                    mine = (t % 2) * RW
                    a = t * TT
                    dve.wait_ge(own_in, t * 16 + 16)
                    dve.wait_ge(tstep, a)
                    dve.tensor_copy(er[:, :], own[:, ds(mine + CW + H, H)]).then_inc(tstep, 1)
                    if self_loop:
                        dve.tensor_tensor(m[:, :], own[:, ds(mine + CW, H)], own[:, ds(mine + CW + H, H)], ALU.add).then_inc(tstep, 1)
                        dve.wait_ge(tstep, a + 2)
                        dve.scalar_tensor_tensor(out=m[:, :], in0=m[:, :], scalar=0.2, in1=m[:, :], op0=ALU.mult, op1=ALU.max).then_inc(tstep, 1)
                        dve.tensor_copy(acc[:, :], own[:, ds(mine, CW)]).then_inc(tstep, 1)
                    else:
                        dve.memset(m[:, :], NEG).then_inc(tstep, 1)
                        dve.memset(acc[:, :], 0.0).then_inc(tstep, 1)
                    with dve.Fori(0, n) as b:
                        g = c0 + b
                        k = g * HB
                        at = (g % RING) * (SLOTS * RW)
                        rows = ring[:, ds(at, SLOTS * RW)].rearrange("p (j w) -> p j w", w=RW)
                        sc3 = score[:, 0:SLOTS * H].rearrange("p (j h) -> p j h", h=H)
                        dve.wait_ge(ready, g + 1)
                        dve.wait_ge(tstep, a + HT)
                        dve.wait_ge(bstep, k)
                        dve.tensor_tensor(sc3, rows[:, :, CW:CW + H], er[:, :].unsqueeze(1).to_broadcast([P, SLOTS, H]), ALU.add).then_inc(bstep, 1)
                        dve.wait_ge(bstep, k + 1)
                        dve.scalar_tensor_tensor(out=sc3, in0=sc3, scalar=0.2, in1=sc3, op0=ALU.mult, op1=ALU.max).then_inc(bstep, 1)
                        dve.wait_ge(bstep, k + 2)
                        dve.tensor_reduce(bm[:, :], sc3.rearrange("p j h -> p h j"), AX.X, ALU.max).then_inc(bstep, 1)
                        dve.wait_ge(bstep, k + 3)
                        dve.tensor_tensor(mn[:, :], m[:, :], bm[:, :], ALU.max).then_inc(bstep, 1)
                        dve.wait_ge(bstep, k + 4)
                        dve.tensor_tensor(score[:, SLOTS * H:], m[:, :], mn[:, :], ALU.subtract)
                        dve.tensor_tensor(sc3, sc3, mn[:, :].unsqueeze(1).to_broadcast([P, SLOTS, H]), ALU.subtract).then_inc(scored, 1)
                        dve.wait_ge(scored, g + 1)
                        dve.tensor_copy(m[:, :], mn[:, :]).then_inc(bstep, 1)
                        dve.wait_ge(probs, g + 1)
                        dve.tensor_tensor(weighted[:, :].rearrange("p (j h c) -> p j h c", j=SLOTS, h=H),
                                          rows[:, :, 0:CW].rearrange("p j (h c) -> p j h c", h=H),
                                          prob[:, 0:SLOTS * H].rearrange("p (j h) -> p j h", h=H).unsqueeze(3).to_broadcast([P, SLOTS, H, C + 1]),
                                          ALU.mult).then_inc(bstep, 1)
                        dve.tensor_tensor(acc[:, :].rearrange("p (h c) -> p h c", h=H), acc[:, :].rearrange("p (h c) -> p h c", h=H),
                                          prob[:, SLOTS * H:].unsqueeze(2).to_broadcast([P, H, C + 1]), ALU.mult).then_inc(bstep, 1)
                        dve.wait_ge(bstep, k + 7)
                        dve.sem_inc(freed, 1)
                        dve.tensor_reduce(summed[:, :], weighted[:, :].rearrange("p (j w) -> p w j", j=SLOTS), AX.X, ALU.add).then_inc(bstep, 1)
                        dve.wait_ge(bstep, k + 8)
                        dve.tensor_tensor(acc[:, :], acc[:, :], summed[:, :], ALU.add).then_inc(bstep, 1)
                    c1 = dve.value_load(inf[0:1, ds(t + (I_CB + 1), 1)], min_val=0, max_val=cfg.max_blocks)
                    dve.wait_ge(bstep, c1 * HB)
                    acc3 = acc[:, :].rearrange("p (h c) -> p h c", h=H)
                    if self_loop:
                        dve.tensor_scalar(den[:, :], acc3[:, :, C], 1e-16, None, ALU.add).then_inc(tstep, 1)
                    else:
                        dve.tensor_scalar(den[:, :], acc3[:, :, C], 1e-16, None, ALU.max).then_inc(tstep, 1)
                    dve.wait_ge(tstep, a + HT + 1)
                    dve.reciprocal(den[:, :], den[:, :]).then_inc(tstep, 1)
                    dve.wait_ge(tstep, a + HT + 2)
                    dve.wait_ge(out_stored, t * 16)
                    dve.tensor_tensor(res[:, :].rearrange("p (h c) -> p h c", h=H), acc3[:, :, 0:C],
                                      den[:, :].unsqueeze(2).to_broadcast([P, H, C]), ALU.mult).then_inc(tile_done, 1)
                    dve.wait_ge(tile_done, t + 1)

            @block.scalar
            def _(act):
                act.wait_ge(info_in, 16)
                act.dma_start(own[:, 0:RW], own_rows[0:P, :]).then_inc(own_in, 16)
                if ffn:
                    ffn.first(act)
                with act.Fori(0, NT) as t:
                    n = act.value_load(inf[0:1, ds(t + I_NB, 1)], min_val=1, max_val=cfg.max_blocks)
                    c0 = act.value_load(inf[0:1, ds(t + I_CB, 1)], min_val=0, max_val=cfg.max_blocks)
                    act.wait_ge(own_in, t * 16 + 16)
                    act.dma_start(own[:, ds(((t + 1) % 2) * RW, RW)], own_rows[ds((t + 1) * P, P), :]).then_inc(own_in, 16)
                    with act.Fori(0, n) as b:
                        act.wait_ge(scored, c0 + b + 1)
                        act.activation(prob[:, :], score[:, :], ACT.Exp).then_inc(probs, 1)
                    if ffn:
                        ffn.scalar(act, t)
                    act.wait_ge(tile_done, t + 1)
                    act.dma_start(out[ds(t * P, P), :], res[:, :]).then_inc(out_stored, 16)
                    act.wait_ge(out_stored, t * 16 + 16)
                act.wait_ge(own_in, (NT + 1) * 16)
                if ffn:
                    ffn.scalar(act, NT)
                    act.wait_ge(ffn.y_stored, NTP * 16)

            if ffn:
                @block.tensor
                def _(pe):
                    pe.wait_ge(ffn.weights_in, ffn.nweights * 16)
                    with pe.Fori(0, NTP) as t:
                        ffn.tensor(pe, t)


class SmallExperts:
    EX, HID = 4, 512

    def __init__(self, xt, w1, b1, w2, b2, y, S):
        self.xt_d, self.w1_d, self.b1_d, self.w2_d, self.b2_d, self.y_d, self.S = xt, w1, b1, w2, b2, y, S

    def allocate(self, nc, s):
        EX, HID = self.EX, self.HID
        self.xt = s.sb("xt", [P, 2 * P])
        self.w1 = s.sb("w1", [P, EX * 2 * HID])
        self.w2 = s.sb("w2", [P, EX * 4 * D])
        self.b1, self.b2, self.ones = s.sb("b1", [1, EX * HID]), s.sb("b2", [1, EX * D]), s.sb("ones", [1, P])
        self.h, self.ht = s.sb("h", [P, 2 * HID]), s.sb("ht", [P, 2 * HID])
        self.ysb = s.sb("ysb", [P, EX * D])
        self.hp, self.tp, self.yp = s.ps("hp", [P, 2 * HID]), s.ps("tp", [P, 2 * HID]), s.ps("yp", [P, EX * D])
        self.weights_in, self.xt_in, self.h_made, self.gelu = s.sem("weights_in"), s.sem("xt_in"), s.sem("h_made"), s.sem("gelu")
        self.turned, self.ht_made, self.y_made, self.y_copied, self.y_stored = [s.sem(n) for n in ("turned", "ht_made", "y_made", "y_copied", "y_stored")]
        self.xt_used, self.ones_made = s.sem("xt_used"), s.sem("ones_made")
        self.nweights = 4

    def first(self, act):
        act.dma_start(self.w1[:, :].rearrange("p (e k n) -> p e k n", e=self.EX, k=2), self.w1_d.rearrange("e (k p) n -> p e k n", p=P)).then_inc(self.weights_in, 16)
        act.dma_start(self.w2[:, :].rearrange("p (e k n) -> p e k n", e=self.EX, k=4), self.w2_d.rearrange("e (k p) n -> p e k n", p=P)).then_inc(self.weights_in, 16)
        act.dma_start(self.b1[:, :], self.b1_d.rearrange("(a e) n -> a (e n)", a=1)).then_inc(self.weights_in, 16)
        act.dma_start(self.b2[:, :], self.b2_d.rearrange("(a e) n -> a (e n)", a=1)).then_inc(self.weights_in, 16)
        act.activation(self.ones[:, :], self.S["ident"][0:1, :], ACT.Copy, scale=0.0, bias=1.0).then_inc(self.ones_made, 1)
        act.dma_start(self.xt[:, :], self.xt_d[0, :, :]).then_inc(self.xt_in, 16)

    def scalar(self, act, t):
        EX, HID = self.EX, self.HID

        def gelu(e):
            act.wait_ge(self.h_made, t * EX + e + 1)
            half = slice((e % 2) * HID, (e % 2 + 1) * HID)
            act.activation(self.h[:, half], self.hp[:, half], ACT.Gelu).then_inc(self.gelu, 1)

        def turn(e):
            act.wait_ge(self.turned, t * EX + e + 1)
            half = slice((e % 2) * HID, (e % 2 + 1) * HID)
            act.activation(self.ht[:, half], self.tp[:, half], ACT.Copy).then_inc(self.ht_made, 1)

        gelu(0)
        for e in range(1, EX):
            gelu(e)
            turn(e - 1)
        turn(EX - 1)
        act.wait_ge(self.xt_used, t + 1)
        act.wait_ge(self.xt_in, t * 16 + 16)
        if not isinstance(t, int):
            act.dma_start(self.xt[:, :], self.xt_d[ds(t + 1, 1), :, :].rearrange("a p n -> (a p) n")).then_inc(self.xt_in, 16)
        act.wait_ge(self.y_made, t * EX + EX)
        act.wait_ge(self.y_stored, t * 16)
        act.activation(self.ysb[:, :], self.yp[:, :], ACT.Copy).then_inc(self.y_copied, 1)
        act.wait_ge(self.y_copied, t + 1)
        dst = self.y_d[t * P:(t + 1) * P, :] if isinstance(t, int) else self.y_d[ds(t * P, P), :]
        act.dma_start(dst, self.ysb[:, :]).then_inc(self.y_stored, 16)

    def tensor(self, pe, t):
        EX, HID = self.EX, self.HID
        pe.wait_ge(self.ones_made, 1)
        pe.wait_ge(self.xt_in, t * 16 + 16)

        def hidden(e):
            half = self.hp[:, (e % 2) * HID:(e % 2 + 1) * HID]
            if e < 2:
                pe.wait_ge(self.gelu, t * EX)
            else:
                pe.wait_ge(self.gelu, t * EX + e - 1)
            for k in range(2):
                pe.matmul(half, self.xt[:, k * P:(k + 1) * P], self.w1[:, (e * 2 + k) * HID:(e * 2 + k + 1) * HID], start=(k == 0), stop=False)
            mm = pe.matmul(half, self.ones[:, :], self.b1[:, e * HID:(e + 1) * HID], start=False, stop=True)
            mm.then_inc(self.h_made, 1)
            if e == EX - 1:
                pe.wait_ge(self.h_made, t * EX + EX)
                pe.sem_inc(self.xt_used, 1)

        def second(e):
            off = (e % 2) * HID
            pe.wait_ge(self.gelu, t * EX + e + 1)
            if e < 2:
                pe.wait_ge(self.ht_made, t * EX)
            else:
                pe.wait_ge(self.ht_made, t * EX + e - 1)
            for c in range(4):
                mm = pe.transpose(self.tp[:, off + c * P:off + (c + 1) * P], self.h[:, off + c * P:off + (c + 1) * P], self.S["ident"][:, :])
            mm.then_inc(self.turned, 1)
            pe.wait_ge(self.ht_made, t * EX + e + 1)
            if e == 0:
                pe.wait_ge(self.y_copied, t)
            y = self.yp[:, e * D:(e + 1) * D]
            for c in range(4):
                pe.matmul(y, self.ht[:, off + c * P:off + (c + 1) * P], self.w2[:, (e * 4 + c) * D:(e * 4 + c + 1) * D], start=(c == 0), stop=False)
            pe.matmul(y, self.ones[:, :], self.b2[:, e * D:(e + 1) * D], start=False, stop=True).then_inc(self.y_made, 1)

        hidden(0)
        for e in range(1, EX):
            hidden(e)
            second(e - 1)
        second(EX - 1)


U = 5
ROUNDS = NTP // U


def choose(dve, st, score, E, tri, work, sel, prob, eps):
    gt, eq, rank, keep, mx, z = work
    si = score.unsqueeze(3).to_broadcast([P, U, E, E])
    sj = score.unsqueeze(2).to_broadcast([P, U, E, E])
    st.inc(dve.tensor_tensor(gt, sj, si, ALU.is_gt))
    st.link(dve, dve.tensor_tensor(eq, sj, si, ALU.is_equal))
    st.link(dve, dve.tensor_tensor(eq, eq, tri.unsqueeze(1).to_broadcast([P, U, E, E]), ALU.mult))
    st.link(dve, dve.tensor_tensor(gt, gt, eq, ALU.add))
    st.link(dve, dve.tensor_reduce(rank, gt, AX.X, ALU.add))
    st.inc(dve.tensor_scalar(keep, rank, 1.5, None, ALU.is_lt))
    st.link(dve, dve.tensor_reduce(mx, score, AX.X, ALU.max))
    st.link(dve, dve.tensor_tensor(prob, score, mx.unsqueeze(2).to_broadcast([P, U, E]), ALU.subtract))


def dense(nc, k, H, C, x_in, x_out, table, own_rows, inv_next, weights, S, agg=None, inv=None, extra=None):
    last = k == 3
    CW = H * (C + 1) if not last else 0
    RW = CW + 2 * H if not last else 8
    W = H * C + 2 * H if not last else 8
    with Scope(nc, f"dense{k}", S["keep"]) as s:
        x = s.sb("x", [P, U * D])
        xn = s.sb("xn", [P, U * D])
        stats, mv = s.sb("stats", [P, U * 6]), s.sb("mv", [P, U * 2])
        rstd = s.sb("rstd", [P, U])
        eps = s.sb("eps", [P, 1])
        xt = s.sb("xt", [P, U * D])
        wcat = s.sb("wcat", [P, 2 * W])
        rows = s.sb("rows", [P, U * RW])
        tp, mp = s.ps("tp", [P, 3 * 512]), s.ps("mp", [P, U * 512])
        w_in, w_step, w_ready, made = s.sem("w_in"), s.sem("w_step"), s.sem("w_ready"), s.sem("made")
        x_in_s, x_read, got, inv_in, inv_set = s.sem("x_in"), s.sem("x_read"), s.pool_sem("got"), s.sem("inv_in"), s.sem("inv_set")
        step, var_done, std_done, normed, turned, xt_made, product, rows_made = [s.sem(n) for n in
            ("step", "var_done", "std_done", "normed", "turned", "xt_made", "product", "rows_made")]
        x_stored, t_stored, t_scattered, dve_passed, o_stored, sp_passed, pool_passed, gathered_used, summed = [s.pool_sem(n) if n == "t_scattered" else s.sem(n) for n in
            ("x_stored", "t_stored", "t_scattered", "dve_passed", "o_stored", "sp_passed", "pool_passed", "gathered_used", "summed")]
        if not last:
            inv_n, inv_n5 = s.sb("inv_n", [P, NTP], I32), s.sb("inv_n5", [P, U], I32)
        if k:
            inv_a, inv_a5 = s.sb("inv_a", [P, NTP], I32), s.sb("inv_a5", [P, U], I32)
            GW = 16 if k == 2 else D
            gat = s.sb("gathered", [P, U * GW])
        if k == 2:
            y = s.sb("y", [P, U * 4 * D])
            lnw, lnb, bg = s.sb("gamma", [P, 16]), s.sb("beta", [P, 16]), s.sb("b_gat", [P, 16])
            sq, ssum = s.sb("sq", [P, U * 16]), s.sb("ssum", [P, U])
            sc_std = s.sb("sc_std", [P, U])
        if last:
            bias = s.sb("bias", [P, D])
        if k >= 2:
            E = 4 if k == 2 else 8
            tri, tri_i = s.sb("tri", [P, E, E]), s.sb("tri_i", [P, E, E], I32)
            score = s.sb("score", [P, U, E])
            gt, eq, rank, keep = s.sb("gt", [P, U, E, E]), s.sb("eq", [P, U, E, E]), s.sb("rank", [P, U, E]), s.sb("keep", [P, U, E])
            mx, z, prob = s.sb("mx", [P, U]), s.sb("z", [P, U]), s.sb("prob", [P, U, E])
            sc_ready, sc_exp, sc_sq, sc_rt = s.sem("sc_ready"), s.sem("sc_exp"), s.sem("sc_sq"), s.sem("sc_rt")
        x3 = x[:, :].rearrange("p (u d) -> p u d", u=U)
        xn3 = xn[:, :].rearrange("p (u d) -> p u d", u=U)
        mv3 = mv[:, :].rearrange("p (u a) -> p u a", u=U)
        rows3 = rows[:, :].rearrange("p (u w) -> p u w", u=U)
        mp3 = mp[:, :].rearrange("p (u w) -> p u w", u=U)
        if k == 0:
            w_nat = s.sb("w_nat", [P, 2 * D])
        if not last:
            a_l, a_r = s.sb("a_l", [P, H * C]), s.sb("a_r", [P, H * C])
            fold = s.sb("fold", [P, H * C])
        nw = {0: 3, 1: 3, 2: 3 + 3, 3: 3}[k] + 0
        nw = {0: 3, 1: 3, 2: 3 + H - 1 + 3, 3: 2}[k]
        wc3 = wcat[:, :].rearrange("p (k w) -> p k w", k=2)
        NINV = (0 if last else 1) + (1 if k else 0)
        with nc.Block() as block:
            @block.sync
            def _(sp):
                if k == 0:
                    sp.dma_start(w_nat[:, :].rearrange("p (a d) -> p a d", a=2), weights["w"].rearrange("(a p) d -> p a d", p=P)).then_inc(w_in, 16)
                elif k == 1:
                    sp.dma_start(wc3[:, :, 0:H * C], weights["w"].rearrange("(k p) n -> p k n", p=P)).then_inc(w_in, 16)
                elif k == 2:
                    for h in range(H):
                        sp.dma_start(wc3[:, :, h * C:(h + 1) * C], weights["w"][h].rearrange("(k p) c -> p k c", p=P)).then_inc(w_in, 16)
                    for t, src in ((lnw, "gamma"), (lnb, "beta"), (bg, "b_gat")):
                        sp.dma_start(t[:, :], weights[src].rearrange("(a n) -> a n", a=1).to_broadcast([P, 16])).then_inc(w_in, 16)
                else:
                    with nc.allow_non_contiguous_dma(reason="2048 words, transposed"):
                        for kc in range(2):
                            sp.dma_start(wc3[:, kc, :], weights["w"][:, kc * P:(kc + 1) * P].rearrange("e p -> p e")).then_inc(w_in, 16)
                    sp.dma_start(bias[:, :], weights["bias"].rearrange("(a n) -> a n", a=1).to_broadcast([P, D])).then_inc(w_in, 16)
                if not last:
                    sp.dma_start(a_l[:, :], weights["neigh"].to_broadcast([P, H * C])).then_inc(w_in, 16)
                    sp.dma_start(a_r[:, :], weights["mine"].to_broadcast([P, H * C])).then_inc(w_in, 16)
                    with nc.allow_non_contiguous_dma(reason="node order"):
                        sp.dma_start(inv_n[:, :], inv_next.rearrange("(t p) -> p t", p=P)).then_inc(inv_in, 16)
                if k:
                    with nc.allow_non_contiguous_dma(reason="node order"):
                        sp.dma_start(inv_a[:, :], inv.rearrange("(t p) -> p t", p=P)).then_inc(inv_in, 16)
                with sp.Fori(0, ROUNDS) as i:
                    r0 = i * (U * P)
                    sp.wait_ge(x_read, i)
                    sp.sem_inc(sp_passed, 1)
                    if k:
                        sp.wait_ge(x_stored, i * 16)
                        sp.sem_inc(sp_passed, 1)
                    sp.dma_start(x3, x_in[ds(r0, U * P), :].rearrange("(u p) d -> p u d", p=P)).then_inc(x_in_s, 16)
                    if k == 2:
                        sp.dma_start(y[:, :].rearrange("p (u d) -> p u d", u=U), extra["y"][ds(r0, U * P), :].rearrange("(u p) d -> p u d", p=P)).then_inc(x_in_s, 16)
                    if k:
                        sp.wait_ge(summed, i + 1)
                        sp.sem_inc(sp_passed, 1)
                        sp.dma_start(x_out[ds(r0, U * P), :].rearrange("(u p) d -> p u d", p=P), x3).then_inc(x_stored, 16)
                    if k == 1:
                        sp.wait_ge(xt_made, i + 1)
                        sp.sem_inc(sp_passed, 1)
                        sp.dma_start(extra["xt"][ds(i * U, U), :, :].rearrange("u p n -> p u n"), xt[:, :].rearrange("p (u n) -> p u n", u=U)).then_inc(o_stored, 16)
                    if last:
                        sp.wait_ge(normed, i + 1)
                        sp.sem_inc(sp_passed, 1)
                        sp.dma_start(extra["xn"][ds(r0, U * P), :].rearrange("(u p) d -> p u d", p=P), xn3).then_inc(o_stored, 16)
                    else:
                        sp.wait_ge(rows_made, i * 2 + 2)
                        sp.sem_inc(sp_passed, 1)
                        sp.dma_start(table[ds(r0, U * P), :].rearrange("(u p) d -> p u d", p=P), rows3).then_inc(t_stored, 16)
                if k:
                    sp.wait_ge(x_stored, ROUNDS * 16)
                if k in (1, 3):
                    sp.wait_ge(o_stored, ROUNDS * 16)
                if not last:
                    sp.wait_ge(t_stored, ROUNDS * 16)
                    sp.wait_ge(t_scattered, ROUNDS * 16 * U)

            @block.gpsimd
            def _(pool):
                if k >= 2:
                    pool.iota(tri_i[:, :, :], [[1, E], [-1, E]], base=0, channel_multiplier=0).then_inc(made, 1)
                with pool.Fori(0, ROUNDS) as i:
                    if k:
                        pool.wait_ge(inv_set, i * NINV + NINV)
                        pool.wait_ge(gathered_used, i)
                        pool.sem_inc(pool_passed, 1)
                        for u in range(U):
                            pool.indirect_dma_start(out=gat[:, u * GW:(u + 1) * GW], out_offset=None, in_=agg,
                                                    in_offset=bass.IndirectOffsetOnAxis(ap=inv_a5[:, u:u + 1], axis=0)).then_inc(got, 16)
                    if not last:
                        pool.wait_ge(inv_set, i * NINV + NINV)
                        pool.wait_ge(rows_made, i * 2 + 2)
                        pool.sem_inc(pool_passed, 1)
                        for u in range(U):
                            pool.indirect_dma_start(out=own_rows, in_=rows[:, u * RW:(u + 1) * RW], in_offset=None,
                                                    out_offset=bass.IndirectOffsetOnAxis(ap=inv_n5[:, u:u + 1], axis=0)).then_inc(t_scattered, 16)

            @block.vector
            def _(dve):
                ws = Count(w_step)
                ws.link(dve, dve.memset(eps[:, :], 1e-5))
                if k >= 2:
                    dve.wait_ge(made, 1)
                    ws.link(dve, dve.tensor_scalar(tri[:, :, :], tri_i[:, :, :], 0.5, None, ALU.is_gt))
                if not last:
                    if CW:
                        ws.link(dve, dve.memset(rows[:, :], 1.0))
                    dve.wait_ge(w_in, nw * 16)
                    if k == 0:
                        dve.wait_ge(w_ready, 1)
                        for kc in range(2):
                            ws.link(dve, dve.tensor_copy(wc3[:, kc, 0:D], tp[:, kc * D:(kc + 1) * D]))
                    for kc in range(2):
                        for side, a in ((0, a_l), (1, a_r)):
                            ws.link(dve, dve.tensor_tensor(fold[:, :], wc3[:, kc, 0:H * C], a[:, :], ALU.mult))
                            ws.link(dve, dve.tensor_reduce(wc3[:, kc, H * C + side * H:H * C + (side + 1) * H],
                                                           fold[:, :].rearrange("p (h c) -> p h c", h=H), AX.X, ALU.add))
                else:
                    dve.wait_ge(w_in, 48)
                ws.link(dve, dve.memset(rstd[:, :], 0.0))
                dve.sem_inc(w_ready, 1)
                if NINV:
                    dve.wait_ge(inv_in, NINV * 16)

                def body(i, st):
                    if not last:
                        dve.wait_ge(t_scattered, i * (16 * U))
                        dve.tensor_copy(inv_n5[:, :], inv_n[:, ds(i * U, U)]).then_inc(inv_set, 1)
                    if k:
                        dve.wait_ge(got, i * (U * 16))
                        dve.tensor_copy(inv_a5[:, :], inv_a[:, ds(i * U, U)]).then_inc(inv_set, 1)
                        dve.wait_ge(x_in_s, i * (32 if k == 2 else 16) + (32 if k == 2 else 16))
                        dve.wait_ge(got, i * (U * 16) + U * 16)
                    if k in (1, 3):
                        ins = st.inc(dve.tensor_tensor(x[:, :], x[:, :], gat[:, :], ALU.add))
                        st.wait(dve)
                        dve.sem_inc(gathered_used, 1)
                        if last:
                            st.link(dve, dve.tensor_tensor(x3, x3, bias[:, :].unsqueeze(1).to_broadcast([P, U, D]), ALU.add))
                        dve.sem_inc(summed, 1)
                    elif k == 2:
                        g3 = gat[:, :].rearrange("p (u c) -> p u c", u=U)
                        b3 = lambda t: t[:, :].unsqueeze(1).to_broadcast([P, U, 16])
                        w3 = lambda t: t[:, :].unsqueeze(2).to_broadcast([P, U, 16])
                        sq3 = sq[:, :].rearrange("p (u c) -> p u c", u=U)
                        st.link(dve, dve.tensor_tensor(sq3, g3, b3(bg), ALU.add))
                        dve.sem_inc(gathered_used, 1)
                        st.link(dve, dve.tensor_reduce(ssum[:, :], sq3, AX.X, ALU.add))
                        st.link(dve, dve.tensor_scalar(ssum[:, :], ssum[:, :], -1.0 / 16, None, ALU.mult))
                        st.link(dve, dve.tensor_tensor(sq3, sq3, w3(ssum), ALU.add))
                        st.link(dve, dve.tensor_tensor(g3, sq3, sq3, ALU.mult))
                        st.link(dve, dve.tensor_reduce(ssum[:, :], g3, AX.X, ALU.add))
                        st.link(dve, dve.tensor_scalar(ssum[:, :], ssum[:, :], 1.0 / 16, 1e-5, ALU.mult, ALU.add))
                        dve.sem_inc(sc_sq, 1)
                        dve.wait_ge(sc_rt, i + 1)
                        st.link(dve, dve.reciprocal(sc_std[:, :], sc_std[:, :]))
                        st.link(dve, dve.tensor_tensor(sq3, sq3, w3(sc_std), ALU.mult))
                        st.link(dve, dve.tensor_tensor(sq3, sq3, b3(lnw), ALU.mult))
                        st.link(dve, dve.tensor_tensor(sq3, sq3, b3(lnb), ALU.add))
                        st.link(dve, dve.tensor_reduce(score[:, :, :], sq[:, :].rearrange("p (u h e) -> p u e h", u=U, h=4), AX.X, ALU.add))
                        st.link(dve, dve.tensor_scalar(score[:, :, :], score[:, :, :], 0.25, None, ALU.mult))
                        choose(dve, st, score[:, :, :], E, tri[:, :, :], (gt[:, :, :, :], eq[:, :, :, :], rank[:, :, :], keep[:, :, :], mx[:, :], z[:, :]), None, prob[:, :, :], 0.0)
                        dve.sem_inc(sc_ready, 1)
                        dve.wait_ge(sc_exp, i + 1)
                        st.link(dve, dve.tensor_tensor(prob[:, :, :], prob[:, :, :], keep[:, :, :], ALU.mult))
                        st.link(dve, dve.tensor_reduce(z[:, :], prob[:, :, :], AX.X, ALU.add))
                        st.link(dve, dve.reciprocal(z[:, :], z[:, :]))
                        st.link(dve, dve.tensor_tensor(prob[:, :, :], prob[:, :, :], z[:, :].unsqueeze(2).to_broadcast([P, U, E]), ALU.mult))
                        for e in range(E):
                            for u in range(U):
                                st.inc(dve.scalar_tensor_tensor(out=x3[:, u, :], in0=y[:, (u * 4 + e) * D:(u * 4 + e + 1) * D], scalar=prob[:, u, e:e + 1],
                                                                in1=x3[:, u, :], op0=ALU.mult, op1=ALU.add))
                            st.wait(dve)
                        dve.sem_inc(summed, 1)
                    else:
                        dve.wait_ge(x_in_s, i * 16 + 16)
                    for u in range(U):
                        st.inc(dve.bn_stats(stats[:, u * 6:(u + 1) * 6], x3[:, u, :]))
                    st.wait(dve)
                    dve.sem_inc(dve_passed, 1)
                    for u in range(U):
                        st.inc(dve.bn_aggr(mv[:, u * 2:(u + 1) * 2], stats[:, u * 6:(u + 1) * 6]))
                    st.wait(dve)
                    dve.sem_inc(var_done, 1)
                    dve.wait_ge(std_done, i + 1)
                    st.link(dve, dve.reciprocal(rstd[:, :], rstd[:, :]))
                    dve.wait_ge(turned, i)
                    if last:
                        dve.wait_ge(o_stored, i * 16)
                    for u in range(U):
                        st.inc(dve.tensor_scalar(xn3[:, u, :], x3[:, u, :], mv[:, u * 2:u * 2 + 1], rstd[:, u:u + 1], ALU.subtract, ALU.mult))
                    st.wait(dve)
                    dve.sem_inc(normed, 1)
                    dve.sem_inc(x_read, 1)
                    if last:
                        dve.wait_ge(rows_made, i * 2 + 2)
                        st.link(dve, dve.tensor_copy(score[:, :, :], rows3))
                        choose(dve, st, score[:, :, :], E, tri[:, :, :], (gt[:, :, :, :], eq[:, :, :, :], rank[:, :, :], keep[:, :, :], mx[:, :], z[:, :]), None, prob[:, :, :], 0.0)
                        dve.sem_inc(sc_ready, 1)
                        dve.wait_ge(sc_exp, i + 1)
                        st.link(dve, dve.tensor_reduce(z[:, :], prob[:, :, :], AX.X, ALU.add))
                        st.link(dve, dve.reciprocal(z[:, :], z[:, :]))
                        st.link(dve, dve.tensor_tensor(prob[:, :, :], prob[:, :, :], z[:, :].unsqueeze(2).to_broadcast([P, U, E]), ALU.mult))
                        st.link(dve, dve.tensor_tensor(prob[:, :, :], prob[:, :, :], keep[:, :, :], ALU.mult))
                        st.link(dve, dve.tensor_reduce(z[:, :], prob[:, :, :], AX.X, ALU.add))
                        st.link(dve, dve.tensor_scalar(z[:, :], z[:, :], 1e-9, None, ALU.add))
                        st.link(dve, dve.reciprocal(z[:, :], z[:, :]))
                        st.link(dve, dve.tensor_tensor(extra["gate"][:, ds(i * U, U), :], prob[:, :, :], z[:, :].unsqueeze(2).to_broadcast([P, U, E]), ALU.mult))
                        st.link(dve, dve.tensor_copy(extra["rank"][:, ds(i * U, U), :], rank[:, :, :]))

                STEPS = {0: 16, 1: 17, 2: 61, 3: 18 + 1 + 8 + 9}[k]
                with dve.Fori(0, ROUNDS) as i:
                    st = Count(step, i * STEPS)
                    body(i, st)
                    assert st.n == STEPS, (k, st.n, STEPS)

            @block.scalar
            def _(act):
                act.wait_ge(w_ready, 2 if k == 0 else 1)
                with act.Fori(0, ROUNDS) as i:
                    if k == 2:
                        act.wait_ge(sc_sq, i + 1)
                        act.activation(sc_std[:, :], ssum[:, :], ACT.Sqrt).then_inc(sc_rt, 1)
                        act.wait_ge(sc_ready, i + 1)
                        act.activation(prob[:, :, :], prob[:, :, :], ACT.Exp).then_inc(sc_exp, 1)
                    act.wait_ge(var_done, i + 1)
                    act.activation(rstd[:, :], mv3[:, :, 1], ACT.Sqrt, bias=eps[:, :]).then_inc(std_done, 1)
                    act.wait_ge(turned, i + 1)
                    act.wait_ge(product, i)
                    if k == 1:
                        act.wait_ge(o_stored, i * 16)
                    act.activation(xt[:, :], tp[:, 0:U * D], ACT.Copy).then_inc(xt_made, 1)
                    act.wait_ge(product, i + 1)
                    if last:
                        act.activation(rows3, mp3[:, :, 0:8], ACT.Copy).then_inc(rows_made, 2)
                        act.wait_ge(sc_ready, i + 1)
                        act.activation(prob[:, :, :], prob[:, :, :], ACT.Exp).then_inc(sc_exp, 1)
                    else:
                        act.wait_ge(t_stored, i * 16)
                        act.wait_ge(t_scattered, i * (16 * U))
                        for u in range(U):
                            ins = act.activation(rows3[:, u, 0:CW].rearrange("p (h c) -> p h c", h=H)[:, :, 0:C],
                                                 mp3[:, u, 0:H * C].rearrange("p (h c) -> p h c", h=H), ACT.Copy)
                        ins.then_inc(rows_made, 1)
                        act.activation(rows3[:, :, CW:RW], mp3[:, :, H * C:W], ACT.Copy).then_inc(rows_made, 1)

            @block.tensor
            def _(pe):
                if k == 0:
                    pe.wait_ge(w_in, nw * 16)
                    for kc in range(2):
                        for a in range(2):
                            mm = pe.transpose(tp[:, kc * D + a * P:kc * D + (a + 1) * P], w_nat[:, a * D + kc * P:a * D + (kc + 1) * P], S["ident"][:, :])
                    mm.then_inc(w_ready, 1)
                pe.wait_ge(w_ready, 2 if k == 0 else 1)
                with pe.Fori(0, ROUNDS) as i:
                    pe.wait_ge(normed, i + 1)
                    pe.wait_ge(xt_made, i)
                    for u in range(U):
                        for kc in range(2):
                            c = (u * 2 + kc) * P
                            mm = pe.transpose(tp[:, c:c + P], xn[:, c:c + P], S["ident"][:, :])
                    mm.then_inc(turned, 1)
                    pe.wait_ge(xt_made, i + 1)
                    pe.wait_ge(rows_made, i * 2)
                    for u in range(U):
                        for kc in range(2):
                            c = (u * 2 + kc) * P
                            mm = pe.matmul(mp3[:, u, 0:W], xt[:, c:c + P], wc3[:, kc, :], start=(kc == 0), stop=(kc == 1))
                    mm.then_inc(product, 1)


def prepare(nc, x, x0, tables, zeroed, S):
    with Scope(nc, "prep") as s:
        z = s.sb("z", [P, 2048])
        xl = s.sb("xl", [P, D])
        empty = [s.sb(f"empty{i}", [1, t.shape[1]]) for i, (t, H) in enumerate(tables)]
        cleared, filled, stored, step = s.sem("cleared"), s.sem("filled"), s.sem("stored"), s.sem("step")
        rest = N - (NT - 1) * P
        n = 0
        with nc.Block() as block:
            @block.vector
            def _(dve):
                dve.memset(z[:, :], 0.0).then_inc(cleared, 1)
                st = Count(step)
                for e, (t, H) in zip(empty, tables):
                    RW = t.shape[1]
                    st.link(dve, dve.memset(e[:, :], 0.0))
                    st.link(dve, dve.memset(e[:, RW - 2 * H:RW - H], NEG))
                dve.sem_inc(filled, 1)

            @block.sync
            def _(sp):
                st = Count(stored)
                st.inc(sp.dma_start(x0[0:(NT - 1) * P, :].rearrange("(a b) d -> a (b d)", a=P), x[0:(NT - 1) * P, :].rearrange("(a b) d -> a (b d)", a=P)), 16)
                st.inc(sp.dma_start(x0[(NT - 1) * P:N, :], x[(NT - 1) * P:N, :]), 16)
                sp.wait_ge(cleared, 1)
                st.inc(sp.dma_start(x0[N:N + 75, :], z[0:75, 0:D]), 16)
                st.inc(sp.dma_start(x0[N + 75:NP, :], z[0:75, 0:D]), 16)
                for t in zeroed:
                    rows_, width = t.shape
                    for r in range(0, rows_, P):
                        m = min(P, rows_ - r)
                        st.inc(sp.dma_start(t[r:r + m, :], z[0:m, 0:width]), 16)
                sp.wait_ge(filled, 1)
                for e, (t, H) in zip(empty, tables):
                    st.inc(sp.dma_start(t[DUMMY:DUMMY + 1, :], e[:, :]), 16)
                st.wait(sp)


EX = 8
HID = 682
HJ = 6
HR = HID - 5 * P
MT = (2 * N + EX * (P - 1)) // P
SPARE = MT * P
SLOT_ROWS = SPARE + 4 * P


def turn_weights(nc, w1, w2, w3, w13t, w2t, S):
    with Scope(nc, "turnw", S["keep"]) as s:
        n1, n3, n2 = s.sb("n1", [P, HJ * D]), s.sb("n3", [P, HJ * D]), s.sb("n2", [P, 2 * HID])
        t13, t2 = s.sb("t13", [P, 2 * 2 * HID]), s.sb("t2", [P, HJ * D])
        pa, pb = s.ps("pa", [P, 2048]), s.ps("pb", [P, 2048])
        loaded, turned1, turned3, turned2, kept1, kept3, kept2, stored, sp_passed = [s.sem(n) for n in
            ("loaded", "turned1", "turned3", "turned2", "kept1", "kept3", "kept2", "stored", "sp_passed")]
        t13v = t13[:, :].rearrange("p (k n) -> p k n", k=2)
        pav, pbv = [t[:, :].rearrange("p (k n) -> p k n", k=2) for t in (pa, pb)]
        piece = [P] * (HJ - 1) + [HR]
        with nc.Block() as block:
            @block.sync
            def _(sp):
                with sp.Fori(0, EX) as e:
                    sp.wait_ge(turned2, e)
                    sp.sem_inc(sp_passed, 1)
                    for w, n in ((w1, n1), (w3, n3)):
                        sp.dma_start(n[:, 0:5 * D].rearrange("p (j d) -> p j d", j=5),
                                     w[ds(e, 1), 0:5 * P, :].rearrange("a (j p) d -> p (a j) d", p=P)).then_inc(loaded, 16)
                        sp.dma_start(n[0:HR, 5 * D:6 * D], w[ds(e, 1), 5 * P:HID, :].rearrange("a p d -> (a p) d")).then_inc(loaded, 16)
                    sp.dma_start(n2[:, :].rearrange("p (c h) -> p c h", c=2), w2[ds(e, 1), :, :].rearrange("a (c p) h -> p (a c) h", p=P)).then_inc(loaded, 16)
                    sp.wait_ge(kept1, e + 1)
                    sp.sem_inc(sp_passed, 1)
                    sp.wait_ge(kept3, e + 1)
                    sp.sem_inc(sp_passed, 1)
                    sp.dma_start(w13t[ds(e, 1), :, :].rearrange("a p n -> (a p) n"), t13[:, :]).then_inc(stored, 16)
                    sp.wait_ge(kept2, e * 2 + 2)
                    sp.sem_inc(sp_passed, 1)
                    sp.dma_start(w2t[ds(e, 1), :, 0:5 * D].rearrange("a p n -> (a p) n"), t2[:, 0:5 * D]).then_inc(stored, 16)
                    sp.dma_start(w2t[ds(e, 1), 0:HR, 5 * D:6 * D].rearrange("a p n -> (a p) n"), t2[0:HR, 5 * D:6 * D]).then_inc(stored, 16)
                sp.wait_ge(stored, EX * 48)

            @block.tensor
            def _(pe):
                with pe.Fori(0, EX) as e:
                    pe.wait_ge(loaded, e * 80 + 80)
                    pe.wait_ge(kept2, e * 2)
                    for n, pv, done in ((n1, pav, turned1), (n3, pbv, turned3)):
                        if pv is pbv:
                            pe.wait_ge(kept3, e)
                        for kc in range(2):
                            for j, m in enumerate(piece):
                                mm = pe.transpose(pv[:, kc, j * P:j * P + m], n[0:m, j * D + kc * P:j * D + (kc + 1) * P], S["ident"][0:m, 0:m])
                        mm.then_inc(done, 1)
                    pe.wait_ge(kept1, e + 1)
                    for j, m in enumerate(piece):
                        for c in range(2):
                            mm = pe.transpose(pa[0:m, j * D + c * P:j * D + (c + 1) * P], n2[:, c * HID + j * P:c * HID + j * P + m], S["ident"][:, :])
                    mm.then_inc(turned2, 1)

            @block.scalar
            def _(act):
                with act.Fori(0, EX) as e:
                    act.wait_ge(turned1, e + 1)
                    act.wait_ge(stored, e * 48)
                    act.activation(t13v[:, :, 0:HID], pav[:, :, 0:HID], ACT.Copy).then_inc(kept1, 1)
                    act.wait_ge(turned2, e + 1)
                    act.activation(t2[:, 0:5 * D], pa[:, 0:5 * D], ACT.Copy).then_inc(kept2, 1)
                    act.activation(t2[0:HR, 5 * D:6 * D], pa[0:HR, 5 * D:6 * D], ACT.Copy).then_inc(kept2, 1)

            @block.vector
            def _(dve):
                with dve.Fori(0, EX) as e:
                    dve.wait_ge(turned3, e + 1)
                    dve.wait_ge(stored, e * 48)
                    dve.tensor_copy(t13v[:, :, HID:2 * HID], pbv[:, :, 0:HID]).then_inc(kept3, 1)


def clear_slots(nc, xe, ye, S):
    with Scope(nc, "clear", S["keep"]) as s:
        z = s.sb("z", [P, 7 * D])
        cleared, stored, sp_passed = s.sem("cleared"), s.sem("stored"), s.sem("sp_passed")
        with nc.Block() as block:
            @block.vector
            def _(dve):
                dve.memset(z[:, :], 0.0).then_inc(cleared, 1)

            @block.sync
            def _(sp):
                sp.wait_ge(cleared, 1)
                with sp.Fori(0, MT // 7) as i:
                    sp.dma_start(xe[ds(i * (7 * P), 7 * P), :].rearrange("(p a) d -> p (a d)", p=P), z[:, :]).then_inc(stored, 16)
                sp.dma_start(xe[SPARE:SLOT_ROWS, :].rearrange("(p a) d -> p (a d)", p=P), z[:, 0:4 * D]).then_inc(stored, 16)
                sp.dma_start(ye[SPARE:SLOT_ROWS, :].rearrange("(p a) d -> p (a d)", p=P), z[:, 0:4 * D]).then_inc(stored, 16)
                sp.wait_ge(stored, (MT // 7 + 2) * 16)


def dispatch(nc, xn3, xe, R, S):
    with Scope(nc, "dispatch", S["keep"]) as s:
        node, spare, tau_i = s.sb("node", [P, NTP], I32), s.sb("spare", [P, 2, NTP], I32), s.sb("tau_i", [1, MT + 1], I32)
        pq = s.sb("pq", [P, P], I32)
        real, fake, below, ones = s.sb("real", [P, NTP]), s.sb("fake", [P, NTP]), s.sb("below", [P, P]), s.sb("ones", [P, P])
        sel, run, per = s.sb("sel", [P, EX, NTP]), s.sb("run", [P, EX, NTP]), s.sb("per", [P, EX])
        sums = s.ps("sums", [P, 2 * EX])
        tiles_i, tiles, ends, base = s.sb("tiles_i", [P, EX], I32), s.sb("tiles", [P, EX]), s.sb("ends", [P, EX]), s.sb("base", [P, EX])
        one8 = s.sb("one8", [P, EX])
        is_k, prod, posf = s.sb("is_k", [P, NTP, EX]), s.sb("prod", [P, NTP, EX]), s.sb("posf", [P, NTP])
        cmp, tef, tau = s.sb("cmp", [1, MT + 1, EX]), s.sb("tef", [1, MT + 1]), s.sb("tau", [1, MT + 1])
        pos5 = s.sb("pos5", [P, 2, U], I32)
        rows = s.sb("rows", [P, 2 * U * D])
        made, step, counted, summed, ready, loaded, used, sp_passed, pool_passed, set5 = [s.sem(n) for n in
            ("made", "step", "counted", "summed", "ready", "loaded", "used", "sp_passed", "pool_passed", "set5")]
        scattered = s.pool_sem("scattered")
        with nc.Block() as block:
            @block.gpsimd
            def _(pool):
                pool.iota(node[:, :], [[P, NTP]], base=0, channel_multiplier=1).then_inc(made, 1)
                for c in range(2):
                    pool.iota(spare[:, c, :], [[2 * P, NTP]], base=SPARE - 2 * P * (NT - 1) + c * P, channel_multiplier=1).then_inc(made, 1)
                pool.iota(tau_i[:, :], [[1, MT + 1]], base=0, channel_multiplier=0).then_inc(made, 1)
                pool.iota(pq[:, :], [[1, P]], base=0, channel_multiplier=-1).then_inc(made, 1)
                with pool.Fori(0, ROUNDS) as i:
                    pool.wait_ge(set5, i * 2 + 2)
                    pool.wait_ge(loaded, i * 16 + 16)
                    pool.sem_inc(pool_passed, 1)
                    for u in range(U):
                        for c in range(2):
                            pool.indirect_dma_start(out=xe, in_=rows[:, u * D:(u + 1) * D], in_offset=None,
                                                    out_offset=bass.IndirectOffsetOnAxis(ap=pos5[:, c, u:u + 1], axis=0)).then_inc(scattered, 16)
                pool.wait_ge(scattered, ROUNDS * 2 * U * 16)

            @block.sync
            def _(sp):
                with sp.Fori(0, ROUNDS) as i:
                    sp.wait_ge(scattered, i * (2 * U * 16))
                    sp.sem_inc(sp_passed, 1)
                    sp.dma_start(rows[:, 0:U * D].rearrange("p (u d) -> p u d", u=U), xn3[ds(i * (U * P), U * P), :].rearrange("(u p) d -> p u d", p=P)).then_inc(loaded, 16)
                sp.wait_ge(loaded, ROUNDS * 16)

            @block.tensor
            def _(pe):
                pe.wait_ge(counted, 1)
                pe.matmul(sums[:, 0:EX], below[:, :], per[:, :], start=True, stop=True)
                pe.matmul(sums[:, EX:2 * EX], ones[:, :], per[:, :], start=True, stop=True).then_inc(summed, 1)

            @block.vector
            def _(dve):
                st = Count(step)
                dve.wait_ge(made, 5)
                rk = R["rank"]
                st.inc(dve.memset(ones[:, :], 1.0))
                st.inc(dve.memset(one8[:, :], 1.0))
                st.inc(dve.tensor_scalar(below[:, :], pq[:, :], 0.5, None, ALU.is_gt))
                st.inc(dve.tensor_scalar(real[:, :], node[:, :], float(N), None, ALU.is_lt))
                st.inc(dve.tensor_scalar(fake[:, :], node[:, :], float(N), None, ALU.is_ge))
                st.inc(dve.tensor_copy(tau[:, :], tau_i[:, :]))
                st.link(dve, dve.tensor_scalar(prod[:, :, :], rk[:, :, :], 1.5, None, ALU.is_lt))
                st.link(dve, dve.tensor_tensor(sel[:, :, :].rearrange("p e t -> p t e"), prod[:, :, :], real[:, :].unsqueeze(2).to_broadcast([P, NTP, EX]), ALU.mult))
                for e in range(EX):
                    st.inc(dve.tensor_tensor_scan(run[:, e, :], ones[:, 0:NTP], sel[:, e, :], 0.0, ALU.mult, ALU.add))
                st.wait(dve)
                st.link(dve, dve.tensor_copy(per[:, :], run[:, :, NTP - 1]))
                dve.sem_inc(counted, 1)
                dve.wait_ge(summed, 1)
                st.link(dve, dve.tensor_scalar(tiles_i[:, :], sums[:, EX:2 * EX], float(P - 1), None, ALU.add))
                st.link(dve, dve.tensor_scalar(tiles_i[:, :], tiles_i[:, :], 7, None, ALU.logical_shift_right))
                st.link(dve, dve.tensor_copy(tiles[:, :], tiles_i[:, :]))
                st.link(dve, dve.tensor_tensor_scan(ends[:, :], one8[:, :], tiles[:, :], 0.0, ALU.mult, ALU.add))
                st.link(dve, dve.tensor_tensor(base[:, :], ends[:, :], tiles[:, :], ALU.subtract))
                st.link(dve, dve.tensor_scalar(base[:, :], base[:, :], float(P), -1.0, ALU.mult, ALU.add))
                st.link(dve, dve.tensor_tensor(base[:, :], base[:, :], sums[:, 0:EX], ALU.add))
                st.link(dve, dve.tensor_tensor(run[:, :, :], run[:, :, :], base[:, :].unsqueeze(2).to_broadcast([P, EX, NTP]), ALU.add))
                for c in range(2):
                    st.link(dve, dve.tensor_scalar(is_k[:, :, :], rk[:, :, :], float(c), None, ALU.is_equal))
                    st.link(dve, dve.tensor_tensor(prod[:, :, :], run[:, :, :].rearrange("p e t -> p t e"), is_k[:, :, :], ALU.mult))
                    st.link(dve, dve.tensor_reduce(posf[:, :], prod[:, :, :], AX.X, ALU.add))
                    st.link(dve, dve.tensor_tensor(posf[:, :], posf[:, :], real[:, :], ALU.mult))
                    st.link(dve, dve.tensor_tensor(prod[:, :, 0], spare[:, c, :], fake[:, :], ALU.mult))
                    st.link(dve, dve.tensor_tensor(R["pos"][:, c, :], posf[:, :], prod[:, :, 0], ALU.add))
                    st.link(dve, dve.tensor_tensor(prod[:, :, :], R["gate"][:, :, :], is_k[:, :, :], ALU.mult))
                    st.link(dve, dve.tensor_reduce(R["g"][:, c, :], prod[:, :, :], AX.X, ALU.add))
                st.link(dve, dve.tensor_tensor(cmp[:, :, :], tau[:, :].unsqueeze(2).to_broadcast([1, MT + 1, EX]),
                                               ends[0:1, :].unsqueeze(1).to_broadcast([1, MT + 1, EX]), ALU.is_ge))
                st.link(dve, dve.tensor_reduce(tef[:, :], cmp[:, :, :], AX.X, ALU.add))
                st.link(dve, dve.tensor_scalar(R["expert"][:, :], tef[:, :], float(EX - 1), None, ALU.min))
                with dve.Fori(0, ROUNDS) as i:
                    dve.wait_ge(scattered, i * (2 * U * 16))
                    dve.tensor_copy(pos5[:, 0, :], R["pos"][:, 0, ds(i * U, U)]).then_inc(set5, 1)
                    dve.tensor_copy(pos5[:, 1, :], R["pos"][:, 1, ds(i * U, U)]).then_inc(set5, 1)


def experts(nc, xe, ye, w13t, w2t, R, S):
    W13, W2 = 2 * 2 * HID, HJ * D
    HC = HID // 2
    with Scope(nc, "experts", S["keep"]) as s:
        w13, w2 = s.sb("w13", [P, EX * W13]), s.sb("w2", [P, EX * W2])
        x, xt = s.sb("x", [P, D]), s.sb("xt", [P, D])
        sg, h, ht, ysb = s.sb("sg", [P, HID]), s.sb("h", [P, HID]), s.sb("ht", [P, HJ * P]), s.sb("ysb", [P, D])
        xp, hp, htp, yp = s.ps("xp", [P, 512]), s.ps("hp", [P, 4 * 512]), s.ps("htp", [P, 2 * 512]), s.ps("yp", [P, 512])
        w_in, x_in, x_turned, xt_made, hidden, silu, h_made, h_turned, ht_made, y_made, y_copied, stored, sp_passed = [s.sem(n) for n in
            ("w_in", "x_in", "x_turned", "xt_made", "hidden", "silu", "h_made", "h_turned", "ht_made", "y_made", "y_copied", "stored", "sp_passed")]
        hp3 = hp[:, :].rearrange("p (c n) -> p c n", c=4)
        piece = [P] * (HJ - 1) + [HR]
        with nc.Block() as block:
            @block.sync
            def _(sp):
                sp.dma_start(x[:, :], xe[0:P, :]).then_inc(x_in, 16)
                for e in range(EX):
                    sp.dma_start(w13[:, e * W13:(e + 1) * W13], w13t[e, :, :]).then_inc(w_in, 16)
                    sp.dma_start(w2[:, e * W2:e * W2 + 5 * D], w2t[e, :, 0:5 * D]).then_inc(w_in, 16)
                    sp.dma_start(w2[0:HR, e * W2 + 5 * D:(e + 1) * W2], w2t[e, 0:HR, 5 * D:6 * D]).then_inc(w_in, 16)
                with sp.Fori(0, MT) as t:
                    sp.wait_ge(x_turned, t + 1)
                    sp.sem_inc(sp_passed, 1)
                    sp.dma_start(x[:, :], xe[ds((t + 1) * P, P), :]).then_inc(x_in, 16)
                    sp.wait_ge(y_copied, t + 1)
                    sp.sem_inc(sp_passed, 1)
                    sp.dma_start(ye[ds(t * P, P), :], ysb[:, :]).then_inc(stored, 16)
                sp.wait_ge(stored, MT * 16)
                sp.wait_ge(x_in, (MT + 1) * 16)

            @block.tensor
            def _(pe):
                def turn_x(t):
                    pe.wait_ge(x_in, t * 16 + 16)
                    pe.wait_ge(xt_made, t)
                    for kc in range(2):
                        mm = pe.transpose(xp[:, kc * P:(kc + 1) * P], x[:, kc * P:(kc + 1) * P], S["ident"][:, :])
                    mm.then_inc(x_turned, 1)

                def up(t, at):
                    pe.wait_ge(xt_made, t + 1)
                    for kc in range(2):
                        for c in range(4):
                            rhs = w13[:, ds(at * W13 + (kc * 2 * HID + c * HC), HC)]
                            mm = pe.matmul(hp3[:, c, 0:HC], xt[:, kc * P:(kc + 1) * P], rhs, start=(kc == 0), stop=(kc == 1))
                    mm.then_inc(hidden, 1)

                pe.wait_ge(w_in, EX * 48)
                turn_x(0)
                first = pe.value_load(R["expert"][0:1, 0:1], min_val=0, max_val=EX - 1)
                up(0, first)
                with pe.Fori(0, MT) as t:
                    e = pe.value_load(R["expert"][0:1, ds(t, 1)], min_val=0, max_val=EX - 1)
                    nxt = pe.value_load(R["expert"][0:1, ds(t + 1, 1)], min_val=0, max_val=EX - 1)
                    turn_x(t + 1)
                    pe.wait_ge(h_made, t + 1)
                    pe.wait_ge(ht_made, t * 2)
                    for j, m in enumerate(piece):
                        mm = pe.transpose(htp[0:m, j * P:(j + 1) * P], h[:, j * P:j * P + m], S["ident"][:, :])
                    mm.then_inc(h_turned, 1)
                    up(t + 1, nxt)
                    pe.wait_ge(ht_made, t * 2 + 2)
                    pe.wait_ge(y_copied, t)
                    for j, m in enumerate(piece):
                        mm = pe.matmul(yp[:, 0:D], ht[0:m, j * P:(j + 1) * P], w2[0:m, ds(e * W2 + j * D, D)], start=(j == 0), stop=(j == HJ - 1))
                    mm.then_inc(y_made, 1)

            @block.scalar
            def _(act):
                def copy_x(t):
                    act.wait_ge(x_turned, t + 1)
                    act.wait_ge(hidden, t)
                    act.activation(xt[:, :], xp[:, 0:D], ACT.Copy).then_inc(xt_made, 1)

                copy_x(0)
                with act.Fori(0, MT) as t:
                    act.wait_ge(hidden, t + 1)
                    act.activation(sg[:, :].rearrange("p (c n) -> p c n", c=2), hp3[:, 0:2, 0:HC], ACT.Silu).then_inc(silu, 1)
                    copy_x(t + 1)
                    act.wait_ge(y_made, t)
                    act.wait_ge(h_turned, t + 1)
                    act.activation(ht[:, 0:5 * P], htp[:, 0:5 * P], ACT.Copy).then_inc(ht_made, 1)
                    act.activation(ht[0:HR, 5 * P:], htp[0:HR, 5 * P:6 * P], ACT.Copy).then_inc(ht_made, 1)

            @block.vector
            def _(dve):
                with dve.Fori(0, MT) as t:
                    dve.wait_ge(silu, t + 1)
                    dve.wait_ge(h_turned, t)
                    dve.tensor_tensor(h[:, :].rearrange("p (c n) -> p c n", c=2), sg[:, :].rearrange("p (c n) -> p c n", c=2),
                                      hp3[:, 2:4, 0:HC], ALU.mult).then_inc(h_made, 1)
                    dve.wait_ge(y_made, t + 1)
                    dve.wait_ge(stored, t * 16)
                    dve.tensor_copy(ysb[:, :], yp[:, 0:D]).then_inc(y_copied, 1)


def combine(nc, x3, ye, out, R, S):
    with Scope(nc, "combine", S["keep"]) as s:
        pos5 = s.sb("pos5", [P, 2, U], I32)
        x, y = s.sb("x", [P, U * D]), s.sb("y", [P, 2 * U * D])
        set5, x_in, step, done, stored, sp_passed, pool_passed = [s.sem(n) for n in ("set5", "x_in", "step", "done", "stored", "sp_passed", "pool_passed")]
        got = s.pool_sem("got")
        x3v = x[:, :].rearrange("p (u d) -> p u d", u=U)
        whole = ROUNDS - 1
        with nc.Block() as block:
            @block.sync
            def _(sp):
                with sp.Fori(0, whole) as i:
                    sp.wait_ge(stored, i * 16)
                    sp.sem_inc(sp_passed, 1)
                    sp.dma_start(x3v, x3[ds(i * (U * P), U * P), :].rearrange("(u p) d -> p u d", p=P)).then_inc(x_in, 16)
                    sp.wait_ge(done, i + 1)
                    sp.sem_inc(sp_passed, 1)
                    sp.dma_start(out[ds(i * (U * P), U * P), :].rearrange("(u p) d -> p u d", p=P), x3v).then_inc(stored, 16)
                sp.wait_ge(stored, whole * 16)
                sp.dma_start(x3v, x3[whole * U * P:NP, :].rearrange("(u p) d -> p u d", p=P)).then_inc(x_in, 16)
                sp.wait_ge(done, ROUNDS)
                full = NT - 1 - whole * U
                r0 = whole * U * P
                sp.dma_start(out[r0:r0 + full * P, :].rearrange("(u p) d -> p u d", p=P), x3v[:, 0:full, :]).then_inc(stored, 16)
                sp.dma_start(out[(NT - 1) * P:N, :], x[0:N - (NT - 1) * P, full * D:(full + 1) * D]).then_inc(stored, 16)
                sp.wait_ge(stored, (whole + 2) * 16)

            @block.gpsimd
            def _(pool):
                with pool.Fori(0, ROUNDS) as i:
                    pool.wait_ge(set5, i * 2 + 2)
                    pool.sem_inc(pool_passed, 1)
                    for c in range(2):
                        for u in range(U):
                            at = (c * U + u) * D
                            pool.indirect_dma_start(out=y[:, at:at + D], out_offset=None, in_=ye,
                                                    in_offset=bass.IndirectOffsetOnAxis(ap=pos5[:, c, u:u + 1], axis=0)).then_inc(got, 16)

            @block.vector
            def _(dve):
                with dve.Fori(0, ROUNDS) as i:
                    dve.wait_ge(step, i * (2 * U))
                    dve.tensor_copy(pos5[:, 0, :], R["pos"][:, 0, ds(i * U, U)]).then_inc(set5, 1)
                    dve.tensor_copy(pos5[:, 1, :], R["pos"][:, 1, ds(i * U, U)]).then_inc(set5, 1)
                    dve.wait_ge(x_in, i * 16 + 16)
                    dve.wait_ge(got, i * (2 * U * 16) + 2 * U * 16)
                    for c in range(2):
                        for u in range(U):
                            at = (c * U + u) * D
                            dve.scalar_tensor_tensor(out=x3v[:, u, :], in0=y[:, at:at + D], scalar=R["g"][:, c, ds(i * U + u, 1)], in1=x3v[:, u, :],
                                                     op0=ALU.mult, op1=ALU.add).then_inc(step, 1)
                        dve.wait_ge(step, i * (2 * U) + (c + 1) * U)
                    dve.sem_inc(done, 1)


def dram(nc, name, shape, dt=F32):
    return nc.dram_tensor(name, shape, dt, kind="Internal").ap()


def build(nc, a, out, stop=99, probe=None):
    lists = [
        (Cfg("0", 206250, 2048), a["dst"], a["src"], None, 8, 32),
        (Cfg("1", 131072, 1024), a["L0_ffn_edge_index"][1], a["L0_ffn_edge_index"][0], N - 1, 4, 4),
        (Cfg("2", 206250, 2048), a["src"], a["dst"], None, 4, 64),
    ]
    x0, x1, x2, x3 = [dram(nc, f"x{i}", (NP, D)) for i in range(4)]
    xt1 = dram(nc, "xt1", (NTP, P, 2 * P))
    y1 = dram(nc, "y1", (NP, 4 * D))
    tabs, owns, outs, invs, infos, ells, starts = [], [], [], [], [], [], []
    for i, (cfg, key, payload, clamp, H, C) in enumerate(lists):
        RW = H * (C + 1) + 2 * H
        tabs.append(dram(nc, f"table{i}", (NP + 1, RW)))
        owns.append(dram(nc, f"own{i}", (NP, RW)))
        outs.append(dram(nc, f"agg{i}", (NP, H * C)))
        invs.append(dram(nc, f"inv{i}", (NP,), I32))
        infos.append(dram(nc, f"info{i}", (1, INFO), I32))
        ells.append(dram(nc, f"ell{i}", (cfg.max_blocks, P, SLOTS), I32))
        starts.append(dram(nc, f"starts{i}", (NP + 1,)))
    with Scope(nc, "all") as outer:
        S = constants(nc, outer)
        prepare(nc, a["x"], x0, [(tabs[i], lists[i][4]) for i in range(3)], [o[NR:NP, :] for o in outs], S)
        for i, (cfg, key, payload, clamp, H, C) in enumerate(lists):
            if i > stop:
                break
            words, firsts = dram(nc, f"words{i}", (cfg.total,)), dram(nc, f"firsts{i}", (cfg.total // COARSE,))
            copies, maxdeg = dram(nc, f"copies{i}", (WIN, cfg.rows * WIN), I32), dram(nc, f"maxdeg{i}", (NT,))
            preload_lists(nc, cfg, key, payload, clamp, words, firsts, copies, S)
            rank_nodes(nc, cfg, words, firsts, copies, starts[i], invs[i], infos[i], ells[i], maxdeg, S)
        dense(nc, 0, 8, 32, x0, None, tabs[0], owns[0], invs[0],
              {"w": a["L0_gnn_W"], "neigh": a["L0_gnn_a_left"].rearrange("(a h) c -> a (h c)", a=1), "mine": a["L0_gnn_a_right"].rearrange("(a h) c -> a (h c)", a=1)}, S)
        aggregate(nc, lists[0][0], 8, 32, tabs[0], owns[0], infos[0], ells[0], outs[0], True, S)
        if stop == 0:
            return outs[0], invs[0]
        dense(nc, 1, 4, 4, x0, x1, tabs[1], owns[1], invs[1],
              {"w": a["L0_ffn_W_gat"], "neigh": a["L0_ffn_att_src"].rearrange("(a h) c -> a (h c)", a=1), "mine": a["L0_ffn_att_dst"].rearrange("(a h) c -> a (h c)", a=1)}, S,
              agg=outs[0], inv=invs[0], extra={"xt": xt1})
        ffn = SmallExperts(xt1, a["L0_ffn_W1"], a["L0_ffn_b1"], a["L0_ffn_W2"], a["L0_ffn_b2"], y1, S)
        aggregate(nc, lists[1][0], 4, 4, tabs[1], owns[1], infos[1], ells[1], outs[1], True, S, ffn)
        if stop == 1:
            return x1, y1, outs[1], invs[1]
        dense(nc, 2, 4, 64, x1, x2, tabs[2], owns[2], invs[2],
              {"w": a["L1_gnn_weight"], "neigh": a["L1_gnn_att_dst"].rearrange("a h c -> a (h c)"), "mine": a["L1_gnn_att_src"].rearrange("a h c -> a (h c)"),
               "gamma": a["L0_ffn_ln_gamma"], "beta": a["L0_ffn_ln_beta"], "b_gat": a["L0_ffn_b_gat"]}, S,
              agg=outs[1], inv=invs[1], extra={"y": y1})
        aggregate(nc, lists[2][0], 4, 64, tabs[2], owns[2], infos[2], ells[2], outs[2], False, S)
        if stop == 2:
            return x2, outs[2], invs[2]
        w13t, w2t = dram(nc, "w13t", (EX, P, 4 * HID)), dram(nc, "w2t", (EX, P, HJ * D))
        xe, ye, xn3 = dram(nc, "xe", (SLOT_ROWS, D)), dram(nc, "ye", (SLOT_ROWS, D)), dram(nc, "xn3", (NP, D))
        R = {"rank": outer.sb("rank", [P, NTP, EX]), "gate": outer.sb("gate", [P, NTP, EX]), "pos": outer.sb("pos", [P, 2, NTP], I32),
             "g": outer.sb("g", [P, 2, NTP]), "expert": outer.sb("expert", [1, MT + 1], I32)}
        turn_weights(nc, a["L1_ffn_w1"], a["L1_ffn_w2"], a["L1_ffn_w3"], w13t, w2t, S)
        clear_slots(nc, xe, ye, S)
        dense(nc, 3, 0, 0, x2, x3, None, None, None, {"w": a["L1_ffn_router_w"], "bias": a["L1_gnn_bias"]}, S,
              agg=outs[2], inv=invs[2], extra={"xn": xn3, "rank": R["rank"], "gate": R["gate"]})
        dispatch(nc, xn3, xe, R, S)
        experts(nc, xe, ye, w13t, w2t, R, S)
        combine(nc, x3, ye, out, R, S)


_ORDER = ["x", "src", "dst", "L0_gnn_W", "L0_gnn_a_left", "L0_gnn_a_right", "L0_ffn_W_gat", "L0_ffn_att_src", "L0_ffn_att_dst",
          "L0_ffn_b_gat", "L0_ffn_ln_gamma", "L0_ffn_ln_beta", "L0_ffn_W1", "L0_ffn_b1", "L0_ffn_W2", "L0_ffn_b2", "L0_ffn_edge_index",
          "L1_gnn_weight", "L1_gnn_att_src", "L1_gnn_att_dst", "L1_gnn_bias", "L1_ffn_router_w", "L1_ffn_w1", "L1_ffn_w2", "L1_ffn_w3"]


def kernel(**inputs):
    import numpy as np
    import concourse.bacc as bacc
    from concourse import mybir as mb
    from concourse.bass_utils import run_bass_kernel_spmd

    nc = bacc.Bacc("TRN2", target_bir_lowering=False, num_devices=1)
    arrays, aps = {}, {}
    for name in _ORDER:
        arr = np.ascontiguousarray(inputs[name])
        arrays[f"in_{name}"] = arr
        aps[name] = nc.dram_tensor(f"in_{name}", arr.shape, mb.dt.from_np(arr.dtype), kind="ExternalInput").ap()
    out = nc.dram_tensor("out", (N, D), mb.dt.float32, kind="ExternalOutput").ap()
    build(nc, aps, out)
    r = run_bass_kernel_spmd(nc, [arrays], core_ids=[0])
    return r.results[0]["out"]
```

```python
from contextlib import ExitStack

import concourse.bass as bass
from concourse import mybir

ALU = mybir.AluOpType
ACT = mybir.ActivationFunctionType
AX = mybir.AxisListType
F32 = mybir.dt.float32
I32 = mybir.dt.int32
ds = bass.ds

P = 128
N = 6250
D = 256
NT = 49
NR = NT * P
NTP = 50
NP = NTP * P
DUMMY = NP
LOG_RANKS = 13
PAD_RANKS = 2 ** LOG_RANKS - NR
ID_BITS = 13
ID_MASK = 2 ** ID_BITS - 1
KEY_BASE = 0x20000000
DEG_BASE = 1024
SLOTS = 8
WIN = 32
RING = 4
NEG = -1e30
COARSE = 512


class Cfg:

    def __init__(self, name, E, F):
        self.name, self.E, self.F = name, E, F
        self.total = P * F
        self.rows = self.total // WIN + 2
        self.max_blocks = (E + E // P) // SLOTS + 2 * NT + 4 * RING


class Scope:

    def __init__(self, nc, tag, keep=None):
        self.nc, self.tag, self.st, self.sems = nc, tag, ExitStack(), []
        self.keep = keep or self.st

    def __enter__(self):
        return self

    def __exit__(self, *a):
        if self.sems and a[0] is None:
            for x in self.sems:
                self.nc.gpsimd.sem_clear(x)
            self.nc.all_engine_barrier()
        return self.st.__exit__(*a)

    def sb(self, name, shape, dt=F32):
        return self.st.enter_context(self.nc.sbuf_tensor(f"{self.tag}_{name}", shape, dt))

    def ps(self, name, shape, dt=F32):
        return self.st.enter_context(self.nc.psum_tensor(f"{self.tag}_{name}", shape, dt))

    def sem(self, name):
        self.sems.append(self.st.enter_context(self.nc.semaphore(f"{self.tag}_{name}")))
        return self.sems[-1]

    def pool_sem(self, name):
        return self.keep.enter_context(self.nc.semaphore(f"{self.tag}_{name}"))


class Count:

    def __init__(self, sem, base=0):
        self.sem, self.base, self.n = sem, base, 0

    def inc(self, ins, by=1):
        ins.then_inc(self.sem, by)
        self.n += by
        return ins

    def wait(self, eng):
        eng.wait_ge(self.sem, self.base + self.n)

    def link(self, eng, ins):
        self.inc(ins)
        self.wait(eng)


def sort_steps(log_part, log_free):
    steps = []
    for k in range(1, log_part + log_free + 1):
        if k >= log_free:
            steps.append(("sign", k - log_free))
        if k > log_free:
            steps.append(("turn",))
            steps += [("cross", j - log_free) for j in range(k - 1, log_free - 1, -1)]
            steps.append(("back",))
        for j in range(min(k, log_free) - 1, -1, -1):
            steps.append(("free", k, j))
    return steps


class Sorter:

    def __init__(self, log_part, log_free, bufs, turned, sign, ident, cmp_done, turned_in_psum, copied):
        self.lp, self.lf = log_part, log_free
        self.PB, self.F = 2 ** log_part, 2 ** log_free
        self.nb = max(1, self.F // P)
        self.steps = sort_steps(log_part, log_free)
        self.bufs, self.turned, self.sign, self.ident = bufs, turned, sign, ident
        self.cmp_done, self.in_psum, self.copied = cmp_done, turned_in_psum, copied
        self.at = []
        n, cur = 0, 0
        for s in self.steps:
            self.at.append((n, cur))
            if s[0] in ("cross", "sign"):
                n += 2 if s[0] == "cross" else 1
            elif s[0] == "free":
                n += 4 if s[1] < self.lf else 2
            cur ^= 1
        self.result = cur
        self.total = n

    def groups(self):
        return [(g, min(g + 512, self.F)) for g in range(0, self.F, 512)]

    def part(self, lo, hi):
        turns = 0
        for i, (s, (n, cur)) in enumerate(zip(self.steps, self.at)):
            if lo <= i < hi:
                yield s, n, cur, turns
            turns += s[0] in ("turn", "back")

    def vector(self, dve, lo=0, hi=1 << 30):
        for s, n, cur, nturn in self.part(lo, hi):
            src, dst = self.bufs[cur][0:self.PB, 0:self.F], self.bufs[cur ^ 1][0:self.PB, 0:self.F]
            if s[0] in ("turn", "back"):
                continue
            if nturn:
                dve.wait_ge(self.copied, nturn * self.ngroups)
            if n:
                dve.wait_ge(self.cmp_done, n)
            if s[0] == "sign":
                dve.tensor_scalar(dst, src, self.sign[0:self.PB, s[1]:s[1] + 1], None, ALU.mult).then_inc(self.cmp_done, 1)
            elif s[0] == "cross":
                a, b = self.bufs[cur][:, 0:self.nb * self.PB], self.bufs[cur ^ 1][:, 0:self.nb * self.PB]
                y = 2 ** s[1]
                a = a.rearrange("q (x two y) -> q x two y", two=2, y=y)
                b = b.rearrange("q (x two y) -> q x two y", two=2, y=y)
                for half, op in ((0, ALU.min), (1, ALU.max)):
                    dve.tensor_tensor(b[:, :, half, :], a[:, :, 0, :], a[:, :, 1, :], op).then_inc(self.cmp_done, 1)
            elif s[1] >= self.lf:
                y = 2 ** s[2]
                a = src.rearrange("q (x two y) -> q x two y", two=2, y=y)
                b = dst.rearrange("q (x two y) -> q x two y", two=2, y=y)
                for half, op in ((0, ALU.min), (1, ALU.max)):
                    dve.tensor_tensor(b[:, :, half, :], a[:, :, 0, :], a[:, :, 1, :], op).then_inc(self.cmp_done, 1)
            else:
                y, m = 2 ** s[2], 2 ** (s[1] - 1 - s[2])
                a = src.rearrange("q (x dir m two y) -> q x dir m two y", dir=2, m=m, two=2, y=y)
                b = dst.rearrange("q (x dir m two y) -> q x dir m two y", dir=2, m=m, two=2, y=y)
                for d in (0, 1):
                    for half, op in ((d, ALU.min), (1 - d, ALU.max)):
                        dve.tensor_tensor(b[:, :, d, :, half, :], a[:, :, d, :, 0, :], a[:, :, d, :, 1, :], op).then_inc(self.cmp_done, 1)

    @property
    def ngroups(self):
        return len(self.groups())

    def tensor(self, pe, lo=0, hi=1 << 30):
        for s, n, cur, nturn in self.part(lo, hi):
            if s[0] not in ("turn", "back"):
                continue
            pe.wait_ge(self.cmp_done, n)
            if nturn:
                pe.wait_ge(self.copied, nturn * self.ngroups)
            src = self.bufs[cur]
            for first, end in self.groups():
                if s[0] == "turn":
                    for b in range(first // P, end // P):
                        mm = pe.transpose(self.turned[:, b * self.PB:(b + 1) * self.PB], src[0:self.PB, b * P:(b + 1) * P],
                                          self.ident[0:self.PB, 0:self.PB])
                else:
                    for b in range(first // P, end // P):
                        mm = pe.transpose(self.turned[0:self.PB, b * P:(b + 1) * P], src[:, b * self.PB:(b + 1) * self.PB],
                                          self.ident[:, :])
                mm.then_inc(self.in_psum, 1)

    def scalar(self, act, lo=0, hi=1 << 30):
        for s, n, cur, nturn in self.part(lo, hi):
            if s[0] not in ("turn", "back"):
                continue
            dst = self.bufs[cur ^ 1]
            for i, (first, end) in enumerate(self.groups()):
                act.wait_ge(self.in_psum, nturn * self.ngroups + i + 1)
                if s[0] == "turn":
                    a, b = first // P * self.PB, end // P * self.PB
                    act.activation(dst[:, a:b], self.turned[:, a:b], ACT.Copy).then_inc(self.copied, 1)
                else:
                    act.activation(dst[0:self.PB, first:end], self.turned[0:self.PB, first:end], ACT.Copy).then_inc(self.copied, 1)


class ListSort:

    def __init__(self, cfg, key, payload, clamp, words, firsts, copies):
        self.cfg, self.key, self.payload, self.clamp = cfg, key, payload, clamp
        self.words, self.firsts, self.copies = words, firsts, copies

    def allocate(self, s, S):
        F = self.cfg.F
        self.bufs = [s.sb("words0", [P, F]), s.sb("words1", [P, F])]
        self.zeros = s.sb("zeros", [WIN, 2 * WIN], I32)
        turned = s.ps("words_turned", [P, 2048])
        self.cleared, self.in_place, self.word_packed = s.sem("cleared"), s.sem("in_place"), s.sem("word_packed")
        self.cmp_done, in_psum, copied = s.sem("words_compared"), s.sem("words_in_psum"), s.sem("words_copied")
        self.ids_ready, self.stored = s.sem("ids_ready"), s.sem("stored")
        self.so = Sorter(7, F.bit_length() - 1, self.bufs, turned, S["sign"], S["ident"], self.cmp_done, in_psum, copied)
        self.ki, self.vi = self.bufs[0][:, :].bitcast(I32), self.bufs[1][:, :].bitcast(I32)
        self.result, self.ids = self.bufs[self.so.result], self.bufs[self.so.result ^ 1][:, :].bitcast(I32)

    def load(self, eng):
        F, E = self.cfg.F, self.cfg.E
        full, rest = E // F, E % F
        eng.wait_ge(self.cleared, 3)
        for t, src in ((self.ki, self.key), (self.vi, self.payload)):
            eng.dma_start(t[0:full, :], src[0:full * F].rearrange("(p f) -> p f", f=F)).then_inc(self.in_place, 16)
            if rest:
                eng.dma_start(t[full:full + 1, 0:rest], src[full * F:E].rearrange("(p f) -> p f", p=1)).then_inc(self.in_place, 16)
        eng.dma_start(self.copies[:, self.cfg.total:self.cfg.rows * WIN], self.zeros[:, :]).then_inc(self.stored, 16)

    def store(self, nc, eng):
        F = self.cfg.F
        eng.wait_ge(self.stored, 16)
        eng.wait_ge(self.cmp_done, self.so.total)
        eng.dma_start(self.words.rearrange("(p f) -> p f", f=F), self.result[:, :]).then_inc(self.stored, 16)
        with nc.allow_non_contiguous_dma(reason="one word in 512"):
            eng.dma_start(self.firsts.rearrange("(p f) -> p f", p=P),
                          self.result[:, :].rearrange("p (f c) -> p f c", c=COARSE)[:, :, 0]).then_inc(self.stored, 16)
        eng.wait_ge(self.ids_ready, 1)
        for c in range(WIN):
            eng.dma_start(self.copies[c, WIN - c:WIN - c + self.cfg.total].rearrange("(p f) -> p f", f=F), self.ids).then_inc(self.stored, 16)
        eng.wait_ge(self.stored, 16 * (3 + WIN))

    def clear(self, dve):
        dve.memset(self.ki, ID_MASK).then_inc(self.cleared, 1)
        dve.memset(self.vi, 0).then_inc(self.cleared, 1)
        dve.memset(self.zeros[:, :], 0).then_inc(self.cleared, 1)

    def pack(self, dve):
        dve.wait_ge(self.in_place, 64 if self.cfg.E % self.cfg.F else 32)
        pk = Count(self.word_packed)
        if self.clamp is not None:
            pk.link(dve, dve.tensor_scalar(self.vi, self.vi, self.clamp, None, ALU.min))
        pk.link(dve, dve.tensor_scalar(self.ki, self.ki, ID_BITS, KEY_BASE, ALU.logical_shift_left, ALU.bitwise_or))
        pk.link(dve, dve.tensor_tensor(self.ki, self.ki, self.vi, ALU.bitwise_or))

    def separate(self, dve):
        dve.wait_ge(self.cmp_done, self.so.total)
        dve.tensor_scalar(self.ids, self.result[:, :].bitcast(I32), ID_MASK, None, ALU.bitwise_and).then_inc(self.ids_ready, 1)


def sort_first(nc, ls, S):
    with Scope(nc, f"sort{ls.cfg.name}", S["keep"]) as s:
        ls.allocate(s, S)
        with nc.Block() as block:
            @block.sync
            def _(sp):
                ls.load(sp)
                ls.store(nc, sp)

            @block.vector
            def _(dve):
                ls.clear(dve)
                ls.pack(dve)
                ls.so.vector(dve)
                ls.separate(dve)

            @block.tensor
            def _(pe):
                ls.so.tensor(pe)

            @block.scalar
            def _(act):
                ls.so.scalar(act)


INFO = 256
I_NB, I_NW, I_CB, I_CW, I_RINGS, I_T0, I_LEFT = 0, 50, 100, 150, 200, 201, 202
INFO_STEPS = 20


def rank_nodes(nc, cfg, words, firsts, copies, starts, inv, info, ell, maxdeg, S, after=None, setup=None):
    NF = cfg.total // COARSE
    R0 = PAD_RANKS // P
    U = 7
    HALF = 5
    NSEARCH = NTP // (2 * HALF)
    with Scope(nc, f"rank{cfg.name}", S["keep"]) as s:
        thr = s.sb("thresholds", [P, NTP])
        thr_i = thr[:, :].bitcast(I32)
        firsts_b, junk = s.sb("firsts", [P, NF]), s.sb("junk", [P, COARSE])
        cnt1, cnt2, q, qi = s.sb("cnt1", [P, NTP]), s.sb("cnt2", [P, NTP]), s.sb("q", [P, NTP]), s.sb("qi", [P, NTP], I32)
        q_now = [s.sb(f"q_now{i}", [P, HALF], I32) for i in range(2)]
        row = [s.sb(f"row{i}", [P, HALF * COARSE]) for i in range(2)]
        start = s.sb("start", [P, NTP])
        zero1 = s.sb("zero1", [1, 1])
        lo, hi = s.sb("lo", [NTP, P]), s.sb("hi", [NTP, P])
        vrow = s.sb("vrow", [64, P])
        vrow_i = s.sb("vrow_i", [64, P], I32)
        real, deg, tmp, tmp_i = s.sb("real", [64, P]), s.sb("deg", [64, P]), s.sb("tmp", [64, P]), s.sb("tmp_i", [64, P], I32)
        bufs = [s.sb("dwords0", [P, P]), s.sb("dwords1", [P, P])]
        turned = s.ps("turned", [P, 512])
        idf, degf = s.sb("idf", [64, P]), s.sb("degf", [64, P])
        tr = s.ps("tr", [P, 2, 64])
        node_i, degt = s.sb("node_i", [P, 64], I32), s.sb("degt", [P, 64])
        rank_i = s.sb("rank_i", [P, NTP], I32)
        node7, rank7, start7 = s.sb("node7", [P, U], I32), s.sb("rank7", [P, U], I32), s.sb("start7", [P, U])
        start_r, si = s.sb("start_r", [P, NT]), s.sb("si", [P, NT], I32)
        qr, cr = s.sb("qr", [P, NT]), s.sb("cr", [P, NT])
        row_i = s.sb("row_i", [P, 2 * NT], I32)
        md, mdi, mdw = s.sb("md", [1, NTP]), s.sb("mdi", [1, NTP], I32), s.sb("mdw", [1, NTP], I32)
        cums, one = s.sb("cums", [1, 2 * NTP]), s.sb("one", [1, NTP])
        inf = s.sb("info", [1, INFO], I32)
        iota_w = s.sb("iota_w", [P, WIN])
        cur, rem, mask = s.sb("cur", [P, 1]), s.sb("rem", [P, 1]), s.sb("mask", [P, WIN])
        iota_2w, wide_tiles = s.sb("iota_2w", [P, 2 * WIN]), s.sb("wide_tiles", [1, 1])
        curs, ridx_all, ridx7 = s.sb("curs", [P, NT]), s.sb("ridx_all", [P, 2, NT], I32), s.sb("ridx7", [P, 2, U], I32)
        wide, wmask, slots7 = s.sb("wide", [P, U * 2 * WIN], I32), s.sb("wmask", [P, U, 2 * WIN]), s.sb("slots7", [P, U * 2 * WIN], I32)
        group_ready, group_full, group_stored = s.sem("group_ready"), s.sem("group_full"), s.sem("group_stored")
        wide_got, inv_set = s.pool_sem("wide_got"), s.pool_sem("inv_set")
        ridx, win, picked, slots = s.sb("ridx", [P, 1], I32), s.sb("win", [P, WIN], I32), s.sb("picked", [P, WIN]), s.sb("slots", [P, WIN], I32)
        empty = s.sb("empty", [P, 2 * RING * SLOTS], I32)
        made, loaded, searched, qready = s.sem("made"), s.sem("loaded"), s.sem("searched"), s.sem("qready")
        got_row = [s.pool_sem(f"got_row{i}") for i in range(2)]
        counted, startd, st_stored = s.sem("counted"), s.sem("startd"), s.sem("st_stored")
        neigh, packed, cmp_done, in_psum, copied = s.sem("neigh"), s.sem("packed"), s.sem("cmp_done"), s.sem("in_psum"), s.sem("copied")
        decoded, turned_ids, node_done, seven, seven_got = s.sem("decoded"), s.sem("turned_ids"), s.sem("node_done"), s.sem("seven"), s.pool_sem("seven_got")
        taken7, md_done, md_back, tables, passed = s.sem("taken7"), s.sem("md_done"), s.sem("md_back"), s.sem("tables"), s.sem("passed")
        info_done, info_stored, sp_passed = s.sem("info_done"), s.sem("info_stored"), s.sem("sp_passed")
        win_step, win_ready, win_got, win_full, win_stored, passed2, empty_done = [s.pool_sem(n) if n == "win_got" else s.sem(n) for n in
            ("win_step", "win_ready", "win_got", "win_full", "win_stored", "passed2", "empty_done")]
        so = Sorter(6, 7, bufs, turned, S["sign"], S["ident"], cmp_done, in_psum, copied)
        key_i = bufs[0][0:64, :].bitcast(I32)
        res = bufs[so.result][0:64, 0:P]
        shares = [5] * (2 * NSEARCH) + [9] * (NT // U) + [22] * (NT // U)
        cuts = [0] * (len(shares) + 1)
        if after:
            after.allocate(s, S)
            cuts = [len(after.so.steps) * sum(shares[:i]) // sum(shares) for i in range(len(shares) + 1)]
        if setup:
            setup.allocate(s, S)
        before_rank = cuts[2 * NSEARCH]
        res_i = res.bitcast(I32)
        with nc.Block() as block:
            @block.sync
            def _(sp):
                sp.dma_start(firsts_b[:, :], firsts.rearrange("(a f) -> a f", a=1).to_broadcast([P, NF])).then_inc(loaded, 16)
                sp.wait_ge(startd, 4)
                with nc.allow_non_contiguous_dma(reason="node order"):
                    sp.dma_start(starts[0:NP].rearrange("(t p) -> p t", p=P), start[:, :]).then_inc(st_stored, 16)
                sp.dma_start(starts[NP:NP + 1].rearrange("(a b) -> a b", a=1), zero1[:, :]).then_inc(st_stored, 16)
                sp.wait_ge(made, 3)
                with nc.allow_non_contiguous_dma(reason="node order"):
                    sp.dma_start(inv[NR:NP].rearrange("(t p) -> p t", p=P), rank_i[:, NT:NTP]).then_inc(st_stored, 16)
                sp.wait_ge(st_stored, 48)
                sp.dma_start(lo[:, :], starts[0:NP].rearrange("(t p) -> t p", p=P)).then_inc(neigh, 16)
                sp.dma_start(hi[:, :], starts[1:NP + 1].rearrange("(t p) -> t p", p=P)).then_inc(neigh, 16)
                sp.wait_ge(decoded, 5)
                with nc.allow_non_contiguous_dma(reason="one per tile"):
                    sp.dma_start(maxdeg.rearrange("(t a) -> t a", a=1), degf[R0:64, P - 1:P]).then_inc(md_back, 16)
                sp.wait_ge(md_back, 16)
                sp.dma_start(md[:, 0:NT], maxdeg.rearrange("(a t) -> a t", a=1)).then_inc(md_back, 16)
                sp.wait_ge(info_done, INFO_STEPS)
                sp.dma_start(info, inf[:, :]).then_inc(info_stored, 16)
                sp.wait_ge(info_stored, 16)
                with sp.Fori(0, NT // U) as i:
                    sp.wait_ge(group_full, i + 1)
                    sp.sem_inc(sp_passed, 1)
                    for u in range(U):
                        c0 = sp.value_load(inf[0:1, ds(i * U + (u + I_CB), 1)], min_val=0, max_val=cfg.max_blocks - 2 * WIN // SLOTS)
                        sp.dma_start(ell[ds(c0, 2 * WIN // SLOTS), :, :].rearrange("b p j -> p b j"),
                                     slots7[:, u * 2 * WIN:(u + 1) * 2 * WIN].rearrange("p (b j) -> p b j", j=SLOTS)).then_inc(group_stored, 16)
                        sp.wait_ge(group_stored, i * (16 * U) + (u + 1) * 16)
                        sp.sem_inc(sp_passed, 1)
                t0 = sp.value_load(inf[0:1, I_T0:I_T0 + 1], min_val=0, max_val=NT - 1)
                left = sp.value_load(inf[0:1, I_LEFT:I_LEFT + 1], min_val=1, max_val=NT)
                with sp.Fori(0, left) as i:
                    t = nc.s_assert_within(t0 + i, 0, NT - 1, skip_runtime_bounds_check_because="the tiles from t0 on")
                    n = sp.value_load(inf[0:1, ds(t + I_NW, 1)], min_val=1, max_val=cfg.max_blocks)
                    c0 = sp.value_load(inf[0:1, ds(t + I_CB, 1)], min_val=0, max_val=cfg.max_blocks)
                    w0 = sp.value_load(inf[0:1, ds(t + I_CW, 1)], min_val=0, max_val=cfg.max_blocks)
                    with sp.Fori(0, n) as w:
                        sp.wait_ge(win_full, w0 + w + 1)
                        sp.sem_inc(sp_passed, 1)
                        sp.dma_start(ell[ds(nc.s_assert_within(c0 + w * 4, 0, cfg.max_blocks - 4, skip_runtime_bounds_check_because="a window's blocks lie within the list's"), 4), :, :].rearrange("b p j -> p b j"),
                                     slots[:, :].rearrange("p (b j) -> p b j", j=SLOTS)).then_inc(win_stored, 16)
                        sp.wait_ge(win_stored, (w0 + w + 1) * 16)
                        sp.sem_inc(sp_passed, 1)
                last = sp.value_load(inf[0:1, I_CB + NT:I_CB + NT + 1], min_val=1, max_val=cfg.max_blocks - 2 * RING)
                sp.wait_ge(made, 5)
                sp.dma_start(ell[ds(last, 2 * RING), :, :].rearrange("b p j -> p b j"),
                             empty[:, :].rearrange("p (b j) -> p b j", j=SLOTS)).then_inc(empty_done, 16)
                sp.wait_ge(empty_done, 16)

            @block.gpsimd
            def _(pool):
                pool.iota(thr_i, [[P, NTP]], base=0, channel_multiplier=1).then_inc(made, 1)
                pool.iota(vrow_i[:, :], [[1, P]], base=0, channel_multiplier=P).then_inc(made, 1)
                pool.iota(rank_i[:, :], [[P, NTP]], base=0, channel_multiplier=1).then_inc(made, 1)
                pool.iota(iota_w[:, :], [[1, WIN]], base=0, channel_multiplier=0,
                          allow_small_or_imprecise_dtypes=True).then_inc(made, 1)
                pool.memset(empty[:, :], DUMMY).then_inc(made, 1)
                pool.iota(iota_2w[:, :], [[1, 2 * WIN]], base=0, channel_multiplier=0,
                          allow_small_or_imprecise_dtypes=True).then_inc(made, 1)
                rows = words.rearrange("(r c) -> r c", c=COARSE)
                with pool.Fori(0, NSEARCH) as i:
                    for u in range(2):
                        pool.wait_ge(qready, i * 2 + u + 1)
                        pool.sem_inc(passed, 1)
                        for v in range(HALF):
                            pool.indirect_dma_start(out=row[u][:, v * COARSE:(v + 1) * COARSE], out_offset=None, in_=rows,
                                                    in_offset=bass.IndirectOffsetOnAxis(ap=q_now[u][:, v:v + 1], axis=0)).then_inc(got_row[u], 16)
                pool.wait_ge(st_stored, 48)
                with pool.Fori(0, NT // U) as i:
                    pool.wait_ge(seven, i + 1)
                    pool.sem_inc(passed, 1)
                    for u in range(U):
                        pool.indirect_dma_start(out=start7[:, u:u + 1], out_offset=None, in_=starts.rearrange("(n a) -> n a", a=1),
                                                in_offset=bass.IndirectOffsetOnAxis(ap=node7[:, u:u + 1], axis=0)).then_inc(seven_got, 16)
                with pool.Fori(0, NT // U) as i:
                    pool.wait_ge(group_ready, i + 1)
                    pool.sem_inc(passed, 1)
                    for u in range(U):
                        for w in range(2):
                            at = (u * 2 + w) * WIN
                            pool.indirect_dma_start(out=wide[:, at:at + WIN], out_offset=None, in_=copies.rearrange("c (r w) -> (c r) w", w=WIN),
                                                    in_offset=bass.IndirectOffsetOnAxis(ap=ridx7[:, w, u:u + 1], axis=0)).then_inc(wide_got, 16)
                    for u in range(U):
                        pool.indirect_dma_start(out=inv.rearrange("(n a) -> n a", a=1), in_=rank7[:, u:u + 1], in_offset=None,
                                                out_offset=bass.IndirectOffsetOnAxis(ap=node7[:, u:u + 1], axis=0)).then_inc(inv_set, 16)
                pool.wait_ge(inv_set, NT * 16)
                pool.wait_ge(info_done, INFO_STEPS)
                t0 = pool.value_load(inf[0:1, I_T0:I_T0 + 1], min_val=0, max_val=NT - 1)
                left = pool.value_load(inf[0:1, I_LEFT:I_LEFT + 1], min_val=1, max_val=NT)
                with pool.Fori(0, left) as i:
                    t = nc.s_assert_within(t0 + i, 0, NT - 1, skip_runtime_bounds_check_because="the tiles from t0 on")
                    n = pool.value_load(inf[0:1, ds(t + I_NW, 1)], min_val=1, max_val=cfg.max_blocks)
                    w0 = pool.value_load(inf[0:1, ds(t + I_CW, 1)], min_val=0, max_val=cfg.max_blocks)
                    with pool.Fori(0, n) as w:
                        pool.wait_ge(win_ready, w0 + w + 1)
                        pool.sem_inc(passed2, 1)
                        pool.indirect_dma_start(out=win[:, :], out_offset=None, in_=copies.rearrange("c (r w) -> (c r) w", w=WIN),
                                                in_offset=bass.IndirectOffsetOnAxis(ap=ridx[:, :], axis=0)).then_inc(win_got, 16)

            @block.vector
            def _(dve):
                if setup:
                    setup.vector(dve)
                if after:
                    after.clear(dve)

                def beside(i):
                    if after:
                        after.so.vector(dve, cuts[i], cuts[i + 1])

                dve.wait_ge(made, 6)
                sc = Count(searched)
                dve.memset(zero1[:, :], 0.0)
                dve.memset(one[:, :], 1.0)
                sc.link(dve, dve.tensor_scalar(thr_i, thr_i, ID_BITS, KEY_BASE, ALU.logical_shift_left, ALU.bitwise_or))
                dve.wait_ge(loaded, 16)
                with dve.Fori(0, NTP) as t:
                    dve.wait_ge(searched, t + 1)
                    dve.tensor_scalar(junk[:, 0:NF], firsts_b[:, :], thr[:, ds(t, 1)], 0.0, ALU.is_lt, ALU.add,
                                      accum_out=cnt1[:, ds(t, 1)]).then_inc(searched, 1)
                sc.n += NTP
                sc.wait(dve)
                sc.link(dve, dve.tensor_scalar(q[:, :], cnt1[:, :], -1.0, 0.0, ALU.add, ALU.max))
                sc.link(dve, dve.tensor_copy(qi[:, :], q[:, :]))
                for u in range(2):
                    dve.tensor_copy(q_now[u][:, :], qi[:, u * HALF:(u + 1) * HALF]).then_inc(qready, 1)

                def count_rows(i, u):
                    dve.wait_ge(got_row[u], i * (16 * HALF) + 16 * HALF)
                    for v in range(HALF):
                        t = i * (2 * HALF) + (u * HALF + v)
                        if t:
                            dve.wait_ge(counted, t)
                        dve.tensor_scalar(junk[:, :], row[u][:, v * COARSE:(v + 1) * COARSE], thr[:, t:t + 1], 0.0, ALU.is_lt, ALU.add,
                                          accum_out=cnt2[:, t:t + 1]).then_inc(counted, 1)

                if after:
                    after.pack(dve)
                for i in range(NSEARCH):
                    for u in range(2):
                        beside(i * 2 + u)
                        count_rows(i, u)
                        if i < NSEARCH - 1:
                            at = (i + 1) * (2 * HALF) + u * HALF
                            dve.wait_ge(counted, i * (2 * HALF) + (u + 1) * HALF)
                            dve.tensor_copy(q_now[u][:, :], qi[:, at:at + HALF]).then_inc(qready, 1)
                dve.wait_ge(counted, NTP)
                sd = Count(startd)
                sd.link(dve, dve.scalar_tensor_tensor(out=start[:, :], in0=q[:, :], scalar=float(COARSE), in1=cnt2[:, :],
                                                      op0=ALU.mult, op1=ALU.add))
                sd.link(dve, dve.tensor_copy(vrow[:, :], vrow_i[:, :]))
                sd.link(dve, dve.tensor_scalar(real[:, :], vrow[:, :], float(N), None, ALU.is_lt))
                sd.link(dve, dve.memset(deg[:, :], 0.0))
                pk = Count(packed)
                pk.link(dve, dve.tensor_scalar(tmp[:, :], real[:, :], float(PAD_RANKS), float(-PAD_RANKS), ALU.mult, ALU.add))
                pk.link(dve, dve.tensor_tensor(tmp_i[:, :], tmp[:, :], vrow[:, :], ALU.add))
                dve.wait_ge(neigh, 32)
                pk.link(dve, dve.tensor_tensor(deg[0:NTP, :], hi[:, :], lo[:, :], ALU.subtract))
                pk.link(dve, dve.scalar_tensor_tensor(out=deg[:, :], in0=deg[:, :], scalar=1.0, in1=real[:, :], op0=ALU.add, op1=ALU.mult))
                pk.link(dve, dve.tensor_scalar(key_i, deg[:, :], float(DEG_BASE), None, ALU.add))
                pk.link(dve, dve.tensor_scalar(key_i, key_i, ID_BITS, None, ALU.logical_shift_left))
                pk.link(dve, dve.tensor_tensor(key_i, key_i, tmp_i[:, :], ALU.bitwise_or))
                so.vector(dve)
                dve.wait_ge(cmp_done, so.total)
                dc = Count(decoded)
                dc.link(dve, dve.tensor_scalar(vrow_i[:, :], res_i, ID_MASK, None, ALU.bitwise_and))
                dc.link(dve, dve.tensor_copy(idf[:, :], vrow_i[:, :]))
                dc.link(dve, dve.tensor_scalar(tmp_i[:, :], res_i, ID_BITS, None, ALU.logical_shift_right))
                dc.link(dve, dve.tensor_scalar(degf[:, :], tmp_i[:, :], -float(DEG_BASE + 1), 0.0, ALU.add, ALU.max))
                dc.link(dve, dve.tensor_copy(tmp[:, :], degf[:, :]))
                dve.wait_ge(turned_ids, 2)
                nd = Count(node_done)
                nd.link(dve, dve.tensor_copy(node_i[:, :], tr[:, 0, :]))
                nd.link(dve, dve.tensor_copy(degt[:, :], tr[:, 1, :]))
                ic = Count(info_done)
                ic.link(dve, dve.memset(inf[:, :], 0))
                dve.wait_ge(md_back, 32)
                ic.link(dve, dve.memset(mdw[:, :], 0))
                ic.link(dve, dve.tensor_scalar(mdi[:, 0:NT], md[:, 0:NT], float(SLOTS - 1), None, ALU.add))
                ic.link(dve, dve.tensor_scalar(mdi[:, 0:NT], mdi[:, 0:NT], 3, None, ALU.logical_shift_right))
                ic.link(dve, dve.tensor_scalar(inf[:, I_NB:I_NB + NT], mdi[:, 0:NT], 1, None, ALU.max))
                ic.link(dve, dve.tensor_scalar(mdw[:, 0:NT], inf[:, I_NB:I_NB + NT], 3, None, ALU.add))
                ic.link(dve, dve.tensor_scalar(inf[:, I_NW:I_NW + NT], mdw[:, 0:NT], 2, None, ALU.logical_shift_right))
                ic.link(dve, dve.memset(cums[:, :], 0.0))
                ic.link(dve, dve.tensor_copy(md[:, 0:NT], inf[:, I_NW:I_NW + NT]))
                ic.link(dve, dve.scalar_tensor_tensor(out=md[:, 0:NT], in0=md[:, 0:NT], scalar=2.0, in1=md[:, 0:NT], op0=ALU.is_gt, op1=ALU.mult))
                for k, sizes in ((0, inf[:, I_NB:I_NB + NT]), (1, md[:, 0:NT])):
                    ic.link(dve, dve.tensor_tensor_scan(cums[:, k * NTP + 1:k * NTP + NTP], one[:, 0:NT], sizes, 0.0,
                                                        ALU.mult, ALU.add))
                ic.link(dve, dve.tensor_copy(inf[:, I_CB:I_CB + 2 * NTP], cums[:, :]))
                ic.link(dve, dve.tensor_scalar(md[:, 0:NT], inf[:, I_NW:I_NW + NT], 2.0, None, ALU.is_le))
                ic.link(dve, dve.tensor_reduce(wide_tiles[:, :], md[:, 0:NT], AX.X, ALU.add))
                ic.link(dve, dve.tensor_scalar(inf[:, I_T0:I_T0 + 1], wide_tiles[:, :], float(NT - 1), None, ALU.min))
                ic.link(dve, dve.tensor_scalar(wide_tiles[:, :], wide_tiles[:, :], -1.0, float(NT), ALU.mult, ALU.add))
                ic.link(dve, dve.tensor_scalar(inf[:, I_LEFT:I_LEFT + 1], wide_tiles[:, :], 1.0, None, ALU.max))
                ic.link(dve, dve.tensor_scalar(mdi[:, 0:1], inf[:, I_CB + NT:I_CB + NT + 1], RING - 1, None, ALU.add))
                ic.link(dve, dve.tensor_scalar(inf[:, I_RINGS:I_RINGS + 1], mdi[:, 0:1], 2, None, ALU.logical_shift_right))
                assert ic.n == INFO_STEPS
                for i in range(NT // U):
                    if i:
                        dve.wait_ge(taken7, i)
                    dve.tensor_copy(node7[:, :], node_i[:, i * U + R0:i * U + R0 + U]).then_inc(seven, 1)
                    beside(2 * NSEARCH + i)
                    dve.wait_ge(seven_got, i * (U * 16) + U * 16)
                    dve.tensor_copy(start_r[:, i * U:(i + 1) * U], start7[:, :]).then_inc(taken7, 1)
                dve.wait_ge(taken7, NT // U)
                tb = Count(tables)
                tb.link(dve, dve.tensor_copy(si[:, :], start_r[:, :]))
                tb.link(dve, dve.tensor_scalar(row_i[:, 0:NT], si[:, :], 5, None, ALU.logical_shift_right))
                tb.link(dve, dve.tensor_scalar(row_i[:, NT:2 * NT], si[:, :], WIN - 1, None, ALU.bitwise_and))
                tb.link(dve, dve.tensor_scalar(qr[:, :], row_i[:, 0:NT], 1.0, None, ALU.add))
                tb.link(dve, dve.tensor_scalar(cr[:, :], row_i[:, NT:2 * NT], float(cfg.rows), None, ALU.mult))
                for w in range(2):
                    tb.link(dve, dve.tensor_scalar(curs[:, :], qr[:, :], float(w), float(cfg.rows - 1), ALU.add, ALU.min))
                    tb.link(dve, dve.tensor_tensor(ridx_all[:, w, :], curs[:, :], cr[:, :], ALU.add))
                for i in range(NT // U):
                    if i:
                        dve.wait_ge(inv_set, i * (U * 16))
                    dve.tensor_copy(rank7[:, :], rank_i[:, i * U:(i + 1) * U]).then_inc(md_done, 1)
                    dve.tensor_copy(node7[:, :], node_i[:, i * U + R0:i * U + R0 + U]).then_inc(md_done, 1)
                    dve.tensor_copy(ridx7[:, :, :], ridx_all[:, :, i * U:(i + 1) * U]).then_inc(md_done, 1)
                    dve.wait_ge(md_done, i * 6 + 3)
                    dve.sem_inc(group_ready, 1)
                    dve.tensor_tensor(wmask[:, :, :], iota_2w[:, :].unsqueeze(1).to_broadcast([P, U, 2 * WIN]),
                                      degt[:, i * U + R0:i * U + R0 + U].unsqueeze(2).to_broadcast([P, U, 2 * WIN]), ALU.is_lt).then_inc(md_done, 1)
                    dve.wait_ge(md_done, i * 6 + 4)
                    beside(2 * NSEARCH + NT // U + i)
                    dve.wait_ge(wide_got, i * (2 * U * 16) + 2 * U * 16)
                    dve.scalar_tensor_tensor(out=wmask[:, :, :], in0=wide[:, :].rearrange("p (u w) -> p u w", u=U), scalar=float(-DUMMY),
                                             in1=wmask[:, :, :], op0=ALU.add, op1=ALU.mult).then_inc(md_done, 1)
                    dve.wait_ge(md_done, i * 6 + 5)
                    if i:
                        dve.wait_ge(group_stored, i * (16 * U))
                    dve.tensor_scalar(slots7[:, :].rearrange("p (u w) -> p u w", u=U), wmask[:, :, :], float(DUMMY), None, ALU.add).then_inc(md_done, 1)
                    dve.wait_ge(md_done, i * 6 + 6)
                    dve.sem_inc(group_full, 1)
                if after:
                    after.separate(dve)
                t0 = dve.value_load(inf[0:1, I_T0:I_T0 + 1], min_val=0, max_val=NT - 1)
                left = dve.value_load(inf[0:1, I_LEFT:I_LEFT + 1], min_val=1, max_val=NT)
                with dve.Fori(0, left) as i:
                    t = nc.s_assert_within(t0 + i, 0, NT - 1, skip_runtime_bounds_check_because="the tiles from t0 on")
                    n = dve.value_load(inf[0:1, ds(t + I_NW, 1)], min_val=1, max_val=cfg.max_blocks)
                    w0 = dve.value_load(inf[0:1, ds(t + I_CW, 1)], min_val=0, max_val=cfg.max_blocks)
                    a = i * 2 + w0 * 6
                    dve.wait_ge(win_step, a)
                    dve.tensor_copy(cur[:, :], qr[:, ds(t, 1)]).then_inc(win_step, 1)
                    dve.tensor_copy(rem[:, :], degt[:, ds(t + R0, 1)]).then_inc(win_step, 1)
                    with dve.Fori(0, n) as w:
                        b = i * 2 + w0 * 6 + w * 6 + 2
                        dve.wait_ge(win_step, b)
                        dve.tensor_scalar(ridx[:, :], cur[:, :], float(cfg.rows - 1), cr[:, ds(t, 1)], ALU.min, ALU.add).then_inc(win_step, 1)
                        dve.wait_ge(win_step, b + 1)
                        dve.sem_inc(win_ready, 1)
                        dve.tensor_scalar(mask[:, :], iota_w[:, :], rem[:, 0:1], None, ALU.is_lt).then_inc(win_step, 1)
                        dve.tensor_scalar(cur[:, :], cur[:, :], 1.0, None, ALU.add).then_inc(win_step, 1)
                        dve.wait_ge(win_step, b + 3)
                        dve.tensor_scalar(rem[:, :], rem[:, :], float(-WIN), None, ALU.add).then_inc(win_step, 1)
                        dve.wait_ge(win_got, (w0 + w + 1) * 16)
                        dve.scalar_tensor_tensor(out=picked[:, :], in0=win[:, :], scalar=float(-DUMMY), in1=mask[:, :],
                                                 op0=ALU.add, op1=ALU.mult).then_inc(win_step, 1)
                        dve.wait_ge(win_step, b + 5)
                        dve.wait_ge(win_stored, (w0 + w) * 16)
                        dve.tensor_scalar(slots[:, :], picked[:, :], float(DUMMY), None, ALU.add).then_inc(win_step, 1)
                        dve.wait_ge(win_step, b + 6)
                        dve.sem_inc(win_full, 1)

            @block.tensor
            def _(pe):
                if after:
                    after.so.tensor(pe, 0, before_rank)
                so.tensor(pe)
                pe.wait_ge(decoded, 5)
                pe.transpose(tr[:, 0, :], idf[:, :], S["ident"][0:64, 0:64]).then_inc(turned_ids, 1)
                pe.transpose(tr[:, 1, :], degf[:, :], S["ident"][0:64, 0:64]).then_inc(turned_ids, 1)
                if after:
                    after.so.tensor(pe, before_rank)
                if setup:
                    setup.tensor(pe)

            @block.scalar
            def _(act):
                if after:
                    after.load(act)
                    after.so.scalar(act, 0, before_rank)
                so.scalar(act)
                if after:
                    after.so.scalar(act, before_rank)
                    after.store(nc, act)
                if setup:
                    setup.scalar(act)


def constants(nc, outer):
    S = {"ident": outer.sb("ident", [P, P]), "sign": outer.sb("sign", [P, 8]), "keep": outer.st}
    with Scope(nc, "const") as s:
        pi, sh, g = s.sb("pi", [P, 1], I32), s.sb("sh", [P, 1], I32), s.sb("g", [P, 8], I32)
        gf = s.sb("gf", [P, 8])
        made, step = s.sem("made"), s.sem("step")
        with nc.Block() as block:
            @block.gpsimd
            def _(pool):
                pool.memset(S["ident"][:, :], 0.0).then_inc(made, 1)
                pool.iota(pi[:, :], [[0, 1]], base=0, channel_multiplier=1).then_inc(made, 1)
                pool.wait_ge(made, 2)
                pool.affine_select(out=S["ident"][:, :], in_=S["ident"][:, :], compare_op=ALU.not_equal, fill=1.0, base=0,
                                   pattern=[[-1, P]], channel_multiplier=1).then_inc(made, 1)

            @block.vector
            def _(dve):
                dve.wait_ge(made, 3)
                st = Count(step)
                st.link(dve, dve.tensor_scalar(sh[:, :], pi[:, :], 1, None, ALU.logical_shift_left))
                st.link(dve, dve.tensor_tensor(sh[:, :], sh[:, :], pi[:, :], ALU.bitwise_xor))
                for r in range(8):
                    st.inc(dve.tensor_scalar(g[:, r:r + 1], sh[:, :], r, 1, ALU.logical_shift_right, ALU.bitwise_and))
                st.wait(dve)
                st.link(dve, dve.tensor_copy(gf[:, :], g[:, :]))
                st.link(dve, dve.tensor_scalar(S["sign"][:, :], gf[:, :], -2.0, 1.0, ALU.mult, ALU.add))
    return S


def aggregate(nc, cfg, H, C, table, own_rows, info, ell, out, self_loop, S, ffn=None):
    CW = H * (C + 1)
    RW = CW + 2 * H
    HB, HT = 9, 4 if self_loop else 3
    TT = HT + 2
    with Scope(nc, f"agg{cfg.name}", S["keep"]) as s:
        inf = s.sb("info", [1, INFO], I32)
        idx = [s.sb(f"idx{i}", [P, SLOTS], I32) for i in range(RING)]
        ring = s.sb("ring", [P, RING * SLOTS * RW])
        own = s.sb("own", [P, 2 * RW])
        er = s.sb("er", [P, H])
        score = s.sb("score", [P, (SLOTS + 1) * H])
        prob = s.sb("prob", [P, (SLOTS + 1) * H])
        m, bm, mn = s.sb("m", [P, H]), s.sb("bm", [P, H]), s.sb("mn", [P, H])
        weighted, summed, acc = s.sb("weighted", [P, SLOTS * CW]), s.sb("summed", [P, CW]), s.sb("acc", [P, CW])
        den, res = s.sb("den", [P, H]), s.sb("res", [P, H * C])
        info_in, start_pool, ready, freed = s.sem("info_in"), s.sem("start_pool"), s.sem("ready"), s.sem("freed")
        idx_in = [s.sem(f"idx_in{i}") for i in range(RING)]
        got = [s.pool_sem(f"got{i}") for i in range(RING)]
        sp_passed, act_passed = s.sem("sp_passed"), s.sem("act_passed")
        own_in, tstep, bstep = s.sem("own_in"), s.sem("tstep"), s.sem("bstep")
        scored, probs, tile_done, out_stored = s.sem("scored"), s.sem("probs"), s.sem("tile_done"), s.sem("out_stored")
        if ffn:
            ffn.allocate(nc, s)
        with nc.Block() as block:
            @block.sync
            def _(sp):
                sp.dma_start(inf[:, :], info).then_inc(info_in, 16)
                sp.wait_ge(info_in, 16)
                rings = sp.value_load(inf[0:1, I_RINGS:I_RINGS + 1], min_val=1, max_val=cfg.max_blocks // RING - 2)
                for i in range(RING):
                    sp.dma_start(idx[i][:, :], ell[i, :, :]).then_inc(idx_in[i], 16)
                with sp.Fori(0, rings) as r:
                    for i in range(RING):
                        sp.wait_ge(got[i], (r + 1) * (16 * SLOTS))
                        sp.sem_inc(ready, 1)
                        nxt = nc.s_assert_within(r * RING + (i + RING), 0, cfg.max_blocks - 1,
                                                 skip_runtime_bounds_check_because="the list ends in two rings of empty blocks")
                        sp.dma_start(idx[i][:, :], ell[ds(nxt, 1), :, :].rearrange("b p j -> (b p) j")).then_inc(idx_in[i], 16)
                for i in range(RING):
                    sp.wait_ge(idx_in[i], (rings + 1) * 16)
                    sp.sem_inc(sp_passed, 1)

            @block.gpsimd
            def _(pool):
                pool.wait_ge(info_in, 16)
                rings = pool.value_load(inf[0:1, I_RINGS:I_RINGS + 1], min_val=1, max_val=cfg.max_blocks // RING - 2)
                with pool.Fori(0, rings) as r:
                    for i in range(RING):
                        pool.wait_ge(freed, r * RING + i + 1)
                        pool.wait_ge(idx_in[i], (r + 1) * 16)
                        pool.sem_inc(start_pool, 1)
                        for j in range(SLOTS):
                            at = (i * SLOTS + j) * RW
                            pool.indirect_dma_start(out=ring[:, at:at + RW], out_offset=None, in_=table,
                                                    in_offset=bass.IndirectOffsetOnAxis(ap=idx[i][:, j:j + 1], axis=0)).then_inc(got[i], 16)

            @block.vector
            def _(dve):
                dve.sem_inc(freed, RING)
                dve.wait_ge(info_in, 16)
                with dve.Fori(0, NT) as t:
                    n = dve.value_load(inf[0:1, ds(t + I_NB, 1)], min_val=1, max_val=cfg.max_blocks)
                    c0 = dve.value_load(inf[0:1, ds(t + I_CB, 1)], min_val=0, max_val=cfg.max_blocks)
                    mine = (t % 2) * RW
                    a = t * TT
                    dve.wait_ge(own_in, t * 16 + 16)
                    dve.wait_ge(tstep, a)
                    dve.tensor_copy(er[:, :], own[:, ds(mine + CW + H, H)]).then_inc(tstep, 1)
                    if self_loop:
                        dve.tensor_tensor(m[:, :], own[:, ds(mine + CW, H)], own[:, ds(mine + CW + H, H)], ALU.add).then_inc(tstep, 1)
                        dve.wait_ge(tstep, a + 2)
                        dve.scalar_tensor_tensor(out=m[:, :], in0=m[:, :], scalar=0.2, in1=m[:, :], op0=ALU.mult, op1=ALU.max).then_inc(tstep, 1)
                        dve.tensor_copy(acc[:, :], own[:, ds(mine, CW)]).then_inc(tstep, 1)
                    else:
                        dve.memset(m[:, :], NEG).then_inc(tstep, 1)
                        dve.memset(acc[:, :], 0.0).then_inc(tstep, 1)
                    with dve.Fori(0, n) as b:
                        g = c0 + b
                        k = g * HB
                        at = (g % RING) * (SLOTS * RW)
                        rows = ring[:, ds(at, SLOTS * RW)].rearrange("p (j w) -> p j w", w=RW)
                        sc3 = score[:, 0:SLOTS * H].rearrange("p (j h) -> p j h", h=H)
                        dve.wait_ge(ready, g + 1)
                        dve.wait_ge(tstep, a + HT)
                        dve.wait_ge(bstep, k)
                        dve.tensor_tensor(sc3, rows[:, :, CW:CW + H], er[:, :].unsqueeze(1).to_broadcast([P, SLOTS, H]), ALU.add).then_inc(bstep, 1)
                        dve.wait_ge(bstep, k + 1)
                        dve.scalar_tensor_tensor(out=sc3, in0=sc3, scalar=0.2, in1=sc3, op0=ALU.mult, op1=ALU.max).then_inc(bstep, 1)
                        dve.wait_ge(bstep, k + 2)
                        dve.tensor_reduce(bm[:, :], sc3.rearrange("p j h -> p h j"), AX.X, ALU.max).then_inc(bstep, 1)
                        dve.wait_ge(bstep, k + 3)
                        dve.tensor_tensor(mn[:, :], m[:, :], bm[:, :], ALU.max).then_inc(bstep, 1)
                        dve.wait_ge(bstep, k + 4)
                        dve.tensor_tensor(score[:, SLOTS * H:], m[:, :], mn[:, :], ALU.subtract)
                        dve.tensor_tensor(sc3, sc3, mn[:, :].unsqueeze(1).to_broadcast([P, SLOTS, H]), ALU.subtract).then_inc(scored, 1)
                        dve.wait_ge(scored, g + 1)
                        dve.tensor_copy(m[:, :], mn[:, :]).then_inc(bstep, 1)
                        dve.wait_ge(probs, g + 1)
                        dve.tensor_tensor(weighted[:, :].rearrange("p (j h c) -> p j h c", j=SLOTS, h=H),
                                          rows[:, :, 0:CW].rearrange("p j (h c) -> p j h c", h=H),
                                          prob[:, 0:SLOTS * H].rearrange("p (j h) -> p j h", h=H).unsqueeze(3).to_broadcast([P, SLOTS, H, C + 1]),
                                          ALU.mult).then_inc(bstep, 1)
                        dve.tensor_tensor(acc[:, :].rearrange("p (h c) -> p h c", h=H), acc[:, :].rearrange("p (h c) -> p h c", h=H),
                                          prob[:, SLOTS * H:].unsqueeze(2).to_broadcast([P, H, C + 1]), ALU.mult).then_inc(bstep, 1)
                        dve.wait_ge(bstep, k + 7)
                        dve.sem_inc(freed, 1)
                        dve.tensor_reduce(summed[:, :], weighted[:, :].rearrange("p (j w) -> p w j", j=SLOTS), AX.X, ALU.add).then_inc(bstep, 1)
                        dve.wait_ge(bstep, k + 8)
                        dve.tensor_tensor(acc[:, :], acc[:, :], summed[:, :], ALU.add).then_inc(bstep, 1)
                    c1 = dve.value_load(inf[0:1, ds(t + (I_CB + 1), 1)], min_val=0, max_val=cfg.max_blocks)
                    dve.wait_ge(bstep, c1 * HB)
                    acc3 = acc[:, :].rearrange("p (h c) -> p h c", h=H)
                    if self_loop:
                        dve.tensor_scalar(den[:, :], acc3[:, :, C], 1e-16, None, ALU.add).then_inc(tstep, 1)
                    else:
                        dve.tensor_scalar(den[:, :], acc3[:, :, C], 1e-16, None, ALU.max).then_inc(tstep, 1)
                    dve.wait_ge(tstep, a + HT + 1)
                    dve.reciprocal(den[:, :], den[:, :]).then_inc(tstep, 1)
                    dve.wait_ge(tstep, a + HT + 2)
                    dve.wait_ge(out_stored, t * 16)
                    dve.tensor_tensor(res[:, :].rearrange("p (h c) -> p h c", h=H), acc3[:, :, 0:C],
                                      den[:, :].unsqueeze(2).to_broadcast([P, H, C]), ALU.mult).then_inc(tile_done, 1)
                    dve.wait_ge(tile_done, t + 1)

            @block.scalar
            def _(act):
                act.wait_ge(info_in, 16)
                act.dma_start(own[:, 0:RW], own_rows[0:P, :]).then_inc(own_in, 16)
                if ffn:
                    ffn.first(act)
                with act.Fori(0, NT) as t:
                    n = act.value_load(inf[0:1, ds(t + I_NB, 1)], min_val=1, max_val=cfg.max_blocks)
                    c0 = act.value_load(inf[0:1, ds(t + I_CB, 1)], min_val=0, max_val=cfg.max_blocks)
                    act.wait_ge(own_in, t * 16 + 16)
                    act.dma_start(own[:, ds(((t + 1) % 2) * RW, RW)], own_rows[ds((t + 1) * P, P), :]).then_inc(own_in, 16)
                    with act.Fori(0, n) as b:
                        act.wait_ge(scored, c0 + b + 1)
                        act.activation(prob[:, :], score[:, :], ACT.Exp).then_inc(probs, 1)
                    if ffn:
                        ffn.scalar(act, t)
                    act.wait_ge(tile_done, t + 1)
                    act.dma_start(out[ds(t * P, P), :], res[:, :]).then_inc(out_stored, 16)
                    act.wait_ge(out_stored, t * 16 + 16)
                act.wait_ge(own_in, (NT + 1) * 16)
                if ffn:
                    ffn.scalar(act, NT)
                    act.wait_ge(ffn.y_stored, NTP * 16)

            if ffn:
                @block.tensor
                def _(pe):
                    pe.wait_ge(ffn.weights_in, ffn.nweights * 16)
                    with pe.Fori(0, NTP) as t:
                        ffn.tensor(pe, t)


class SmallExperts:
    EX, HID = 4, 512

    def __init__(self, xt, w1, b1, w2, b2, y, S):
        self.xt_d, self.w1_d, self.b1_d, self.w2_d, self.b2_d, self.y_d, self.S = xt, w1, b1, w2, b2, y, S

    def allocate(self, nc, s):
        EX, HID = self.EX, self.HID
        self.xt = s.sb("xt", [P, 2 * P])
        self.w1 = s.sb("w1", [P, EX * 2 * HID])
        self.w2 = s.sb("w2", [P, EX * 4 * D])
        self.b1, self.b2, self.ones = s.sb("b1", [1, EX * HID]), s.sb("b2", [1, EX * D]), s.sb("ones", [1, P])
        self.h, self.ht = s.sb("h", [P, 2 * HID]), s.sb("ht", [P, 2 * HID])
        self.ysb = s.sb("ysb", [P, EX * D])
        self.hp, self.tp, self.yp = s.ps("hp", [P, 2 * HID]), s.ps("tp", [P, 2 * HID]), s.ps("yp", [P, EX * D])
        self.weights_in, self.xt_in, self.h_made, self.gelu = s.sem("weights_in"), s.sem("xt_in"), s.sem("h_made"), s.sem("gelu")
        self.turned, self.ht_made, self.y_made, self.y_copied, self.y_stored = [s.sem(n) for n in ("turned", "ht_made", "y_made", "y_copied", "y_stored")]
        self.xt_used, self.ones_made = s.sem("xt_used"), s.sem("ones_made")
        self.nweights = 4

    def first(self, act):
        act.dma_start(self.w1[:, :].rearrange("p (e k n) -> p e k n", e=self.EX, k=2), self.w1_d.rearrange("e (k p) n -> p e k n", p=P)).then_inc(self.weights_in, 16)
        act.dma_start(self.w2[:, :].rearrange("p (e k n) -> p e k n", e=self.EX, k=4), self.w2_d.rearrange("e (k p) n -> p e k n", p=P)).then_inc(self.weights_in, 16)
        act.dma_start(self.b1[:, :], self.b1_d.rearrange("(a e) n -> a (e n)", a=1)).then_inc(self.weights_in, 16)
        act.dma_start(self.b2[:, :], self.b2_d.rearrange("(a e) n -> a (e n)", a=1)).then_inc(self.weights_in, 16)
        act.activation(self.ones[:, :], self.S["ident"][0:1, :], ACT.Copy, scale=0.0, bias=1.0).then_inc(self.ones_made, 1)
        act.dma_start(self.xt[:, :], self.xt_d[0, :, :]).then_inc(self.xt_in, 16)

    def scalar(self, act, t):
        EX, HID = self.EX, self.HID

        def gelu(e):
            act.wait_ge(self.h_made, t * EX + e + 1)
            half = slice((e % 2) * HID, (e % 2 + 1) * HID)
            act.activation(self.h[:, half], self.hp[:, half], ACT.Gelu).then_inc(self.gelu, 1)

        def turn(e):
            act.wait_ge(self.turned, t * EX + e + 1)
            half = slice((e % 2) * HID, (e % 2 + 1) * HID)
            act.activation(self.ht[:, half], self.tp[:, half], ACT.Copy).then_inc(self.ht_made, 1)

        gelu(0)
        for e in range(1, EX):
            gelu(e)
            turn(e - 1)
        turn(EX - 1)
        act.wait_ge(self.xt_used, t + 1)
        act.wait_ge(self.xt_in, t * 16 + 16)
        if not isinstance(t, int):
            act.dma_start(self.xt[:, :], self.xt_d[ds(t + 1, 1), :, :].rearrange("a p n -> (a p) n")).then_inc(self.xt_in, 16)
        act.wait_ge(self.y_made, t * EX + EX)
        act.wait_ge(self.y_stored, t * 16)
        act.activation(self.ysb[:, :], self.yp[:, :], ACT.Copy).then_inc(self.y_copied, 1)
        act.wait_ge(self.y_copied, t + 1)
        dst = self.y_d[t * P:(t + 1) * P, :] if isinstance(t, int) else self.y_d[ds(t * P, P), :]
        act.dma_start(dst, self.ysb[:, :]).then_inc(self.y_stored, 16)

    def tensor(self, pe, t):
        EX, HID = self.EX, self.HID
        pe.wait_ge(self.ones_made, 1)
        pe.wait_ge(self.xt_in, t * 16 + 16)

        def hidden(e):
            half = self.hp[:, (e % 2) * HID:(e % 2 + 1) * HID]
            if e < 2:
                pe.wait_ge(self.gelu, t * EX)
            else:
                pe.wait_ge(self.gelu, t * EX + e - 1)
            for k in range(2):
                pe.matmul(half, self.xt[:, k * P:(k + 1) * P], self.w1[:, (e * 2 + k) * HID:(e * 2 + k + 1) * HID], start=(k == 0), stop=False)
            mm = pe.matmul(half, self.ones[:, :], self.b1[:, e * HID:(e + 1) * HID], start=False, stop=True)
            mm.then_inc(self.h_made, 1)
            if e == EX - 1:
                pe.wait_ge(self.h_made, t * EX + EX)
                pe.sem_inc(self.xt_used, 1)

        def second(e):
            off = (e % 2) * HID
            pe.wait_ge(self.gelu, t * EX + e + 1)
            if e < 2:
                pe.wait_ge(self.ht_made, t * EX)
            else:
                pe.wait_ge(self.ht_made, t * EX + e - 1)
            for c in range(4):
                mm = pe.transpose(self.tp[:, off + c * P:off + (c + 1) * P], self.h[:, off + c * P:off + (c + 1) * P], self.S["ident"][:, :])
            mm.then_inc(self.turned, 1)
            pe.wait_ge(self.ht_made, t * EX + e + 1)
            if e == 0:
                pe.wait_ge(self.y_copied, t)
            y = self.yp[:, e * D:(e + 1) * D]
            for c in range(4):
                pe.matmul(y, self.ht[:, off + c * P:off + (c + 1) * P], self.w2[:, (e * 4 + c) * D:(e * 4 + c + 1) * D], start=(c == 0), stop=False)
            pe.matmul(y, self.ones[:, :], self.b2[:, e * D:(e + 1) * D], start=False, stop=True).then_inc(self.y_made, 1)

        hidden(0)
        for e in range(1, EX):
            hidden(e)
            second(e - 1)
        second(EX - 1)


U = 5
ROUNDS = NTP // U


def choose(dve, st, score, E, tri, work, sel, prob, eps):
    gt, eq, rank, keep, mx, z = work
    si = score.unsqueeze(3).to_broadcast([P, U, E, E])
    sj = score.unsqueeze(2).to_broadcast([P, U, E, E])
    st.inc(dve.tensor_tensor(gt, sj, si, ALU.is_gt))
    st.link(dve, dve.tensor_tensor(eq, sj, si, ALU.is_equal))
    st.link(dve, dve.tensor_tensor(eq, eq, tri.unsqueeze(1).to_broadcast([P, U, E, E]), ALU.mult))
    st.link(dve, dve.tensor_tensor(gt, gt, eq, ALU.add))
    st.link(dve, dve.tensor_reduce(rank, gt, AX.X, ALU.add))
    st.inc(dve.tensor_scalar(keep, rank, 1.5, None, ALU.is_lt))
    st.link(dve, dve.tensor_reduce(mx, score, AX.X, ALU.max))
    st.link(dve, dve.tensor_tensor(prob, score, mx.unsqueeze(2).to_broadcast([P, U, E]), ALU.subtract))


def dense(nc, k, H, C, x_in, x_out, table, own_rows, inv_next, weights, S, agg=None, inv=None, extra=None):
    last = k == 3
    CW = H * (C + 1) if not last else 0
    RW = CW + 2 * H if not last else 8
    W = H * C + 2 * H if not last else 8
    with Scope(nc, f"dense{k}", S["keep"]) as s:
        x = s.sb("x", [P, U * D])
        xn = s.sb("xn", [P, U * D])
        stats, mv = s.sb("stats", [P, U * 6]), s.sb("mv", [P, U * 2])
        rstd = s.sb("rstd", [P, U])
        eps = s.sb("eps", [P, 1])
        xt = s.sb("xt", [P, U * D])
        wcat = s.sb("wcat", [P, 2 * W])
        rows = s.sb("rows", [P, U * RW])
        tp, mp = s.ps("tp", [P, 3 * 512]), s.ps("mp", [P, U * 512])
        w_in, w_step, w_ready, made = s.sem("w_in"), s.sem("w_step"), s.sem("w_ready"), s.sem("made")
        x_in_s, x_read, got, inv_in, inv_set = s.sem("x_in"), s.sem("x_read"), s.pool_sem("got"), s.sem("inv_in"), s.sem("inv_set")
        step, var_done, std_done, normed, turned, xt_made, product, rows_made = [s.sem(n) for n in
            ("step", "var_done", "std_done", "normed", "turned", "xt_made", "product", "rows_made")]
        x_stored, t_stored, t_scattered, dve_passed, o_stored, sp_passed, pool_passed, gathered_used, summed = [s.pool_sem(n) if n == "t_scattered" else s.sem(n) for n in
            ("x_stored", "t_stored", "t_scattered", "dve_passed", "o_stored", "sp_passed", "pool_passed", "gathered_used", "summed")]
        if not last:
            inv_n, inv_n5 = s.sb("inv_n", [P, NTP], I32), s.sb("inv_n5", [P, U], I32)
        if k:
            inv_a, inv_a5 = s.sb("inv_a", [P, NTP], I32), s.sb("inv_a5", [P, U], I32)
            GW = 16 if k == 2 else D
            gat = s.sb("gathered", [P, U * GW])
        if k == 2:
            y = s.sb("y", [P, U * 4 * D])
            lnw, lnb, bg = s.sb("gamma", [P, 16]), s.sb("beta", [P, 16]), s.sb("b_gat", [P, 16])
            sq, ssum = s.sb("sq", [P, U * 16]), s.sb("ssum", [P, U])
            sc_std = s.sb("sc_std", [P, U])
        if last:
            bias = s.sb("bias", [P, D])
        if k >= 2:
            E = 4 if k == 2 else 8
            tri, tri_i = s.sb("tri", [P, E, E]), s.sb("tri_i", [P, E, E], I32)
            score = s.sb("score", [P, U, E])
            gt, eq, rank, keep = s.sb("gt", [P, U, E, E]), s.sb("eq", [P, U, E, E]), s.sb("rank", [P, U, E]), s.sb("keep", [P, U, E])
            mx, z, prob = s.sb("mx", [P, U]), s.sb("z", [P, U]), s.sb("prob", [P, U, E])
            sc_ready, sc_exp, sc_sq, sc_rt = s.sem("sc_ready"), s.sem("sc_exp"), s.sem("sc_sq"), s.sem("sc_rt")
        x3 = x[:, :].rearrange("p (u d) -> p u d", u=U)
        xn3 = xn[:, :].rearrange("p (u d) -> p u d", u=U)
        mv3 = mv[:, :].rearrange("p (u a) -> p u a", u=U)
        rows3 = rows[:, :].rearrange("p (u w) -> p u w", u=U)
        mp3 = mp[:, :].rearrange("p (u w) -> p u w", u=U)
        if k == 0:
            w_nat = s.sb("w_nat", [P, 2 * D])
        if not last:
            a_l, a_r = s.sb("a_l", [P, H * C]), s.sb("a_r", [P, H * C])
            fold = s.sb("fold", [P, H * C])
        nw = {0: 3, 1: 3, 2: 3 + H - 1 + 3, 3: 2}[k]
        wc3 = wcat[:, :].rearrange("p (k w) -> p k w", k=2)
        NINV = (0 if last else 1) + (1 if k else 0)
        with nc.Block() as block:
            @block.sync
            def _(sp):
                if k == 0:
                    sp.dma_start(w_nat[:, :].rearrange("p (a d) -> p a d", a=2), weights["w"].rearrange("(a p) d -> p a d", p=P)).then_inc(w_in, 16)
                elif k == 1:
                    sp.dma_start(wc3[:, :, 0:H * C], weights["w"].rearrange("(k p) n -> p k n", p=P)).then_inc(w_in, 16)
                elif k == 2:
                    for h in range(H):
                        sp.dma_start(wc3[:, :, h * C:(h + 1) * C], weights["w"][h].rearrange("(k p) c -> p k c", p=P)).then_inc(w_in, 16)
                    for t, src in ((lnw, "gamma"), (lnb, "beta"), (bg, "b_gat")):
                        sp.dma_start(t[:, :], weights[src].rearrange("(a n) -> a n", a=1).to_broadcast([P, 16])).then_inc(w_in, 16)
                else:
                    with nc.allow_non_contiguous_dma(reason="2048 words, transposed"):
                        for kc in range(2):
                            sp.dma_start(wc3[:, kc, :], weights["w"][:, kc * P:(kc + 1) * P].rearrange("e p -> p e")).then_inc(w_in, 16)
                    sp.dma_start(bias[:, :], weights["bias"].rearrange("(a n) -> a n", a=1).to_broadcast([P, D])).then_inc(w_in, 16)
                if not last:
                    sp.dma_start(a_l[:, :], weights["neigh"].to_broadcast([P, H * C])).then_inc(w_in, 16)
                    sp.dma_start(a_r[:, :], weights["mine"].to_broadcast([P, H * C])).then_inc(w_in, 16)
                    with nc.allow_non_contiguous_dma(reason="node order"):
                        sp.dma_start(inv_n[:, :], inv_next.rearrange("(t p) -> p t", p=P)).then_inc(inv_in, 16)
                if k:
                    with nc.allow_non_contiguous_dma(reason="node order"):
                        sp.dma_start(inv_a[:, :], inv.rearrange("(t p) -> p t", p=P)).then_inc(inv_in, 16)
                with sp.Fori(0, ROUNDS) as i:
                    r0 = i * (U * P)
                    sp.wait_ge(x_read, i)
                    sp.sem_inc(sp_passed, 1)
                    if k:
                        sp.wait_ge(x_stored, i * 16)
                        sp.sem_inc(sp_passed, 1)
                    sp.dma_start(x3, x_in[ds(r0, U * P), :].rearrange("(u p) d -> p u d", p=P)).then_inc(x_in_s, 16)
                    if k == 2:
                        sp.dma_start(y[:, :].rearrange("p (u d) -> p u d", u=U), extra["y"][ds(r0, U * P), :].rearrange("(u p) d -> p u d", p=P)).then_inc(x_in_s, 16)
                    if k:
                        sp.wait_ge(summed, i + 1)
                        sp.sem_inc(sp_passed, 1)
                        sp.dma_start(x_out[ds(r0, U * P), :].rearrange("(u p) d -> p u d", p=P), x3).then_inc(x_stored, 16)
                    if k == 1:
                        sp.wait_ge(xt_made, i + 1)
                        sp.sem_inc(sp_passed, 1)
                        sp.dma_start(extra["xt"][ds(i * U, U), :, :].rearrange("u p n -> p u n"), xt[:, :].rearrange("p (u n) -> p u n", u=U)).then_inc(o_stored, 16)
                    if last:
                        sp.wait_ge(normed, i + 1)
                        sp.sem_inc(sp_passed, 1)
                        sp.dma_start(extra["xn"][ds(r0, U * P), :].rearrange("(u p) d -> p u d", p=P), xn3).then_inc(o_stored, 16)
                    else:
                        sp.wait_ge(rows_made, i * 2 + 2)
                        sp.sem_inc(sp_passed, 1)
                        sp.dma_start(table[ds(r0, U * P), :].rearrange("(u p) d -> p u d", p=P), rows3).then_inc(t_stored, 16)
                if k:
                    sp.wait_ge(x_stored, ROUNDS * 16)
                if k in (1, 3):
                    sp.wait_ge(o_stored, ROUNDS * 16)
                if not last:
                    sp.wait_ge(t_stored, ROUNDS * 16)
                    sp.wait_ge(t_scattered, ROUNDS * 16 * U)

            @block.gpsimd
            def _(pool):
                if k >= 2:
                    pool.iota(tri_i[:, :, :], [[1, E], [-1, E]], base=0, channel_multiplier=0).then_inc(made, 1)
                with pool.Fori(0, ROUNDS) as i:
                    if k:
                        pool.wait_ge(inv_set, i * NINV + NINV)
                        pool.wait_ge(gathered_used, i)
                        pool.sem_inc(pool_passed, 1)
                        for u in range(U):
                            pool.indirect_dma_start(out=gat[:, u * GW:(u + 1) * GW], out_offset=None, in_=agg,
                                                    in_offset=bass.IndirectOffsetOnAxis(ap=inv_a5[:, u:u + 1], axis=0)).then_inc(got, 16)
                    if not last:
                        pool.wait_ge(inv_set, i * NINV + NINV)
                        pool.wait_ge(rows_made, i * 2 + 2)
                        pool.sem_inc(pool_passed, 1)
                        for u in range(U):
                            pool.indirect_dma_start(out=own_rows, in_=rows[:, u * RW:(u + 1) * RW], in_offset=None,
                                                    out_offset=bass.IndirectOffsetOnAxis(ap=inv_n5[:, u:u + 1], axis=0)).then_inc(t_scattered, 16)

            @block.vector
            def _(dve):
                ws = Count(w_step)
                ws.link(dve, dve.memset(eps[:, :], 1e-5))
                if k >= 2:
                    dve.wait_ge(made, 1)
                    ws.link(dve, dve.tensor_scalar(tri[:, :, :], tri_i[:, :, :], 0.5, None, ALU.is_gt))
                if not last:
                    if CW:
                        ws.link(dve, dve.memset(rows[:, :], 1.0))
                    dve.wait_ge(w_in, nw * 16)
                    if k == 0:
                        dve.wait_ge(w_ready, 1)
                        for kc in range(2):
                            ws.link(dve, dve.tensor_copy(wc3[:, kc, 0:D], tp[:, kc * D:(kc + 1) * D]))
                    for kc in range(2):
                        for side, a in ((0, a_l), (1, a_r)):
                            ws.link(dve, dve.tensor_tensor(fold[:, :], wc3[:, kc, 0:H * C], a[:, :], ALU.mult))
                            ws.link(dve, dve.tensor_reduce(wc3[:, kc, H * C + side * H:H * C + (side + 1) * H],
                                                           fold[:, :].rearrange("p (h c) -> p h c", h=H), AX.X, ALU.add))
                else:
                    dve.wait_ge(w_in, 48)
                ws.link(dve, dve.memset(rstd[:, :], 0.0))
                dve.sem_inc(w_ready, 1)
                if NINV:
                    dve.wait_ge(inv_in, NINV * 16)

                def body(i, st):
                    if not last:
                        dve.wait_ge(t_scattered, i * (16 * U))
                        dve.tensor_copy(inv_n5[:, :], inv_n[:, ds(i * U, U)]).then_inc(inv_set, 1)
                    if k:
                        dve.wait_ge(got, i * (U * 16))
                        dve.tensor_copy(inv_a5[:, :], inv_a[:, ds(i * U, U)]).then_inc(inv_set, 1)
                        dve.wait_ge(x_in_s, i * (32 if k == 2 else 16) + (32 if k == 2 else 16))
                        dve.wait_ge(got, i * (U * 16) + U * 16)
                    if k in (1, 3):
                        ins = st.inc(dve.tensor_tensor(x[:, :], x[:, :], gat[:, :], ALU.add))
                        st.wait(dve)
                        dve.sem_inc(gathered_used, 1)
                        if last:
                            st.link(dve, dve.tensor_tensor(x3, x3, bias[:, :].unsqueeze(1).to_broadcast([P, U, D]), ALU.add))
                        dve.sem_inc(summed, 1)
                    elif k == 2:
                        g3 = gat[:, :].rearrange("p (u c) -> p u c", u=U)
                        b3 = lambda t: t[:, :].unsqueeze(1).to_broadcast([P, U, 16])
                        w3 = lambda t: t[:, :].unsqueeze(2).to_broadcast([P, U, 16])
                        sq3 = sq[:, :].rearrange("p (u c) -> p u c", u=U)
                        st.link(dve, dve.tensor_tensor(sq3, g3, b3(bg), ALU.add))
                        dve.sem_inc(gathered_used, 1)
                        st.link(dve, dve.tensor_reduce(ssum[:, :], sq3, AX.X, ALU.add))
                        st.link(dve, dve.tensor_scalar(ssum[:, :], ssum[:, :], -1.0 / 16, None, ALU.mult))
                        st.link(dve, dve.tensor_tensor(sq3, sq3, w3(ssum), ALU.add))
                        st.link(dve, dve.tensor_tensor(g3, sq3, sq3, ALU.mult))
                        st.link(dve, dve.tensor_reduce(ssum[:, :], g3, AX.X, ALU.add))
                        st.link(dve, dve.tensor_scalar(ssum[:, :], ssum[:, :], 1.0 / 16, 1e-5, ALU.mult, ALU.add))
                        dve.sem_inc(sc_sq, 1)
                        dve.wait_ge(sc_rt, i + 1)
                        st.link(dve, dve.reciprocal(sc_std[:, :], sc_std[:, :]))
                        st.link(dve, dve.tensor_tensor(sq3, sq3, w3(sc_std), ALU.mult))
                        st.link(dve, dve.tensor_tensor(sq3, sq3, b3(lnw), ALU.mult))
                        st.link(dve, dve.tensor_tensor(sq3, sq3, b3(lnb), ALU.add))
                        st.link(dve, dve.tensor_reduce(score[:, :, :], sq[:, :].rearrange("p (u h e) -> p u e h", u=U, h=4), AX.X, ALU.add))
                        st.link(dve, dve.tensor_scalar(score[:, :, :], score[:, :, :], 0.25, None, ALU.mult))
                        choose(dve, st, score[:, :, :], E, tri[:, :, :], (gt[:, :, :, :], eq[:, :, :, :], rank[:, :, :], keep[:, :, :], mx[:, :], z[:, :]), None, prob[:, :, :], 0.0)
                        dve.sem_inc(sc_ready, 1)
                        dve.wait_ge(sc_exp, i + 1)
                        st.link(dve, dve.tensor_tensor(prob[:, :, :], prob[:, :, :], keep[:, :, :], ALU.mult))
                        st.link(dve, dve.tensor_reduce(z[:, :], prob[:, :, :], AX.X, ALU.add))
                        st.link(dve, dve.reciprocal(z[:, :], z[:, :]))
                        st.link(dve, dve.tensor_tensor(prob[:, :, :], prob[:, :, :], z[:, :].unsqueeze(2).to_broadcast([P, U, E]), ALU.mult))
                        for e in range(E):
                            for u in range(U):
                                st.inc(dve.scalar_tensor_tensor(out=x3[:, u, :], in0=y[:, (u * 4 + e) * D:(u * 4 + e + 1) * D], scalar=prob[:, u, e:e + 1],
                                                                in1=x3[:, u, :], op0=ALU.mult, op1=ALU.add))
                            st.wait(dve)
                        dve.sem_inc(summed, 1)
                    else:
                        dve.wait_ge(x_in_s, i * 16 + 16)
                    for u in range(U):
                        st.inc(dve.bn_stats(stats[:, u * 6:(u + 1) * 6], x3[:, u, :]))
                    st.wait(dve)
                    dve.sem_inc(dve_passed, 1)
                    for u in range(U):
                        st.inc(dve.bn_aggr(mv[:, u * 2:(u + 1) * 2], stats[:, u * 6:(u + 1) * 6]))
                    st.wait(dve)
                    dve.sem_inc(var_done, 1)
                    dve.wait_ge(std_done, i + 1)
                    st.link(dve, dve.reciprocal(rstd[:, :], rstd[:, :]))
                    dve.wait_ge(turned, i)
                    if last:
                        dve.wait_ge(o_stored, i * 16)
                    for u in range(U):
                        st.inc(dve.tensor_scalar(xn3[:, u, :], x3[:, u, :], mv[:, u * 2:u * 2 + 1], rstd[:, u:u + 1], ALU.subtract, ALU.mult))
                    st.wait(dve)
                    dve.sem_inc(normed, 1)
                    dve.sem_inc(x_read, 1)
                    if last:
                        dve.wait_ge(rows_made, i * 2 + 2)
                        st.link(dve, dve.tensor_copy(score[:, :, :], rows3))
                        choose(dve, st, score[:, :, :], E, tri[:, :, :], (gt[:, :, :, :], eq[:, :, :, :], rank[:, :, :], keep[:, :, :], mx[:, :], z[:, :]), None, prob[:, :, :], 0.0)
                        dve.sem_inc(sc_ready, 1)
                        dve.wait_ge(sc_exp, i + 1)
                        st.link(dve, dve.tensor_reduce(z[:, :], prob[:, :, :], AX.X, ALU.add))
                        st.link(dve, dve.reciprocal(z[:, :], z[:, :]))
                        st.link(dve, dve.tensor_tensor(prob[:, :, :], prob[:, :, :], z[:, :].unsqueeze(2).to_broadcast([P, U, E]), ALU.mult))
                        st.link(dve, dve.tensor_tensor(prob[:, :, :], prob[:, :, :], keep[:, :, :], ALU.mult))
                        st.link(dve, dve.tensor_reduce(z[:, :], prob[:, :, :], AX.X, ALU.add))
                        st.link(dve, dve.tensor_scalar(z[:, :], z[:, :], 1e-9, None, ALU.add))
                        st.link(dve, dve.reciprocal(z[:, :], z[:, :]))
                        st.link(dve, dve.tensor_tensor(extra["gate"][:, ds(i * U, U), :], prob[:, :, :], z[:, :].unsqueeze(2).to_broadcast([P, U, E]), ALU.mult))
                        st.link(dve, dve.tensor_copy(extra["rank"][:, ds(i * U, U), :], rank[:, :, :]))

                STEPS = {0: 16, 1: 17, 2: 61, 3: 18 + 1 + 8 + 9}[k]
                with dve.Fori(0, ROUNDS) as i:
                    st = Count(step, i * STEPS)
                    body(i, st)
                    assert st.n == STEPS, (k, st.n, STEPS)

            @block.scalar
            def _(act):
                act.wait_ge(w_ready, 2 if k == 0 else 1)
                with act.Fori(0, ROUNDS) as i:
                    if k == 2:
                        act.wait_ge(sc_sq, i + 1)
                        act.activation(sc_std[:, :], ssum[:, :], ACT.Sqrt).then_inc(sc_rt, 1)
                        act.wait_ge(sc_ready, i + 1)
                        act.activation(prob[:, :, :], prob[:, :, :], ACT.Exp).then_inc(sc_exp, 1)
                    act.wait_ge(var_done, i + 1)
                    act.activation(rstd[:, :], mv3[:, :, 1], ACT.Sqrt, bias=eps[:, :]).then_inc(std_done, 1)
                    act.wait_ge(turned, i + 1)
                    act.wait_ge(product, i)
                    if k == 1:
                        act.wait_ge(o_stored, i * 16)
                    act.activation(xt[:, :], tp[:, 0:U * D], ACT.Copy).then_inc(xt_made, 1)
                    act.wait_ge(product, i + 1)
                    if last:
                        act.activation(rows3, mp3[:, :, 0:8], ACT.Copy).then_inc(rows_made, 2)
                        act.wait_ge(sc_ready, i + 1)
                        act.activation(prob[:, :, :], prob[:, :, :], ACT.Exp).then_inc(sc_exp, 1)
                    else:
                        act.wait_ge(t_stored, i * 16)
                        act.wait_ge(t_scattered, i * (16 * U))
                        for u in range(U):
                            ins = act.activation(rows3[:, u, 0:CW].rearrange("p (h c) -> p h c", h=H)[:, :, 0:C],
                                                 mp3[:, u, 0:H * C].rearrange("p (h c) -> p h c", h=H), ACT.Copy)
                        ins.then_inc(rows_made, 1)
                        act.activation(rows3[:, :, CW:RW], mp3[:, :, H * C:W], ACT.Copy).then_inc(rows_made, 1)

            @block.tensor
            def _(pe):
                if k == 0:
                    pe.wait_ge(w_in, nw * 16)
                    for kc in range(2):
                        for a in range(2):
                            mm = pe.transpose(tp[:, kc * D + a * P:kc * D + (a + 1) * P], w_nat[:, a * D + kc * P:a * D + (kc + 1) * P], S["ident"][:, :])
                    mm.then_inc(w_ready, 1)
                pe.wait_ge(w_ready, 2 if k == 0 else 1)
                with pe.Fori(0, ROUNDS) as i:
                    pe.wait_ge(normed, i + 1)
                    pe.wait_ge(xt_made, i)
                    for u in range(U):
                        for kc in range(2):
                            c = (u * 2 + kc) * P
                            mm = pe.transpose(tp[:, c:c + P], xn[:, c:c + P], S["ident"][:, :])
                    mm.then_inc(turned, 1)
                    pe.wait_ge(xt_made, i + 1)
                    pe.wait_ge(rows_made, i * 2)
                    for u in range(U):
                        for kc in range(2):
                            c = (u * 2 + kc) * P
                            mm = pe.matmul(mp3[:, u, 0:W], xt[:, c:c + P], wc3[:, kc, :], start=(kc == 0), stop=(kc == 1))
                    mm.then_inc(product, 1)


def prepare(nc, x, x0, tables, zeroed, S):
    with Scope(nc, "prep") as s:
        z = s.sb("z", [P, 2048])
        xl = s.sb("xl", [P, D])
        empty = [s.sb(f"empty{i}", [1, t.shape[1]]) for i, (t, H) in enumerate(tables)]
        cleared, filled, stored, step = s.sem("cleared"), s.sem("filled"), s.sem("stored"), s.sem("step")
        rest = N - (NT - 1) * P
        n = 0
        with nc.Block() as block:
            @block.vector
            def _(dve):
                dve.memset(z[:, :], 0.0).then_inc(cleared, 1)
                st = Count(step)
                for e, (t, H) in zip(empty, tables):
                    RW = t.shape[1]
                    st.link(dve, dve.memset(e[:, :], 0.0))
                    st.link(dve, dve.memset(e[:, RW - 2 * H:RW - H], NEG))
                dve.sem_inc(filled, 1)

            @block.sync
            def _(sp):
                st = Count(stored)
                st.inc(sp.dma_start(x0[0:(NT - 1) * P, :].rearrange("(a b) d -> a (b d)", a=P), x[0:(NT - 1) * P, :].rearrange("(a b) d -> a (b d)", a=P)), 16)
                st.inc(sp.dma_start(x0[(NT - 1) * P:N, :], x[(NT - 1) * P:N, :]), 16)
                sp.wait_ge(cleared, 1)
                st.inc(sp.dma_start(x0[N:N + 75, :], z[0:75, 0:D]), 16)
                st.inc(sp.dma_start(x0[N + 75:NP, :], z[0:75, 0:D]), 16)
                for t in zeroed:
                    rows_, width = t.shape
                    for r in range(0, rows_, P):
                        m = min(P, rows_ - r)
                        st.inc(sp.dma_start(t[r:r + m, :], z[0:m, 0:width]), 16)
                sp.wait_ge(filled, 1)
                for e, (t, H) in zip(empty, tables):
                    st.inc(sp.dma_start(t[DUMMY:DUMMY + 1, :], e[:, :]), 16)
                st.wait(sp)


EX = 8
HID = 682
HJ = 6
HR = HID - 5 * P
MT = (2 * N + EX * (P - 1)) // P
SPARE = MT * P
SLOT_ROWS = SPARE + 4 * P


class MixtureSetUp:

    def __init__(self, w1, w2, w3, w13t, w2t, xe, ye):
        self.w1, self.w2, self.w3, self.w13t, self.w2t, self.xe, self.ye = w1, w2, w3, w13t, w2t, xe, ye

    def allocate(self, s, S):
        self.ident = S["ident"]
        self.n1, self.n3, self.n2 = s.sb("n1", [P, HJ * D]), s.sb("n3", [P, HJ * D]), s.sb("n2", [P, 2 * HID])
        self.t13, self.t2, self.z = s.sb("t13", [P, 2 * 2 * HID]), s.sb("t2", [P, HJ * D]), s.sb("z", [P, 7 * D])
        self.ps = s.ps("weights_turned", [P, 2048])
        self.zeroed, self.weights_in, self.turned, self.kept, self.turned_stored, self.zeros_stored = [s.sem(n) for n in
            ("zeroed", "weights_in", "weights_in_psum", "kept", "turned_stored", "zeros_stored")]

    def vector(self, dve):
        dve.memset(self.z[:, :], 0.0).then_inc(self.zeroed, 1)

    def scalar(self, act):
        act.wait_ge(self.zeroed, 1)
        with act.Fori(0, MT // 7) as i:
            act.dma_start(self.xe[ds(i * (7 * P), 7 * P), :].rearrange("(p a) d -> p (a d)", p=P), self.z[:, :]).then_inc(self.zeros_stored, 16)
        for rows in (self.xe, self.ye):
            act.dma_start(rows[SPARE:SLOT_ROWS, :].rearrange("(p a) d -> p (a d)", p=P), self.z[:, 0:4 * D]).then_inc(self.zeros_stored, 16)
        t13v = self.t13[:, :].rearrange("p (k n) -> p k n", k=2)
        psv = self.ps[:, :].rearrange("p (k n) -> p k n", k=2)
        with act.Fori(0, EX) as e:
            act.wait_ge(self.turned, e * 3)
            for w, n in ((self.w1, self.n1), (self.w3, self.n3)):
                act.dma_start(n[:, 0:5 * D].rearrange("p (j d) -> p j d", j=5),
                              w[ds(e, 1), 0:5 * P, :].rearrange("a (j p) d -> p (a j) d", p=P)).then_inc(self.weights_in, 16)
                act.dma_start(n[0:HR, 5 * D:6 * D], w[ds(e, 1), 5 * P:HID, :].rearrange("a p d -> (a p) d")).then_inc(self.weights_in, 16)
            act.dma_start(self.n2[:, :].rearrange("p (c h) -> p c h", c=2),
                          self.w2[ds(e, 1), :, :].rearrange("a (c p) h -> p (a c) h", p=P)).then_inc(self.weights_in, 16)
            act.wait_ge(self.turned_stored, e * 48)
            for k in range(2):
                act.wait_ge(self.turned, e * 3 + k + 1)
                act.activation(t13v[:, :, k * HID:(k + 1) * HID], psv[:, :, 0:HID], ACT.Copy).then_inc(self.kept, 1)
            act.wait_ge(self.kept, e * 4 + 2)
            act.dma_start(self.w13t[ds(e, 1), :, :].rearrange("a p n -> (a p) n"), self.t13[:, :]).then_inc(self.turned_stored, 16)
            act.wait_ge(self.turned, e * 3 + 3)
            act.activation(self.t2[:, 0:5 * D], self.ps[:, 0:5 * D], ACT.Copy).then_inc(self.kept, 1)
            act.activation(self.t2[0:HR, 5 * D:6 * D], self.ps[0:HR, 5 * D:6 * D], ACT.Copy).then_inc(self.kept, 1)
            act.wait_ge(self.kept, e * 4 + 4)
            act.dma_start(self.w2t[ds(e, 1), :, 0:5 * D].rearrange("a p n -> (a p) n"), self.t2[:, 0:5 * D]).then_inc(self.turned_stored, 16)
            act.dma_start(self.w2t[ds(e, 1), 0:HR, 5 * D:6 * D].rearrange("a p n -> (a p) n"), self.t2[0:HR, 5 * D:6 * D]).then_inc(self.turned_stored, 16)
        act.wait_ge(self.turned_stored, EX * 48)
        act.wait_ge(self.zeros_stored, (MT // 7 + 2) * 16)

    def tensor(self, pe):
        psv = self.ps[:, :].rearrange("p (k n) -> p k n", k=2)
        piece = [P] * (HJ - 1) + [HR]
        with pe.Fori(0, EX) as e:
            pe.wait_ge(self.weights_in, e * 80 + 80)
            for k, n in enumerate((self.n1, self.n3)):
                pe.wait_ge(self.kept, e * 4 + k)
                for kc in range(2):
                    for j, m in enumerate(piece):
                        mm = pe.transpose(psv[:, kc, j * P:j * P + m], n[0:m, j * D + kc * P:j * D + (kc + 1) * P], self.ident[0:m, 0:m])
                mm.then_inc(self.turned, 1)
            pe.wait_ge(self.kept, e * 4 + 2)
            for j, m in enumerate(piece):
                for c in range(2):
                    mm = pe.transpose(self.ps[0:m, j * D + c * P:j * D + (c + 1) * P], self.n2[:, c * HID + j * P:c * HID + j * P + m], self.ident[:, :])
            mm.then_inc(self.turned, 1)


W13, W2 = 4 * HID, HJ * D


def dispatch(nc, xn3, xe, w13t, w2t, R, S):
    with Scope(nc, "dispatch", S["keep"]) as s:
        node, spare, tau_i = s.sb("node", [P, NTP], I32), s.sb("spare", [P, 2, NTP], I32), s.sb("tau_i", [1, MT + 1], I32)
        pq = s.sb("pq", [P, P], I32)
        real, fake, below, ones = s.sb("real", [P, NTP]), s.sb("fake", [P, NTP]), s.sb("below", [P, P]), s.sb("ones", [P, P])
        sel, run, per = s.sb("sel", [P, EX, NTP]), s.sb("run", [P, EX, NTP]), s.sb("per", [P, EX])
        sums = s.ps("sums", [P, 2 * EX])
        tiles_i, tiles, ends, base = s.sb("tiles_i", [P, EX], I32), s.sb("tiles", [P, EX]), s.sb("ends", [P, EX]), s.sb("base", [P, EX])
        one8 = s.sb("one8", [P, EX])
        is_k, prod, posf = s.sb("is_k", [P, NTP, EX]), s.sb("prod", [P, NTP, EX]), s.sb("posf", [P, NTP])
        cmp, tef, tau = s.sb("cmp", [1, MT + 1, EX]), s.sb("tef", [1, MT + 1]), s.sb("tau", [1, MT + 1])
        pos5 = s.sb("pos5", [P, 2, U], I32)
        rows = s.sb("rows", [P, 2 * U * D])
        made, step, counted, summed, ready, loaded, used, sp_passed, pool_passed, set5 = [s.sem(n) for n in
            ("made", "step", "counted", "summed", "ready", "loaded", "used", "sp_passed", "pool_passed", "set5")]
        scattered = s.pool_sem("scattered")
        with nc.Block() as block:
            @block.scalar
            def _(act):
                w13, w2, w_in = R["w13"], R["w2"], R["w_in"]
                for e in range(EX):
                    act.dma_start(w13[:, e * W13:(e + 1) * W13], w13t[e, :, :]).then_inc(w_in, 16)
                    act.dma_start(w2[:, e * W2:e * W2 + 5 * D], w2t[e, :, 0:5 * D]).then_inc(w_in, 16)
                    act.dma_start(w2[0:HR, e * W2 + 5 * D:(e + 1) * W2], w2t[e, 0:HR, 5 * D:6 * D]).then_inc(w_in, 16)
                act.wait_ge(w_in, EX * 48)

            @block.gpsimd
            def _(pool):
                pool.iota(node[:, :], [[P, NTP]], base=0, channel_multiplier=1).then_inc(made, 1)
                for c in range(2):
                    pool.iota(spare[:, c, :], [[2 * P, NTP]], base=SPARE - 2 * P * (NT - 1) + c * P, channel_multiplier=1).then_inc(made, 1)
                pool.iota(tau_i[:, :], [[1, MT + 1]], base=0, channel_multiplier=0).then_inc(made, 1)
                pool.iota(pq[:, :], [[1, P]], base=0, channel_multiplier=-1).then_inc(made, 1)
                with pool.Fori(0, ROUNDS) as i:
                    pool.wait_ge(set5, i * 2 + 2)
                    pool.wait_ge(loaded, i * 16 + 16)
                    pool.sem_inc(pool_passed, 1)
                    for u in range(U):
                        for c in range(2):
                            pool.indirect_dma_start(out=xe, in_=rows[:, u * D:(u + 1) * D], in_offset=None,
                                                    out_offset=bass.IndirectOffsetOnAxis(ap=pos5[:, c, u:u + 1], axis=0)).then_inc(scattered, 16)
                pool.wait_ge(scattered, ROUNDS * 2 * U * 16)

            @block.sync
            def _(sp):
                with sp.Fori(0, ROUNDS) as i:
                    sp.wait_ge(scattered, i * (2 * U * 16))
                    sp.sem_inc(sp_passed, 1)
                    sp.dma_start(rows[:, 0:U * D].rearrange("p (u d) -> p u d", u=U), xn3[ds(i * (U * P), U * P), :].rearrange("(u p) d -> p u d", p=P)).then_inc(loaded, 16)
                sp.wait_ge(loaded, ROUNDS * 16)

            @block.tensor
            def _(pe):
                pe.wait_ge(counted, 1)
                pe.matmul(sums[:, 0:EX], below[:, :], per[:, :], start=True, stop=True)
                pe.matmul(sums[:, EX:2 * EX], ones[:, :], per[:, :], start=True, stop=True).then_inc(summed, 1)

            @block.vector
            def _(dve):
                st = Count(step)
                dve.wait_ge(made, 5)
                rk = R["rank"]
                st.inc(dve.memset(ones[:, :], 1.0))
                st.inc(dve.memset(one8[:, :], 1.0))
                st.inc(dve.tensor_scalar(below[:, :], pq[:, :], 0.5, None, ALU.is_gt))
                st.inc(dve.tensor_scalar(real[:, :], node[:, :], float(N), None, ALU.is_lt))
                st.inc(dve.tensor_scalar(fake[:, :], node[:, :], float(N), None, ALU.is_ge))
                st.inc(dve.tensor_copy(tau[:, :], tau_i[:, :]))
                st.link(dve, dve.tensor_scalar(prod[:, :, :], rk[:, :, :], 1.5, None, ALU.is_lt))
                st.link(dve, dve.tensor_tensor(sel[:, :, :].rearrange("p e t -> p t e"), prod[:, :, :], real[:, :].unsqueeze(2).to_broadcast([P, NTP, EX]), ALU.mult))
                for e in range(EX):
                    st.inc(dve.tensor_tensor_scan(run[:, e, :], ones[:, 0:NTP], sel[:, e, :], 0.0, ALU.mult, ALU.add))
                st.wait(dve)
                st.link(dve, dve.tensor_copy(per[:, :], run[:, :, NTP - 1]))
                dve.sem_inc(counted, 1)
                dve.wait_ge(summed, 1)
                st.link(dve, dve.tensor_scalar(tiles_i[:, :], sums[:, EX:2 * EX], float(P - 1), None, ALU.add))
                st.link(dve, dve.tensor_scalar(tiles_i[:, :], tiles_i[:, :], 7, None, ALU.logical_shift_right))
                st.link(dve, dve.tensor_copy(tiles[:, :], tiles_i[:, :]))
                st.link(dve, dve.tensor_tensor_scan(ends[:, :], one8[:, :], tiles[:, :], 0.0, ALU.mult, ALU.add))
                st.link(dve, dve.tensor_tensor(base[:, :], ends[:, :], tiles[:, :], ALU.subtract))
                st.link(dve, dve.tensor_scalar(base[:, :], base[:, :], float(P), -1.0, ALU.mult, ALU.add))
                st.link(dve, dve.tensor_tensor(base[:, :], base[:, :], sums[:, 0:EX], ALU.add))
                st.link(dve, dve.tensor_tensor(run[:, :, :], run[:, :, :], base[:, :].unsqueeze(2).to_broadcast([P, EX, NTP]), ALU.add))
                for c in range(2):
                    st.link(dve, dve.tensor_scalar(is_k[:, :, :], rk[:, :, :], float(c), None, ALU.is_equal))
                    st.link(dve, dve.tensor_tensor(prod[:, :, :], run[:, :, :].rearrange("p e t -> p t e"), is_k[:, :, :], ALU.mult))
                    st.link(dve, dve.tensor_reduce(posf[:, :], prod[:, :, :], AX.X, ALU.add))
                    st.link(dve, dve.tensor_tensor(posf[:, :], posf[:, :], real[:, :], ALU.mult))
                    st.link(dve, dve.tensor_tensor(prod[:, :, 0], spare[:, c, :], fake[:, :], ALU.mult))
                    st.link(dve, dve.tensor_tensor(R["pos"][:, c, :], posf[:, :], prod[:, :, 0], ALU.add))
                    st.link(dve, dve.tensor_tensor(prod[:, :, :], R["gate"][:, :, :], is_k[:, :, :], ALU.mult))
                    st.link(dve, dve.tensor_reduce(R["g"][:, c, :], prod[:, :, :], AX.X, ALU.add))
                st.link(dve, dve.tensor_tensor(cmp[:, :, :], tau[:, :].unsqueeze(2).to_broadcast([1, MT + 1, EX]),
                                               ends[0:1, :].unsqueeze(1).to_broadcast([1, MT + 1, EX]), ALU.is_ge))
                st.link(dve, dve.tensor_reduce(tef[:, :], cmp[:, :, :], AX.X, ALU.add))
                st.link(dve, dve.tensor_scalar(R["expert"][:, :], tef[:, :], float(EX - 1), None, ALU.min))
                with dve.Fori(0, ROUNDS) as i:
                    dve.wait_ge(scattered, i * (2 * U * 16))
                    dve.tensor_copy(pos5[:, 0, :], R["pos"][:, 0, ds(i * U, U)]).then_inc(set5, 1)
                    dve.tensor_copy(pos5[:, 1, :], R["pos"][:, 1, ds(i * U, U)]).then_inc(set5, 1)


def experts(nc, xe, ye, R, S):
    HC = HID // 2
    with Scope(nc, "experts", S["keep"]) as s:
        w13, w2 = R["w13"], R["w2"]
        x, xt = s.sb("x", [P, D]), s.sb("xt", [P, D])
        sg, h, ht, ysb = s.sb("sg", [P, HID]), s.sb("h", [P, HID]), s.sb("ht", [P, HJ * P]), s.sb("ysb", [P, D])
        xp, hp, htp, yp = s.ps("xp", [P, 512]), s.ps("hp", [P, 4 * 512]), s.ps("htp", [P, 2 * 512]), s.ps("yp", [P, 512])
        x_in, x_turned, xt_made, hidden, silu, h_made, h_turned, ht_made, y_made, y_copied, stored, sp_passed = [s.sem(n) for n in
            ("x_in", "x_turned", "xt_made", "hidden", "silu", "h_made", "h_turned", "ht_made", "y_made", "y_copied", "stored", "sp_passed")]
        hp3 = hp[:, :].rearrange("p (c n) -> p c n", c=4)
        piece = [P] * (HJ - 1) + [HR]
        with nc.Block() as block:
            @block.sync
            def _(sp):
                sp.dma_start(x[:, :], xe[0:P, :]).then_inc(x_in, 16)
                sp.wait_ge(x_turned, 1)
                sp.dma_start(x[:, :], xe[P:2 * P, :]).then_inc(x_in, 16)
                with sp.Fori(0, MT - 1) as t:
                    sp.wait_ge(x_turned, t + 2)
                    sp.sem_inc(sp_passed, 1)
                    sp.dma_start(x[:, :], xe[ds((t + 2) * P, P), :]).then_inc(x_in, 16)
                    sp.wait_ge(y_copied, t + 1)
                    sp.sem_inc(sp_passed, 1)
                    sp.dma_start(ye[ds(t * P, P), :], ysb[:, :]).then_inc(stored, 16)
                sp.wait_ge(y_copied, MT)
                sp.dma_start(ye[(MT - 1) * P:MT * P, :], ysb[:, :]).then_inc(stored, 16)
                sp.wait_ge(stored, MT * 16)
                sp.wait_ge(x_in, (MT + 1) * 16)

            @block.tensor
            def _(pe):
                def turn_x(t):
                    pe.wait_ge(x_in, t * 16 + 16)
                    pe.wait_ge(xt_made, t)
                    for kc in range(2):
                        mm = pe.transpose(xp[:, kc * P:(kc + 1) * P], x[:, kc * P:(kc + 1) * P], S["ident"][:, :])
                    mm.then_inc(x_turned, 1)

                def up(t, at):
                    pe.wait_ge(xt_made, t + 1)
                    for kc in range(2):
                        for c in range(4):
                            rhs = w13[:, ds(at * W13 + (kc * 2 * HID + c * HC), HC)]
                            mm = pe.matmul(hp3[:, c, 0:HC], xt[:, kc * P:(kc + 1) * P], rhs, start=(kc == 0), stop=(kc == 1))
                    mm.then_inc(hidden, 1)

                turn_x(0)
                first = pe.value_load(R["expert"][0:1, 0:1], min_val=0, max_val=EX - 1)
                up(0, first)
                with pe.Fori(0, MT) as t:
                    e = pe.value_load(R["expert"][0:1, ds(t, 1)], min_val=0, max_val=EX - 1)
                    nxt = pe.value_load(R["expert"][0:1, ds(t + 1, 1)], min_val=0, max_val=EX - 1)
                    turn_x(t + 1)
                    pe.wait_ge(h_made, t + 1)
                    pe.wait_ge(ht_made, t * 2)
                    for j, m in enumerate(piece):
                        mm = pe.transpose(htp[0:m, j * P:(j + 1) * P], h[:, j * P:j * P + m], S["ident"][:, :])
                    mm.then_inc(h_turned, 1)
                    up(t + 1, nxt)
                    pe.wait_ge(ht_made, t * 2 + 2)
                    pe.wait_ge(y_copied, t)
                    for j, m in enumerate(piece):
                        mm = pe.matmul(yp[:, 0:D], ht[0:m, j * P:(j + 1) * P], w2[0:m, ds(e * W2 + j * D, D)], start=(j == 0), stop=(j == HJ - 1))
                    mm.then_inc(y_made, 1)

            @block.scalar
            def _(act):
                def copy_x(t):
                    act.wait_ge(x_turned, t + 1)
                    act.wait_ge(hidden, t)
                    act.activation(xt[:, :], xp[:, 0:D], ACT.Copy).then_inc(xt_made, 1)

                copy_x(0)
                with act.Fori(0, MT) as t:
                    act.wait_ge(hidden, t + 1)
                    act.activation(sg[:, :].rearrange("p (c n) -> p c n", c=2), hp3[:, 0:2, 0:HC], ACT.Silu).then_inc(silu, 1)
                    copy_x(t + 1)
                    act.wait_ge(y_made, t)
                    act.wait_ge(h_turned, t + 1)
                    act.activation(ht[:, 0:5 * P], htp[:, 0:5 * P], ACT.Copy).then_inc(ht_made, 1)
                    act.activation(ht[0:HR, 5 * P:], htp[0:HR, 5 * P:6 * P], ACT.Copy).then_inc(ht_made, 1)

            @block.vector
            def _(dve):
                with dve.Fori(0, MT) as t:
                    dve.wait_ge(silu, t + 1)
                    dve.wait_ge(h_turned, t)
                    dve.tensor_tensor(h[:, :].rearrange("p (c n) -> p c n", c=2), sg[:, :].rearrange("p (c n) -> p c n", c=2),
                                      hp3[:, 2:4, 0:HC], ALU.mult).then_inc(h_made, 1)
                    dve.wait_ge(y_made, t + 1)
                    dve.wait_ge(stored, t * 16)
                    dve.tensor_copy(ysb[:, :], yp[:, 0:D]).then_inc(y_copied, 1)


def combine(nc, x3, ye, out, R, S):
    with Scope(nc, "combine", S["keep"]) as s:
        pos5 = s.sb("pos5", [P, 2, U], I32)
        x, y = s.sb("x", [P, U * D]), s.sb("y", [P, 2 * U * D])
        set5, x_in, step, done, stored, sp_passed, pool_passed = [s.sem(n) for n in ("set5", "x_in", "step", "done", "stored", "sp_passed", "pool_passed")]
        got = s.pool_sem("got")
        x3v = x[:, :].rearrange("p (u d) -> p u d", u=U)
        whole = ROUNDS - 1
        with nc.Block() as block:
            @block.sync
            def _(sp):
                with sp.Fori(0, whole) as i:
                    sp.wait_ge(stored, i * 16)
                    sp.sem_inc(sp_passed, 1)
                    sp.dma_start(x3v, x3[ds(i * (U * P), U * P), :].rearrange("(u p) d -> p u d", p=P)).then_inc(x_in, 16)
                    sp.wait_ge(done, i + 1)
                    sp.sem_inc(sp_passed, 1)
                    sp.dma_start(out[ds(i * (U * P), U * P), :].rearrange("(u p) d -> p u d", p=P), x3v).then_inc(stored, 16)
                sp.wait_ge(stored, whole * 16)
                sp.dma_start(x3v, x3[whole * U * P:NP, :].rearrange("(u p) d -> p u d", p=P)).then_inc(x_in, 16)
                sp.wait_ge(done, ROUNDS)
                full = NT - 1 - whole * U
                r0 = whole * U * P
                sp.dma_start(out[r0:r0 + full * P, :].rearrange("(u p) d -> p u d", p=P), x3v[:, 0:full, :]).then_inc(stored, 16)
                sp.dma_start(out[(NT - 1) * P:N, :], x[0:N - (NT - 1) * P, full * D:(full + 1) * D]).then_inc(stored, 16)
                sp.wait_ge(stored, (whole + 2) * 16)

            @block.gpsimd
            def _(pool):
                with pool.Fori(0, ROUNDS) as i:
                    pool.wait_ge(set5, i * 2 + 2)
                    pool.sem_inc(pool_passed, 1)
                    for c in range(2):
                        for u in range(U):
                            at = (c * U + u) * D
                            pool.indirect_dma_start(out=y[:, at:at + D], out_offset=None, in_=ye,
                                                    in_offset=bass.IndirectOffsetOnAxis(ap=pos5[:, c, u:u + 1], axis=0)).then_inc(got, 16)

            @block.vector
            def _(dve):
                with dve.Fori(0, ROUNDS) as i:
                    dve.wait_ge(step, i * (2 * U))
                    dve.tensor_copy(pos5[:, 0, :], R["pos"][:, 0, ds(i * U, U)]).then_inc(set5, 1)
                    dve.tensor_copy(pos5[:, 1, :], R["pos"][:, 1, ds(i * U, U)]).then_inc(set5, 1)
                    dve.wait_ge(x_in, i * 16 + 16)
                    dve.wait_ge(got, i * (2 * U * 16) + 2 * U * 16)
                    for c in range(2):
                        for u in range(U):
                            at = (c * U + u) * D
                            dve.scalar_tensor_tensor(out=x3v[:, u, :], in0=y[:, at:at + D], scalar=R["g"][:, c, ds(i * U + u, 1)], in1=x3v[:, u, :],
                                                     op0=ALU.mult, op1=ALU.add).then_inc(step, 1)
                        dve.wait_ge(step, i * (2 * U) + (c + 1) * U)
                    dve.sem_inc(done, 1)


def dram(nc, name, shape, dt=F32):
    return nc.dram_tensor(name, shape, dt, kind="Internal").ap()


def build(nc, a, out):
    lists = [
        (Cfg("0", 206250, 2048), a["dst"], a["src"], None, 8, 32),
        (Cfg("1", 131072, 1024), a["L0_ffn_edge_index"][1], a["L0_ffn_edge_index"][0], N - 1, 4, 4),
        (Cfg("2", 206250, 2048), a["src"], a["dst"], None, 4, 64),
    ]
    x0, x1, x2, x3 = [dram(nc, f"x{i}", (NP, D)) for i in range(4)]
    xt1 = dram(nc, "xt1", (NTP, P, 2 * P))
    y1 = dram(nc, "y1", (NP, 4 * D))
    tabs, owns, outs, invs, infos, ells, starts = [], [], [], [], [], [], []
    for i, (cfg, key, payload, clamp, H, C) in enumerate(lists):
        RW = H * (C + 1) + 2 * H
        tabs.append(dram(nc, f"table{i}", (NP + 1, RW)))
        owns.append(dram(nc, f"own{i}", (NP, RW)))
        outs.append(dram(nc, f"agg{i}", (NP, H * C)))
        invs.append(dram(nc, f"inv{i}", (NP,), I32))
        infos.append(dram(nc, f"info{i}", (1, INFO), I32))
        ells.append(dram(nc, f"ell{i}", (cfg.max_blocks, P, SLOTS), I32))
        starts.append(dram(nc, f"starts{i}", (NP + 1,)))
    with Scope(nc, "all") as outer:
        S = constants(nc, outer)
        prepare(nc, a["x"], x0, [(tabs[i], lists[i][4]) for i in range(3)], [o[NR:NP, :] for o in outs], S)
        sorts = [ListSort(cfg, key, payload, clamp, dram(nc, f"words{i}", (cfg.total,)), dram(nc, f"firsts{i}", (cfg.total // COARSE,)),
                          dram(nc, f"copies{i}", (WIN, cfg.rows * WIN), I32))
                 for i, (cfg, key, payload, clamp, H, C) in enumerate(lists)]
        sort_first(nc, sorts[0], S)
        w13t, w2t = dram(nc, "w13t", (EX, P, 4 * HID)), dram(nc, "w2t", (EX, P, HJ * D))
        xe, ye = dram(nc, "xe", (SLOT_ROWS, D)), dram(nc, "ye", (SLOT_ROWS, D))
        setup = MixtureSetUp(a["L1_ffn_w1"], a["L1_ffn_w2"], a["L1_ffn_w3"], w13t, w2t, xe, ye)
        for i, ls in enumerate(sorts):
            rank_nodes(nc, ls.cfg, ls.words, ls.firsts, ls.copies, starts[i], invs[i], infos[i], ells[i],
                       dram(nc, f"maxdeg{i}", (NT,)), S, *((sorts[i + 1], None) if i + 1 < len(sorts) else (None, setup)))
        dense(nc, 0, 8, 32, x0, None, tabs[0], owns[0], invs[0],
              {"w": a["L0_gnn_W"], "neigh": a["L0_gnn_a_left"].rearrange("(a h) c -> a (h c)", a=1), "mine": a["L0_gnn_a_right"].rearrange("(a h) c -> a (h c)", a=1)}, S)
        aggregate(nc, lists[0][0], 8, 32, tabs[0], owns[0], infos[0], ells[0], outs[0], True, S)
        dense(nc, 1, 4, 4, x0, x1, tabs[1], owns[1], invs[1],
              {"w": a["L0_ffn_W_gat"], "neigh": a["L0_ffn_att_src"].rearrange("(a h) c -> a (h c)", a=1), "mine": a["L0_ffn_att_dst"].rearrange("(a h) c -> a (h c)", a=1)}, S,
              agg=outs[0], inv=invs[0], extra={"xt": xt1})
        ffn = SmallExperts(xt1, a["L0_ffn_W1"], a["L0_ffn_b1"], a["L0_ffn_W2"], a["L0_ffn_b2"], y1, S)
        aggregate(nc, lists[1][0], 4, 4, tabs[1], owns[1], infos[1], ells[1], outs[1], True, S, ffn)
        dense(nc, 2, 4, 64, x1, x2, tabs[2], owns[2], invs[2],
              {"w": a["L1_gnn_weight"], "neigh": a["L1_gnn_att_dst"].rearrange("a h c -> a (h c)"), "mine": a["L1_gnn_att_src"].rearrange("a h c -> a (h c)"),
               "gamma": a["L0_ffn_ln_gamma"], "beta": a["L0_ffn_ln_beta"], "b_gat": a["L0_ffn_b_gat"]}, S,
              agg=outs[1], inv=invs[1], extra={"y": y1})
        aggregate(nc, lists[2][0], 4, 64, tabs[2], owns[2], infos[2], ells[2], outs[2], False, S)
        xn3 = dram(nc, "xn3", (NP, D))
        R = {"rank": outer.sb("rank", [P, NTP, EX]), "gate": outer.sb("gate", [P, NTP, EX]), "pos": outer.sb("pos", [P, 2, NTP], I32),
             "g": outer.sb("g", [P, 2, NTP]), "expert": outer.sb("expert", [1, MT + 1], I32)}
        dense(nc, 3, 0, 0, x2, x3, None, None, None, {"w": a["L1_ffn_router_w"], "bias": a["L1_gnn_bias"]}, S,
              agg=outs[2], inv=invs[2], extra={"xn": xn3, "rank": R["rank"], "gate": R["gate"]})
        R.update(w13=outer.sb("w13", [P, EX * W13]), w2=outer.sb("w2", [P, EX * W2]), w_in=outer.sem("w_in"))
        dispatch(nc, xn3, xe, w13t, w2t, R, S)
        experts(nc, xe, ye, R, S)
        combine(nc, x3, ye, out, R, S)


_ORDER = ["x", "src", "dst", "L0_gnn_W", "L0_gnn_a_left", "L0_gnn_a_right", "L0_ffn_W_gat", "L0_ffn_att_src", "L0_ffn_att_dst",
          "L0_ffn_b_gat", "L0_ffn_ln_gamma", "L0_ffn_ln_beta", "L0_ffn_W1", "L0_ffn_b1", "L0_ffn_W2", "L0_ffn_b2", "L0_ffn_edge_index",
          "L1_gnn_weight", "L1_gnn_att_src", "L1_gnn_att_dst", "L1_gnn_bias", "L1_ffn_router_w", "L1_ffn_w1", "L1_ffn_w2", "L1_ffn_w3"]


def kernel(**inputs):
    import numpy as np
    import concourse.bacc as bacc
    from concourse import mybir as mb
    from concourse.bass_utils import run_bass_kernel_spmd

    nc = bacc.Bacc("TRN2", target_bir_lowering=False, num_devices=1)
    arrays, aps = {}, {}
    for name in _ORDER:
        arr = np.ascontiguousarray(inputs[name])
        arrays[f"in_{name}"] = arr
        aps[name] = nc.dram_tensor(f"in_{name}", arr.shape, mb.dt.from_np(arr.dtype), kind="ExternalInput").ap()
    out = nc.dram_tensor("out", (N, D), mb.dt.float32, kind="ExternalOutput").ap()
    build(nc, aps, out)
    r = run_bass_kernel_spmd(nc, [arrays], core_ids=[0])
    return r.results[0]["out"]
```
